# Optimizing a Trainium2 kernel written in Bass

```python
import numpy as np
import jax
import jax.numpy as jnp

def _softmax(x, axis=-1):
    return jax.nn.softmax(x, axis=axis)

def _gelu(x):
    return jax.nn.gelu(x, approximate=True)

def _silu(x):
    return jax.nn.silu(x)

def _sigmoid(x):
    return jax.nn.sigmoid(x)

def _layernorm(x, axis=-1, eps=1e-05):
    m = jnp.mean(x, axis=axis, keepdims=True)
    v = jnp.var(x, axis=axis, keepdims=True)
    return (x - m) / jnp.sqrt(v + eps)

def _scatter_add(tgt, idx, src, axis=0):
    return tgt.at[idx].add(src)

def _segment_sum(src, seg, n):
    return jax.ops.segment_sum(src, seg, n)
kernel_name = 'mk_hybrid_d1_jaxref_r8_0e1cfc'

def setup_inputs(seed: int=0):
    np.random.seed(seed)
    _w = jnp.asarray

    def _L0_attn_a_setup():
        import jax, jax.numpy as jnp
        import numpy as np
        import math
        N_HEAD = 16
        N_KV_HEAD = 4
        HEAD_DIM = 64
        ROPE_THETA = 10000.0

        def _rope_cache(T, D, dtype):
            inv_freq = 1.0 / ROPE_THETA ** (jnp.arange(0, D, 2, dtype=dtype) / D)
            t = jnp.arange(T, dtype=dtype)
            freqs = jnp.einsum('i,j->ij', t, inv_freq)
            return (jnp.cos(freqs)[None, None], jnp.sin(freqs)[None, None])

        def _apply_rope(x, cos, sin):
            x1 = x[..., ::2]
            x2 = x[..., 1::2]
            return jnp.concatenate([x1 * cos - x2 * sin, x1 * sin + x2 * cos], axis=-1)
        key = jax.random.key(seed)
        k0, k1, k2, k3, k4 = jax.random.split(key, 5)
        B, T, C = (4, 256, 128)
        scale = 0.02
        return {'x': jax.random.normal(k0, (B, T, C), dtype=jnp.float32), 'Wq': jax.random.normal(k1, (C, N_HEAD * HEAD_DIM), dtype=jnp.float32) * scale, 'Wk': jax.random.normal(k2, (C, N_KV_HEAD * HEAD_DIM), dtype=jnp.float32) * scale, 'Wv': jax.random.normal(k3, (C, N_KV_HEAD * HEAD_DIM), dtype=jnp.float32) * scale, 'Wo': jax.random.normal(k4, (N_HEAD * HEAD_DIM, C), dtype=jnp.float32) * scale}
    _L0_attn_a_in = _L0_attn_a_setup()

    def _L0_attn_b_setup():
        import jax, jax.numpy as jnp
        import numpy as np
        D_MODEL, D_QKV, N_HEADS = (128, 64, 16)
        key = jax.random.key(seed)
        k_x, k_qkv, k_out = jax.random.split(key, 3)
        X = jax.random.normal(k_x, (2, 256, D_MODEL), dtype=jnp.float32)
        W_qkv = jax.random.normal(k_qkv, (D_MODEL, 3 * D_QKV * N_HEADS), dtype=jnp.float32) * D_MODEL ** (-0.5)
        W_out = jax.random.normal(k_out, (D_QKV * N_HEADS, D_MODEL), dtype=jnp.float32) * (D_QKV * N_HEADS) ** (-0.5)
        return {'X': X, 'W_qkv': W_qkv, 'W_out': W_out}
    _L0_attn_b_in = _L0_attn_b_setup()

    def _L0_ffn_setup():
        import jax, jax.numpy as jnp
        import numpy as np
        B, T, D, H, E, K = (2, 256, 128, 512, 8, 2)
        EPS = 1e-12

        def moe_forward(x, Wg, bg, W1, b1, W2, b2):
            gates = jax.nn.softmax(x @ Wg + bg, axis=-1)
            _, top_idx = jax.lax.top_k(gates, K)
            mask = jax.nn.one_hot(top_idx, E, dtype=gates.dtype).sum(axis=-2)
            g = gates * mask
            g = g / jnp.maximum(jnp.sum(jnp.abs(g), axis=-1, keepdims=True), EPS)
            h = jnp.einsum('btd,edh->bteh', x, W1) + b1[None, None]
            h = jax.nn.gelu(h, approximate=False)
            eo = jnp.einsum('bteh,ehd->bted', h, W2) + b2[None, None]
            return jnp.einsum('bte,bted->btd', g, eo)
        key = jax.random.key(seed)
        ks = jax.random.split(key, 8)
        s_d = 1.0 / np.sqrt(D)
        s_h = 1.0 / np.sqrt(H)
        return {'x': jax.random.normal(ks[0], (B, T, D), dtype=jnp.float32), 'Wg': jax.random.uniform(ks[1], (D, E), jnp.float32, -s_d, s_d), 'bg': jax.random.uniform(ks[2], (E,), jnp.float32, -s_d, s_d), 'W1': jax.random.uniform(ks[3], (E, D, H), jnp.float32, -s_d, s_d), 'b1': jax.random.uniform(ks[4], (E, H), jnp.float32, -s_d, s_d), 'W2': jax.random.uniform(ks[5], (E, H, D), jnp.float32, -s_h, s_h), 'b2': jax.random.uniform(ks[6], (E, D), jnp.float32, -s_h, s_h)}
    _L0_ffn_in = _L0_ffn_setup()
    _d = {'L0_attn_a_x': _L0_attn_a_in['x'], 'L0_attn_a_Wq': _L0_attn_a_in['Wq'], 'L0_attn_a_Wk': _L0_attn_a_in['Wk'], 'L0_attn_a_Wv': _L0_attn_a_in['Wv'], 'L0_attn_a_Wo': _L0_attn_a_in['Wo'], 'L0_attn_b_W_qkv': _L0_attn_b_in['W_qkv'], 'L0_attn_b_W_out': _L0_attn_b_in['W_out'], 'L0_ffn_Wg': _L0_ffn_in['Wg'], 'L0_ffn_bg': _L0_ffn_in['bg'], 'L0_ffn_W1': _L0_ffn_in['W1'], 'L0_ffn_b1': _L0_ffn_in['b1'], 'L0_ffn_W2': _L0_ffn_in['W2'], 'L0_ffn_b2': _L0_ffn_in['b2']}
    _x0 = _d['L0_attn_a_x']
    _d['L0_attn_a_x'] = jax.random.normal(jax.random.fold_in(jax.random.key(seed), 1), (8, 512, 128), dtype=_x0.dtype)
    del _x0
    return _d

def reference(L0_attn_a_x, L0_attn_a_Wq, L0_attn_a_Wk, L0_attn_a_Wv, L0_attn_a_Wo, L0_attn_b_W_qkv, L0_attn_b_W_out, L0_ffn_Wg, L0_ffn_bg, L0_ffn_W1, L0_ffn_b1, L0_ffn_W2, L0_ffn_b2):

    def _L0_attn_a_ref(x, Wq, Wk, Wv, Wo):
        import jax, jax.numpy as jnp
        import numpy as np
        import math
        N_HEAD = 16
        N_KV_HEAD = 4
        HEAD_DIM = 64
        ROPE_THETA = 10000.0

        def _rope_cache(T, D, dtype):
            inv_freq = 1.0 / ROPE_THETA ** (jnp.arange(0, D, 2, dtype=dtype) / D)
            t = jnp.arange(T, dtype=dtype)
            freqs = jnp.einsum('i,j->ij', t, inv_freq)
            return (jnp.cos(freqs)[None, None], jnp.sin(freqs)[None, None])

        def _apply_rope(x, cos, sin):
            x1 = x[..., ::2]
            x2 = x[..., 1::2]
            return jnp.concatenate([x1 * cos - x2 * sin, x1 * sin + x2 * cos], axis=-1)
        B, T, C = x.shape
        H, Hkv, D = (N_HEAD, N_KV_HEAD, HEAD_DIM)
        q = (x @ Wq).reshape(B, T, H, D).transpose(0, 2, 1, 3)
        k = (x @ Wk).reshape(B, T, Hkv, D).transpose(0, 2, 1, 3)
        v = (x @ Wv).reshape(B, T, Hkv, D).transpose(0, 2, 1, 3)
        rep = H // Hkv
        k = jnp.repeat(k, rep, axis=1)
        v = jnp.repeat(v, rep, axis=1)
        cos, sin = _rope_cache(T, D, x.dtype)
        q = _apply_rope(q, cos, sin)
        k = _apply_rope(k, cos, sin)
        att = jnp.einsum('bhtd,bhsd->bhts', q, k) / math.sqrt(D)
        mask = jnp.tril(jnp.ones((T, T), dtype=bool))
        att = jnp.where(mask, att, -jnp.inf)
        att = jax.nn.softmax(att, axis=-1)
        y = jnp.einsum('bhts,bhsd->bhtd', att, v)
        y = y.transpose(0, 2, 1, 3).reshape(B, T, H * D)
        return y @ Wo

    def _L0_attn_b_ref(X, W_qkv, W_out):
        import jax, jax.numpy as jnp
        import numpy as np
        D_MODEL, D_QKV, N_HEADS = (128, 64, 16)
        b, s, _ = X.shape
        h, d = (N_HEADS, D_QKV)
        scale = d ** 0.5
        qkv = X @ W_qkv
        qkv = qkv.reshape(b, s, h, d, 3)
        q, k, v = (qkv[..., 0], qkv[..., 1], qkv[..., 2])
        scores = jnp.einsum('bqhd,bkhd->bhqk', q, k) / scale
        weights = jax.nn.softmax(scores, axis=-1)
        attn = jnp.einsum('bhqk,bkhd->bqhd', weights, v)
        return attn.reshape(b, s, h * d) @ W_out

    def _L0_ffn_ref(x, Wg, bg, W1, b1, W2, b2):
        import jax, jax.numpy as jnp
        import numpy as np
        B, T, D, H, E, K = (2, 256, 128, 512, 8, 2)
        EPS = 1e-12

        def moe_forward(x, Wg, bg, W1, b1, W2, b2):
            gates = jax.nn.softmax(x @ Wg + bg, axis=-1)
            _, top_idx = jax.lax.top_k(gates, K)
            mask = jax.nn.one_hot(top_idx, E, dtype=gates.dtype).sum(axis=-2)
            g = gates * mask
            g = g / jnp.maximum(jnp.sum(jnp.abs(g), axis=-1, keepdims=True), EPS)
            h = jnp.einsum('btd,edh->bteh', x, W1) + b1[None, None]
            h = jax.nn.gelu(h, approximate=False)
            eo = jnp.einsum('bteh,ehd->bted', h, W2) + b2[None, None]
            return jnp.einsum('bte,bted->btd', g, eo)
        return moe_forward(x, Wg, bg, W1, b1, W2, b2)
    x = L0_attn_a_x
    x = x + _L0_attn_a_ref(_layernorm(x, axis=-1), L0_attn_a_Wq, L0_attn_a_Wk, L0_attn_a_Wv, L0_attn_a_Wo)
    x = x + _L0_ffn_ref(_layernorm(x, axis=-1), L0_ffn_Wg, L0_ffn_bg, L0_ffn_W1, L0_ffn_b1, L0_ffn_W2, L0_ffn_b2)
    x = x + _L0_attn_b_ref(_layernorm(x, axis=-1), L0_attn_b_W_qkv, L0_attn_b_W_out)
    x = x + _L0_ffn_ref(_layernorm(x, axis=-1), L0_ffn_Wg, L0_ffn_bg, L0_ffn_W1, L0_ffn_b1, L0_ffn_W2, L0_ffn_b2)
    return x

_drawn_inputs = setup_inputs


def setup_inputs(seed=0):
    import zlib

    import numpy as np

    out = dict(_drawn_inputs(seed))
    spreads = {}
    factors = {'L0_attn_a_Wq': 8.0, 'L0_attn_a_Wk': 8.0}
    for name, (base, spread) in spreads.items():
        noise = np.random.default_rng([zlib.crc32(name.encode()), seed]).standard_normal(out[name].shape)
        drawn = base * np.exp(spread * noise) if base else spread * noise
        out[name] = jnp.asarray(drawn.astype(out[name].dtype))
    for name, factor in factors.items():
        out[name] = (out[name] * factor).astype(out[name].dtype)
    return out
```

```python
from contextlib import ExitStack

import numpy as np

import concourse.bass as bass
from concourse import mybir

F32 = mybir.dt.float32
F16 = mybir.dt.float16
ALU = mybir.AluOpType
ACT = mybir.ActivationFunctionType
AX = mybir.AxisListType

B, T, D = 8, 512, 128
P = 128
NT = T // P
HEADS, HD = 16, 64
GROUP = 4
STEPS = HEADS // GROUP
UNITS = GROUP * NT
AHEAD = 2
RING = 4
WSCALE = 64.0
EPS = 1e-5
MASKED = -60000.0
BN = 6
VW = HD + 2


class Step:

    def __init__(self, b, g):
        self.b, self.g = b, g

    def count(self, per_step, k):
        return self.b * (STEPS * per_step) + (self.g * per_step + k)

    def next(self):
        return Step(self.b, self.g + 1) if self.g + 1 < STEPS else Step(self.b + 1, 0)

    def is_before_first(self):
        return isinstance(self.b, int) and self.b < 0


def wait(eng, sem, value):
    if isinstance(value, int) and value <= 0:
        return
    eng.wait_ge(sem, value)


class Attention:

    def __init__(self, name, causal, rotary, kv, columns, tasks, evacuated_by, pool_tiles):
        self.name, self.causal, self.rotary, self.kv = name, causal, rotary, kv
        self.columns = columns
        self.tasks = tasks
        self.evacuated_by = evacuated_by
        self.pool_tiles = pool_tiles
        self.transposed = [x for u in range(UNITS) for x in tasks["pe"].get(u, []) if x in evacuated_by]
        self.projections = [x for u in range(UNITS) for x in tasks["pe"].get(u, []) if x[0] in "PQV"]

    def order(self, task):
        return self.transposed.index(task)

    def evacuations(self, engine, upto):
        return sum(self.evacuated_by[x] == engine for x in self.transposed[:self.order(upto) + 1])

    def lows(self, on_pool, unit):
        return sum((u % NT in self.pool_tiles) == on_pool for u in range(unit + 1))


def spec_a():
    pe = {0: ["P0"], 1: ["YT0"], 2: ["P1"], 3: ["YT1"], 4: ["P2"], 6: ["P3"], 8: ["TK01"], 9: ["TQ01"],
          10: ["TQ23", "M0a"], 11: ["M0b", "M1a"], 12: ["M1b", "M2a", "TX"], 13: ["M2b", "M3a", "TT01"],
          14: ["M3b", "WO"], 15: ["TT23"]}
    dve = {0: ["P0"], 1: ["vl0"], 2: ["P1"], 3: ["vl1"], 4: ["P2"], 5: ["vl2"], 6: ["P3"], 7: ["vl3"],
           8: ["TK01", "LX"], 9: ["TQ01"], 10: ["TQ23", "M0a", "XL"], 11: ["M0b", "M1a"],
           12: ["M1b", "M2a", "TX"], 13: ["M2b", "M3a", "TT01"], 14: ["M3b", "WO"], 15: ["TT23"]}
    act = {1: ["vh0", "YT0", "qh0"], 3: ["vh1", "YT1", "qh1"], 5: ["vh2", "qh2"], 7: ["vh3", "qh3"],
           9: ["XH"]}
    pool = {0: ["P0"], 1: ["ql0"], 2: ["P1"], 3: ["ql1"], 4: ["P2"], 5: ["ql2"], 6: ["P3"], 7: ["ql3"]}
    by = {"TK01": "dve", "TQ01": "dve", "TQ23": "dve", "TT01": "dve", "TT23": "dve"}
    return Attention("a", True, True, 1, GROUP * HD + 2 * HD, {"pe": pe, "dve": dve, "act": act, "pool": pool},
                     by, (3,))


def spec_b():
    pe = {0: ["Q0"], 1: ["Q1"], 2: ["Q2"], 3: ["Q3"], 4: ["YT0"], 5: ["V0", "YT1"], 6: ["TQ01"],
          7: ["V1", "TK01"], 8: ["TQ23", "M0a"], 9: ["V2", "TK23", "M0b"], 10: ["M1a", "TL01"],
          11: ["V3", "M1b", "TL23"], 12: ["M2a", "M2b", "TX"], 13: ["TT01", "M3a"], 14: ["M3b", "WO"],
          15: ["TT23"]}
    dve = {u: list(x) for u, x in pe.items()}
    dve[8].append("LX")
    dve[10].append("XL")
    act = {u: [x for x in t if x[0] in "QV" or x[:2] in ("YT", "TL")] for u, t in pe.items()}
    act[9].append("XH")
    by = {"TQ01": "dve", "TK01": "dve", "TQ23": "dve", "TK23": "dve", "TL01": "act", "TL23": "act",
          "TT01": "dve", "TT23": "dve"}
    return Attention("b", False, False, GROUP, 3 * GROUP * HD, {"pe": pe, "dve": dve, "act": act, "pool": {}},
                     by, (3,))


class AttentionSignals:

    def __init__(self, new, phase):
        self.projected = new(f"{phase}_projected")
        self.projection_free = new(f"{phase}_projection_free")
        self.rope_terms = new(f"{phase}_rope_terms")
        self.rope_sum = new(f"{phase}_rope_sum")
        self.heads_high = new(f"{phase}_heads_high")
        self.heads_low = new(f"{phase}_heads_low")
        self.v_high = new(f"{phase}_v_high")
        self.transposed = new(f"{phase}_transposed")
        self.evacuated_dve = new(f"{phase}_evacuated_dve")
        self.evacuated_act = new(f"{phase}_evacuated_act")
        self.max_scored = new(f"{phase}_max_scored")
        self.max_taken = new(f"{phase}_max_taken")
        self.scored = new(f"{phase}_scored")
        self.exped = new(f"{phase}_exped")
        self.low_dve = new(f"{phase}_low_dve")
        self.low_pool = new(f"{phase}_low_pool")
        self.mixed = new(f"{phase}_mixed")
        self.recip = new(f"{phase}_recip")
        self.normed = new(f"{phase}_normed")
        self.y_turned = new(f"{phase}_y_turned")
        self.y_kept = new(f"{phase}_y_kept")
        self.out_projected = new(f"{phase}_out_projected")
        self.x_added = new(f"{phase}_x_added")
        self.stats = new(f"{phase}_stats")
        self.ln_done = new(f"{phase}_ln_done")
        self.ln_high = new(f"{phase}_ln_high")
        self.ln_low = new(f"{phase}_ln_low")
        self.x_turned = new(f"{phase}_x_turned")
        self.x_kept = new(f"{phase}_x_kept")




def pe_projection(pe, m, a, s, n, task):
    t = int(task[1])
    g = n.g
    k = a.projections.index(task)
    wait(pe, s.projection_free, n.count(len(a.projections), k))
    if k == 0 and g == 0:
        wait(pe, s.x_kept, n.b + 1)
    w = m.w[a.name]
    lo, hi = (0, 2 * GROUP * HD) if task[0] == "Q" else (2 * GROUP * HD, 3 * GROUP * HD)
    if task[0] == "P":
        lo, hi = 0, a.columns
    out = m.pj[:, 0:hi - lo]
    tile = slice(t * P, (t + 1) * P)
    pe.matmul(out, m.xt[:, 0, tile], w[:, 0, g, lo:hi], start=True, stop=False)
    pe.matmul(out, m.xt[:, 1, tile], w[:, 0, g, lo:hi], start=False, stop=False)
    pe.matmul(out, m.xt[:, 0, tile], w[:, 1, g, lo:hi], start=False, stop=True).then_inc(s.projected, 1)


def turn_wait(pe, a, s, n, before):
    if before is None:
        before, ref = a.transposed[-1], Step(n.b, n.g - 1)
    else:
        ref = n
    if before == "TX":
        wait(pe, s.x_kept, n.b + 2)
    elif before[:2] == "YT":
        wait(pe, s.y_kept, Step(n.b, n.g - 2).count(2, int(before[2]) + 1))
    else:
        e = a.evacuated_by[before]
        sem = s.evacuated_dve if e == "dve" else s.evacuated_act
        per = a.evacuations(e, a.transposed[-1])
        wait(pe, sem, ref.count(per, a.evacuations(e, before)))


def pe_turn(pe, m, a, s, n, task):
    par = n.g % 2
    if task[1] == "T":
        wait(pe, s.max_taken, n.count(8, 4 if task == "TT01" else 8))
    else:
        wait(pe, s.heads_low if a.rotary else s.projection_free,
             n.count(4, 4) if a.rotary else n.count(8, a.projections.index("Q3") + 1))
    h0 = int(task[2])
    for j in range(2):
        for t in range(NT):
            if task[1] == "Q":
                src = m.tmq[:, t, h0 + j, 0:P]
            elif task[1] == "T":
                src = m.tmq[:, t, h0 + j, HD:HD + P]
            elif a.kv == 1:
                src = m.tmk[:, t, 0, j * P:(j + 1) * P]
            else:
                src = m.tmk[:, t, h0 + j, 0:P] if task[1] == "K" else m.tmk[:, t, h0 + j, P:2 * P]
            last = pe.transpose(m.tr16[:, (j * NT + t) * P:(j * NT + t + 1) * P], src, m.ident16[:, :])
    last.then_inc(s.transposed, 1)


def pe_turn_x(pe, m, s, b):
    wait(pe, s.ln_low, b + 1)
    for part in range(2):
        for t in range(NT):
            last = pe.transpose(m.tr16[:, (part * NT + t) * P:(part * NT + t + 1) * P],
                                m.xn16[:, t, part, :], m.ident16[:, :])
    last.then_inc(s.x_turned, 1)


def pe_max_scores(pe, m, a, s, n, task):
    par = n.g % 2
    h, half = int(task[1]), "ab".index(task[2])
    k = 2 * h + half
    wait(pe, s.max_taken, n.count(8, k))
    for e in ("dve", "act"):
        need = [x for x in (("TQ01", "TK01") if h < 2 or a.kv == 1 else ("TQ23", "TK23")) + (("TQ23",) if h >= 2 else ())
                if a.evacuated_by[x] == e]
        if need and half == 0 and h % 2 == 0:
            upto = max(need, key=a.order)
            wait(pe, s.evacuated_dve if e == "dve" else s.evacuated_act,
                 n.count(a.evacuations(e, a.transposed[-1]), a.evacuations(e, upto)))
    hk = 0 if a.kv == 1 else h
    for j in range(2):
        qt = 2 * half + j
        keys = (qt + 1) * P if a.causal else T
        last = pe.matmul(m.mx[:, j, 0:keys], m.qt[par][:, h, qt * P:(qt + 1) * P], m.kt[par][:, 0, hk, 0:keys],
                         start=True, stop=not a.causal, skip_group_check=True)
        if a.causal:
            last = pe.matmul(m.mx[:, j, keys - P:keys], m.ident16[:, :], m.mask_q[:, :], start=False, stop=True,
                             skip_group_check=True)
    last.then_inc(s.max_scored, 1)


def pe_scores(pe, m, a, s, st, u):
    par = st.g % 2
    h, kc = divmod(u, NT)
    wait(pe, s.exped, st.count(UNITS, u - 1))
    if u in (0, UNITS // 2):
        upto = "TT01" if u == 0 else "TT23"
        for e in ("dve", "act"):
            per = a.evacuations(e, a.transposed[-1])
            if per:
                wait(pe, s.evacuated_dve if e == "dve" else s.evacuated_act, st.count(per, a.evacuations(e, upto)))
    hk = 0 if a.kv == 1 else h
    q0 = kc * P if a.causal else 0
    out = m.st[:, u % 2, q0:T]
    keys = slice(kc * P, (kc + 1) * P)
    pe.matmul(out, m.kt[par][:, 0, hk, keys], m.qt[par][:, h, q0:T], start=True, stop=False, skip_group_check=True)
    last = pe.matmul(out, m.kt[par][:, 1, hk, keys], m.tt[par][:, h, q0:T], start=False, stop=not a.causal,
                     skip_group_check=True)
    if a.causal:
        last = pe.matmul(m.st[:, u % 2, q0:q0 + P], m.ident16[:, :], m.mask_k[:, :], start=False, stop=True,
                         skip_group_check=True)
    last.then_inc(s.scored, 1)


def pe_mix(pe, m, a, s, st, u):
    par = st.g % 2
    h, kc = divmod(u, NT)
    on_pool = kc in a.pool_tiles
    wait(pe, s.low_pool if on_pool else s.low_dve, st.count(a.lows(on_pool, UNITS - 1), a.lows(on_pool, u)))
    if kc == 0:
        wait(pe, s.normed, st.count(GROUP, h - 1))
    if u == 0:
        wait(pe, s.projection_free, st.count(len(a.projections), len(a.projections)))
    hv = 0 if a.kv == 1 else h
    v = m.vb[par]
    first = kc == 0
    r = u % RING
    for qt in range(kc if a.causal else 0, NT):
        q = slice(qt * P, (qt + 1) * P)
        pe.matmul(m.pv[:, h % 2, qt, :], m.ph[:, r, q], v[:, kc, hv, 0:VW], start=first, stop=False,
                  skip_group_check=True)
        first = False
        pe.matmul(m.pv[:, h % 2, qt, 0:HD], m.ph[:, r, q], v[:, kc, hv, VW:VW + HD], start=False, stop=False,
                  skip_group_check=True)
        last = pe.matmul(m.pv[:, h % 2, qt, :], m.pl[:, r, q], v[:, kc, hv, 0:VW], start=False,
                         stop=(kc == NT - 1), skip_group_check=True)
    last.then_inc(s.mixed, 1)


def pe_turn_y(pe, m, s, before, p):
    wait(pe, s.normed, before.count(GROUP, 2 * p + 2))
    for t in range(NT):
        last = pe.transpose(m.tr32[:, t * P:(t + 1) * P],
                            m.y[:, t, 2 * p:2 * p + 2, :].rearrange("p h d -> p (h d)"), m.ident32[:, :])
    last.then_inc(s.y_turned, 1)


def pe_output(pe, m, a, s, b, n):
    wait(pe, s.y_kept, b * (2 * STEPS) + 2 * STEPS)
    wait(pe, s.projection_free, n)
    for t in range(NT):
        for p in range(HEADS // 2):
            last = pe.matmul(m.pj[:, t * P:(t + 1) * P], m.yt[:, p, t * P:(t + 1) * P], m.wo[a.name][:, p, :],
                             start=(p == 0), stop=(p == HEADS // 2 - 1))
    last.then_inc(s.out_projected, 1)


def pe_step(pe, m, a, s, st, main=True, prep=True):
    n = st.next()
    before = None
    for u in range(UNITS):
        ahead = u + AHEAD
        if ahead < UNITS and main:
            pe_scores(pe, m, a, s, st, ahead)
        elif ahead >= UNITS and prep:
            pe_scores(pe, m, a, s, n, ahead - UNITS)
        for task in a.tasks["pe"].get(u, []):
            if task[:2] == "YT":
                if main and not (isinstance(st.b, int) and (st.b, st.g) == (0, 0)):
                    turn_wait(pe, a, s, n, before)
                    pe_turn_y(pe, m, s, Step(st.b, st.g - 1), int(task[2]))
                    before = task
            elif task == "WO":
                if main and st.g == 0 and not (isinstance(st.b, int) and st.b == 0):
                    pe_output(pe, m, a, s, st.b - 1, n.count(len(a.projections), len(a.projections)))
                    wait(pe, s.x_added, st.b)
            elif not prep:
                continue
            elif task == "TX":
                if main and st.g == 2 and not (isinstance(st.b, int) and st.b == B - 1):
                    turn_wait(pe, a, s, n, before)
                    pe_turn_x(pe, m, s, st.b + 1)
                    before = task
            elif task[0] == "M":
                pe_max_scores(pe, m, a, s, n, task)
            elif task[0] in "PQV":
                pe_projection(pe, m, a, s, n, task)
            else:
                turn_wait(pe, a, s, n, before)
                pe_turn(pe, m, a, s, n, task)
                before = task
        if main:
            pe_mix(pe, m, a, s, st, u)


def every_step(eng, step, ends):
    step(Step(-1, STEPS - 1), main=False)
    step(Step(0, 0))
    with eng.Fori(0, B - 1) as b:
        for g in range(1, STEPS):
            step(Step(b, g))
        step(Step(b + 1, 0))
    for g in range(1, STEPS):
        step(Step(B - 1, g), prep=(g < STEPS - 1))
    ends(Step(B - 1, STEPS - 1))


def attention_pe(pe, m, a, s):
    pe_turn_x(pe, m, s, 0)

    def ends(last):
        for p in range(2):
            wait(pe, s.y_kept, last.count(2, p))
            pe_turn_y(pe, m, s, last, p)
        pe_output(pe, m, a, s, B - 1, B * STEPS * len(a.projections))

    every_step(pe, lambda st, **k: pe_step(pe, m, a, s, st, **k), ends)




def act_exp(act, m, a, s, st, u):
    h, kc = divmod(u, NT)
    q0 = kc * P if a.causal else 0
    r = u % RING
    wait(act, s.scored, st.count(UNITS, u + 1))
    wait(act, s.mixed, st.count(UNITS, u - RING + 1))
    act.activation(m.pf[:, r, q0:T], m.st[:, u % 2, q0:T], ACT.Exp, scale=HD ** -0.5)
    act.activation(m.ph[:, r, q0:T], m.st[:, u % 2, q0:T], ACT.Exp, scale=HD ** -0.5).then_inc(s.exped, 1)


def act_split_high(act, m, a, s, n, task):
    t = int(task[-1])
    if task[0] == "Q":
        wait(act, s.projected, n.count(8, a.projections.index(task) + 1))
        act.activation(m.tmq[:, t, :, HD:P], m.pj[:, 0:GROUP * HD].rearrange("p (h d) -> p h d", d=HD),
                       ACT.Copy, scale=1 / WSCALE)
        k = m.pj[:, GROUP * HD:2 * GROUP * HD].rearrange("p (h d) -> p h d", d=HD)
        act.activation(m.tmk[:, t, :, 0:P].rearrange("p h (x d) -> p h x d", x=2),
                       k.unsqueeze(2).to_broadcast([P, GROUP, 2, HD]),
                       ACT.Copy, scale=1 / WSCALE).then_inc(s.heads_high, 1)
    elif task[0] == "V":
        wait(act, s.projected, n.count(8, a.projections.index(task) + 1))
        act.activation(m.vb[n.g % 2][:, t, :, 0:HD], m.pj[:, 0:GROUP * HD].rearrange("p (h d) -> p h d", d=HD),
                       ACT.Copy, scale=1 / WSCALE).then_inc(s.v_high, 1)
    elif task[:2] == "vh":
        wait(act, s.rope_terms, n.count(4, t + 1))
        act.activation(m.vb[n.g % 2][:, t, 0, 0:HD], m.pj[:, (GROUP + 1) * HD:(GROUP + 2) * HD],
                       ACT.Copy, scale=1 / WSCALE).then_inc(s.v_high, 1)
    else:
        wait(act, s.rope_sum, n.count(4, t + 1))
        act.activation(m.tmq[:, t, :, HD:P], m.qr[:, t % 2, 0:GROUP, :], ACT.Copy)
        act.activation(m.tmk[:, t, 0, 0:P].rearrange("p (x d) -> p x d", x=2),
                       m.qr[:, t % 2, GROUP:GROUP + 1, :].to_broadcast([P, 2, HD]),
                       ACT.Copy).then_inc(s.heads_high, 1)


def act_ln_high(act, m, s, b, row_kept=None):
    wait(act, s.ln_done, b + 1)
    if row_kept is not None:
        wait(act, row_kept, b * 16)
    wait(act, s.x_turned, b)
    act.activation(m.xn16[:, :, 0, :], m.xn[:, :, :], ACT.Copy).then_inc(s.ln_high, 1)


def act_keep_y(act, m, s, before, p):
    wait(act, s.y_turned, before.count(2, p + 1))
    act.activation(m.yt[:, 2 * before.g + p, :], m.tr32[:, :], ACT.Copy).then_inc(s.y_kept, 1)


def turned_into(m, a, n, task):
    par, h0 = n.g % 2, int(task[2])
    if task[1] == "Q":
        return m.qt[par][:, h0:h0 + 2, :]
    if task[1] == "T":
        return m.tt[par][:, h0:h0 + 2, :]
    if a.kv == 1:
        return m.kt[par][:, 0:2, 0, :]
    return m.kt[par][:, "KL".index(task[1]), h0:h0 + 2, :]


def act_step(act, m, a, s, st, main=True, prep=True):
    n = st.next()
    for u in range(UNITS):
        ahead = u + AHEAD
        if ahead < UNITS and main:
            act_exp(act, m, a, s, st, ahead)
        elif ahead >= UNITS and prep:
            act_exp(act, m, a, s, n, ahead - UNITS)
        for task in a.tasks["act"].get(u, []):
            if task[:2] == "YT":
                if main and not (isinstance(st.b, int) and (st.b, st.g) == (0, 0)):
                    before = Step(st.b, st.g - 1) if st.g else Step(st.b - 1, STEPS - 1)
                    act_keep_y(act, m, s, before, int(task[2]))
            elif not prep:
                continue
            elif task == "XH":
                if main and st.g == 1 and not (isinstance(st.b, int) and st.b == B - 1):
                    act_ln_high(act, m, s, st.b + 1)
            elif task in a.evacuated_by:
                wait(act, s.transposed, n.count(len(a.transposed), a.order(task) + 1))
                act.activation(turned_into(m, a, n, task), m.tr16[:, :].rearrange("p (h q) -> p h q", h=2),
                               ACT.Copy).then_inc(s.evacuated_act, 1)
            else:
                act_split_high(act, m, a, s, n, task)
    if main and st.g == 0:
        wait(act, s.out_projected, st.b)


def attention_act(act, m, a, s):
    act_ln_high(act, m, s, 0)

    def ends(last):
        for p in range(2):
            act_keep_y(act, m, s, last, p)

    every_step(act, lambda st, **k: act_step(act, m, a, s, st, **k), ends)




def dve_ln(dve, m, s, b):
    wait(dve, s.ln_low, b)
    for t in range(NT):
        last = dve.tensor_scalar(m.xn[:, t, :], m.x[:, bass.ds(b * (NT * D) + t * D, D)],
                                 m.mean[:, bass.ds(b * NT + t, 1)], m.rstd[:, bass.ds(b * NT + t, 1)],
                                 ALU.subtract, ALU.mult)
    last.then_inc(s.ln_done, 1)


def dve_ln_low(dve, m, s, b):
    wait(dve, s.ln_high, b + 1)
    dve.tensor_tensor(m.xn16[:, :, 1, :], m.xn[:, :, :], m.xn16[:, :, 0, :], ALU.subtract).then_inc(s.ln_low, 1)


def dve_keep_x(dve, m, s, b):
    wait(dve, s.x_turned, b + 1)
    dve.tensor_copy(m.xt[:, :, :], m.tr16[:, :].rearrange("p (x q) -> p x q", x=2)).then_inc(s.x_kept, 1)


def dve_stats(dve, m, b):
    for t in range(NT):
        last = dve.bn_stats(m.bn[:, bass.ds(b * (NT * BN) + t * BN, BN)], m.x[:, bass.ds(b * (NT * D) + t * D, D)])
    return last


def dve_add_output(dve, m, s, b):
    wait(dve, s.out_projected, b + 1)
    x = m.x[:, bass.ds(b * (NT * D), NT * D)]
    dve.tensor_tensor(x, m.pj[:, :], x, ALU.add).then_inc(s.x_added, 1)


def dve_low(dve, m, a, s, st, u):
    kc = u % NT
    q0 = kc * P if a.causal else 0
    r = u % RING
    wait(dve, s.exped, st.count(UNITS, u + 1))
    dve.tensor_tensor(m.pl[:, r, q0:T], m.pf[:, r, q0:T], m.ph[:, r, q0:T], ALU.subtract)\
        .then_inc(s.low_pool if kc in a.pool_tiles else s.low_dve, 1)


def dve_norm(dve, m, s, st, h):
    wait(dve, s.mixed, st.count(UNITS, NT * (h + 1)))
    if h == 0:
        wait(dve, s.y_turned, st.count(2, 0))
    dve.reciprocal(m.rs[:, h % 2, :], m.pv[:, h % 2, :, HD]).then_inc(s.recip, 1)
    wait(dve, s.recip, st.count(GROUP, h + 1))
    dve.tensor_tensor(m.y[:, :, h, :], m.pv[:, h % 2, :, 0:HD],
                      m.rs[:, h % 2, :].unsqueeze(2).to_broadcast([P, NT, HD]), ALU.mult).then_inc(s.normed, 1)


def dve_task(dve, m, a, s, n, task):
    if task[0] == "M":
        h, half = int(task[1]), "ab".index(task[2])
        wait(dve, s.max_scored, n.count(8, 2 * h + half + 1))
        if a.causal:
            for j in range(2):
                qt = 2 * half + j
                last = dve.tensor_reduce(m.tmq[:, qt, h, P:P + 1], m.mx[:, j, 0:(qt + 1) * P], AX.X, ALU.max)
        else:
            last = dve.tensor_reduce(m.tmq[:, 2 * half:2 * half + 2, h, P], m.mx[:, :, :], AX.X, ALU.max)
        last.then_inc(s.max_taken, 1)
    elif task in a.evacuated_by:
        if a.evacuated_by[task] == "dve":
            wait(dve, s.transposed, n.count(len(a.transposed), a.order(task) + 1))
            dve.tensor_copy(turned_into(m, a, n, task), m.tr16[:, :].rearrange("p (h q) -> p h q", h=2))\
               .then_inc(s.evacuated_dve, 1)
    elif task[0] == "Q":
        t = int(task[1])
        q = m.pj[:, 0:GROUP * HD].rearrange("p (h d) -> p h d", d=HD)
        k = m.pj[:, GROUP * HD:2 * GROUP * HD].rearrange("p (h d) -> p h d", d=HD)
        wait(dve, s.heads_high, n.count(4, t + 1))
        dve.scalar_tensor_tensor(out=m.tmq[:, t, :, 0:HD], in0=q, scalar=1 / WSCALE, in1=m.tmq[:, t, :, HD:P],
                                 op0=ALU.mult, op1=ALU.subtract)
        dve.scalar_tensor_tensor(out=m.tmk[:, t, :, P:P + HD], in0=k, scalar=1 / WSCALE, in1=m.tmk[:, t, :, 0:HD],
                                 op0=ALU.mult, op1=ALU.subtract).then_inc(s.projection_free, 1)
    elif task[0] == "V":
        t = int(task[1])
        v = m.vb[n.g % 2]
        wait(dve, s.v_high, n.count(4, t + 1))
        dve.scalar_tensor_tensor(out=v[:, t, :, VW:VW + HD], in0=m.pj[:, 0:GROUP * HD].rearrange("p (h d) -> p h d", d=HD),
                                 scalar=1 / WSCALE, in1=v[:, t, :, 0:HD],
                                 op0=ALU.mult, op1=ALU.subtract).then_inc(s.projection_free, 1)
    elif task[:2] == "vl":
        t = int(task[2])
        v = m.vb[n.g % 2]
        wait(dve, s.v_high, n.count(4, t + 1))
        dve.scalar_tensor_tensor(out=v[:, t, 0, VW:VW + HD], in0=m.pj[:, (GROUP + 1) * HD:(GROUP + 2) * HD],
                                 scalar=1 / WSCALE, in1=v[:, t, 0, 0:HD],
                                 op0=ALU.mult, op1=ALU.subtract).then_inc(s.projection_free, 1)
    elif task[0] == "P":
        t = int(task[1])
        heads = GROUP + 1
        wait(dve, s.projected, n.count(4, t + 1))
        wait(dve, s.rope_sum, n.count(4, t))
        qk = m.pj[:, 0:heads * HD]
        dve.tensor_tensor(m.rope1[:, :, :], qk.rearrange("p (h d) -> p h d", d=HD),
                          m.cos[:, t, :].unsqueeze(1).to_broadcast([P, heads, HD]), ALU.mult)
        halves = qk.rearrange("p (h x d) -> p h x d", x=2, d=HD // 2)[:, :, ::-1, :]
        dve.tensor_tensor(m.rope2[:, :, :].rearrange("p h (x d) -> p h x d", x=2), halves,
                          m.sin[:, t, :].rearrange("p (x d) -> p x d", x=2).unsqueeze(1)
                          .to_broadcast([P, heads, 2, HD // 2]), ALU.mult).then_inc(s.rope_terms, 1)


def dve_step(dve, m, a, s, st, main=True, prep=True):
    n = st.next()
    first = isinstance(st.b, int) and (st.b, st.g) == (0, 0)
    for u in range(UNITS):
        if main and u % NT == 0 and not (u == 0 and first):
            before = st if u else (Step(st.b, st.g - 1) if st.g else Step(st.b - 1, STEPS - 1))
            dve_norm(dve, m, s, before, (u // NT - 1) % GROUP)
        ahead = u + AHEAD
        if ahead % NT not in a.pool_tiles:
            if ahead < UNITS and main:
                dve_low(dve, m, a, s, st, ahead)
            elif ahead >= UNITS and prep:
                dve_low(dve, m, a, s, n, ahead - UNITS)
        for task in a.tasks["dve"].get(u, []):
            last_batch = isinstance(st.b, int) and st.b == B - 1
            if task == "WO":
                if main and st.g == 0 and not first:
                    dve_add_output(dve, m, s, st.b - 1)
            elif not prep or task[:2] == "YT":
                continue
            elif task == "LX":
                if main and st.g == 1 and not last_batch:
                    dve_ln(dve, m, s, st.b + 1)
            elif task == "XL":
                if main and st.g == 1 and not last_batch:
                    dve_ln_low(dve, m, s, st.b + 1)
            elif task == "TX":
                if main and st.g == 2 and not last_batch:
                    dve_keep_x(dve, m, s, st.b + 1)
            else:
                if task == "TT23" and main and st.g == 0 and not first:
                    wait(dve, s.x_added, st.b)
                dve_task(dve, m, a, s, n, task)
    if main and st.g == 0 and not first:
        dve_stats(dve, m, st.b - 1).then_inc(s.stats, 1)


def attention_dve(dve, m, a, s):
    dve_ln(dve, m, s, 0)
    dve_ln_low(dve, m, s, 0)
    dve_keep_x(dve, m, s, 0)

    def ends(last):
        dve_norm(dve, m, s, last, GROUP - 1)
        dve_add_output(dve, m, s, B - 1)
        dve.wait_ge(s.x_added, B)
        dve_stats(dve, m, B - 1).then_inc(s.stats, 1)

    every_step(dve, lambda st, **k: dve_step(dve, m, a, s, st, **k), ends)




def pool_step(pool, m, a, s, st, main=True, prep=True):
    n = st.next()
    for u in range(UNITS):
        ahead = u + AHEAD
        if ahead % NT in a.pool_tiles:
            if ahead < UNITS and main:
                dve_low(pool, m, a, s, st, ahead)
            elif ahead >= UNITS and prep:
                dve_low(pool, m, a, s, n, ahead - UNITS)
        for task in a.tasks["pool"].get(u, []):
            if not prep:
                continue
            t = int(task[-1])
            if task[0] == "P":
                wait(pool, s.rope_terms, n.count(4, t + 1))
                wait(pool, s.heads_low, n.count(4, t - 1))
                pool.tensor_tensor(m.qr[:, t % 2, :, :], m.rope1[:, :, :], m.rope2[:, :, :], ALU.add)\
                    .then_inc(s.rope_sum, 1)
            else:
                wait(pool, s.heads_high, n.count(4, t + 1))
                pool.tensor_tensor(m.tmq[:, t, :, 0:HD], m.qr[:, t % 2, 0:GROUP, :], m.tmq[:, t, :, HD:P],
                                   ALU.subtract)
                pool.tensor_tensor(m.tmk[:, t, 0, P:P + HD], m.qr[:, t % 2, GROUP, :], m.tmk[:, t, 0, 0:HD],
                                   ALU.subtract).then_inc(s.heads_low, 1)


def attention_pool(pool, m, a, s):
    every_step(pool, lambda st, **k: pool_step(pool, m, a, s, st, **k), lambda last: None)



EXPERTS, HIDDEN, TOP = 8, 512, 2
TILES = B * NT
CHUNKS = HIDDEN // P
BLOCKS = (TILES * TOP + EXPERTS - 1 + 3) // 4 * 4
LOADS = 4
GATE_FLOOR = 1e-12
GATHERS = 8


class ExpertSignals:

    def __init__(self, new, phase):
        self.ln_done = new(f"{phase}_ln_done")
        self.ln_high = new(f"{phase}_ln_high")
        self.ln_low = new(f"{phase}_ln_low")
        self.x_turned = new(f"{phase}_x_turned")
        self.x_kept = new(f"{phase}_x_kept")
        self.row_kept = new(f"{phase}_row_kept")
        self.logits = new(f"{phase}_logits")
        self.logit_kept = new(f"{phase}_logit_kept")
        self.chosen = new(f"{phase}_chosen")
        self.placed = new(f"{phase}_placed")
        self.exped = new(f"{phase}_exped")
        self.route = new(f"{phase}_route")
        self.gated = new(f"{phase}_gated")
        self.scattered = new(f"{phase}_scattered")
        self.in_turned = new(f"{phase}_in_turned")
        self.in_kept = new(f"{phase}_in_kept")
        self.up = new(f"{phase}_up")
        self.gelu = new(f"{phase}_gelu")
        self.high = new(f"{phase}_high")
        self.low = new(f"{phase}_low")
        self.down = new(f"{phase}_down")
        self.out = new(f"{phase}_out")
        self.linked = new(f"{phase}_linked")
        self.x_added = new(f"{phase}_x_added")
        self.stats = new(f"{phase}_stats")
        self.expert = new(f"{phase}_expert")


def route_pe(pe, m, s):
    def batch(b):
        pe_turn_x(pe, m, s, b)
        wait(pe, s.x_kept, b + 1)
        wait(pe, s.logit_kept, b)
        for t in range(NT):
            out = m.pj[:, t * EXPERTS:(t + 1) * EXPERTS]
            tile = slice(t * P, (t + 1) * P)
            pe.matmul(out, m.xt[:, 0, tile], m.wg[:, 0, :], start=True, stop=False)
            pe.matmul(out, m.xt[:, 1, tile], m.wg[:, 0, :], start=False, stop=False)
            last = pe.matmul(out, m.xt[:, 0, tile], m.wg[:, 1, :], start=False, stop=True)
        last.then_inc(s.logits, 1)

    batch(0)
    with pe.Fori(1, B) as b:
        batch(b)
    wait(pe, s.chosen, 1)
    wait(pe, s.logit_kept, B)
    place = m.pj[:, 0:TILES * EXPERTS]
    pe.matmul(place, m.before[:, :], m.choice[:, :, :].rearrange("p n e -> p (n e)"), start=True, stop=False,
              skip_group_check=True)
    for n in range(TILES - 1):
        rest = TILES - 1 - n
        pe.matmul(place[:, (n + 1) * EXPERTS:].rearrange("p (n e) -> p n e", e=EXPERTS), m.ones[:, :],
                  m.choice[:, n:n + 1, :].to_broadcast([P, rest, EXPERTS]), start=False, stop=(rest == 1),
                  skip_group_check=True)
    pe.matmul(m.mx[:, 0, 0:TILES * EXPERTS], m.ones[:, :], m.choice[:, :, :].rearrange("p n e -> p (n e)"),
              start=True, stop=True).then_inc(s.placed, 1)


def route_act(act, m, s):
    act_ln_high(act, m, s, 0)
    with act.Fori(1, B) as b:
        act_ln_high(act, m, s, b, row_kept=s.row_kept)
    wait(act, s.route, 1)
    act.activation(m.gate_exp[:, :, :], m.gate_exp[:, :, :], ACT.Exp).then_inc(s.exped, 1)


def route_dve(dve, m, s):
    def batch(b):
        dve_ln(dve, m, s, b)
        dve_ln_low(dve, m, s, b)
        dve_keep_x(dve, m, s, b)
        wait(dve, s.logits, b + 1)
        dve.scalar_tensor_tensor(out=m.logit[:, bass.ds(b * (NT * EXPERTS), NT * EXPERTS)]
                                 .rearrange("p (t e) -> p t e", e=EXPERTS),
                                 in0=m.pj[:, 0:NT * EXPERTS].rearrange("p (t e) -> p t e", e=EXPERTS),
                                 scalar=1 / WSCALE, in1=m.bg[:, :].unsqueeze(1).to_broadcast([P, NT, EXPERTS]),
                                 op0=ALU.mult, op1=ALU.add).then_inc(s.logit_kept, 1)
    batch(0)
    with dve.Fori(1, B) as b:
        batch(b)
    wait(dve, s.logit_kept, B)
    logit = m.logit[:, :].rearrange("p (n e) -> p n e", e=EXPERTS)
    all_ = [P, TILES, EXPERTS]
    done = [0]

    def link(ins):
        done[0] += 1
        ins.then_inc(s.linked, 1)
        dve.wait_ge(s.linked, done[0])

    rank = m.rank[:, :].unsqueeze(1).to_broadcast(all_)
    over = lambda v: v.unsqueeze(2).to_broadcast(all_)
    for k, (src, one) in enumerate(((logit, m.one1), (m.t3, m.one2))):
        best = m.best[:, k, :]
        link(dve.tensor_reduce(best, src, AX.X, ALU.max))
        link(dve.tensor_tensor(m.t1[:, :, :], src if k == 0 else m.t3[:, :, :], over(best), ALU.is_equal))
        link(dve.tensor_tensor(m.t1[:, :, :], m.t1[:, :, :], rank, ALU.mult))
        link(dve.tensor_reduce(m.t2[:, :], m.t1[:, :, :], AX.X, ALU.max))
        link(dve.tensor_tensor(one[:, :, :], rank, over(m.t2[:, :]), ALU.is_equal))
        if k == 0:
            link(dve.scalar_tensor_tensor(out=m.t3[:, :, :], in0=one[:, :, :], scalar=-3e38, in1=logit,
                                          op0=ALU.mult, op1=ALU.add))
    dve.tensor_tensor(m.choice[:, :, :], m.one1[:, :, :], m.one2[:, :, :], ALU.add).then_inc(s.chosen, 1)
    dve.tensor_tensor(m.gate_exp[:, :, :], logit, over(m.best[:, 0, :]), ALU.subtract).then_inc(s.route, 1)
    dve.wait_ge(s.placed, 1)
    link(dve.tensor_reduce(m.count[:, 0, :], m.mx[:, 0, 0:TILES * EXPERTS].rearrange("p (n e) -> p e n", e=EXPERTS),
                           AX.X, ALU.add))
    by_tile = [P, EXPERTS, TILES]
    link(dve.tensor_tensor(m.t1b[:, :, :], m.tile_start[:, :].unsqueeze(1).to_broadcast(by_tile),
                           m.count[:, 0, :].unsqueeze(2).to_broadcast(by_tile), ALU.is_lt))
    link(dve.tensor_reduce(m.count[:, 1, :], m.t1b[:, :, :], AX.X, ALU.add))
    link(dve.tensor_tensor(m.t8[:, :, :], m.earlier[:, :, :],
                           m.count[:, 1, :].unsqueeze(1).to_broadcast([P, EXPERTS, EXPERTS]), ALU.mult))
    link(dve.tensor_reduce(m.count[:, 2, :], m.t8[:, :, :], AX.X, ALU.add))
    link(dve.scalar_tensor_tensor(out=m.t3[:, :, :], in0=m.count[:, 2:3, :].to_broadcast(all_), scalar=float(P),
                                  in1=m.pj[:, 0:TILES * EXPERTS].rearrange("p (n e) -> p n e", e=EXPERTS),
                                  op0=ALU.mult, op1=ALU.add))
    for k, one in enumerate((m.one1, m.one2)):
        link(dve.tensor_tensor(m.t1[:, :, :], m.t3[:, :, :], one[:, :, :], ALU.mult))
        link(dve.tensor_reduce(m.slot_f[:, k, :], m.t1[:, :, :], AX.X, ALU.add))
    dve.tensor_copy(m.slot[:, :, :], m.slot_f[:, :, :]).then_inc(s.route, 1)
    link(dve.tensor_tensor(m.count[:, 3, :], m.count[:, 1, :], m.count[:, 2, :], ALU.add))
    by_block = [P, BLOCKS, EXPERTS - 1]
    link(dve.tensor_tensor(m.t_blocks[:, :, :], m.block_no[:, :].unsqueeze(2).to_broadcast(by_block),
                           m.count[:, 3:4, 0:EXPERTS - 1].to_broadcast(by_block), ALU.is_ge))
    link(dve.tensor_reduce(m.expert_f[:, :], m.t_blocks[:, :, :], AX.X, ALU.add))
    dve.tensor_copy(m.expert[:, :], m.expert_f[:, :]).then_inc(s.expert, 1)
    dve.wait_ge(s.exped, 1)
    link(dve.tensor_reduce(m.t2[:, :], m.gate_exp[:, :, :], AX.X, ALU.add))
    link(dve.reciprocal(m.t2[:, :], m.t2[:, :]))
    link(dve.tensor_tensor(m.gate_exp[:, :, :], m.gate_exp[:, :, :], over(m.t2[:, :]), ALU.mult))
    for k, one in enumerate((m.one1, m.one2)):
        link(dve.tensor_tensor(m.t1[:, :, :], m.gate_exp[:, :, :], one[:, :, :], ALU.mult))
        link(dve.tensor_reduce(m.gate[:, k, :], m.t1[:, :, :], AX.X, ALU.add))
    link(dve.tensor_tensor(m.t2[:, :], m.gate[:, 0, :], m.gate[:, 1, :], ALU.add))
    link(dve.tensor_scalar(m.t2[:, :], m.t2[:, :], GATE_FLOOR, None, ALU.max))
    link(dve.reciprocal(m.t2[:, :], m.t2[:, :]))
    dve.tensor_tensor(m.gate[:, :, :], m.gate[:, :, :], m.t2[:, :].unsqueeze(1).to_broadcast([P, TOP, TILES]),
                      ALU.mult).then_inc(s.gated, 1)


def route_sp(sp, m, s):
    with sp.Fori(0, B) as b:
        wait(sp, s.ln_low, b + 1)
        sp.dma_start(m.rows[:, bass.ds(b * (NT * 2 * D), NT * 2 * D)],
                     m.xn16[:, :, :, :].rearrange("p t x d -> p (t x d)")).then_inc(s.row_kept, 16)


def scatter_pool(pool, m, s, g):
    pool.wait_ge(s.route, 2)
    pool.wait_ge(g.zeroed, 16)
    pool.wait_ge(s.row_kept, 16 * B)
    for n in range(TILES):
        for k in range(TOP):
            pool.indirect_dma_start(out=m.slots_in[:, :],
                                    out_offset=bass.IndirectOffsetOnAxis(ap=m.slot[:, k, n:n + 1], axis=0),
                                    in_=m.rows[:, n * 2 * D:(n + 1) * 2 * D], in_offset=None)\
                .then_inc(s.scattered, 16)


def blocks_sp(sp, m, s):
    sp.wait_ge(s.scattered, 16 * TILES * TOP)
    for j in range(LOADS):
        load_block(sp, m, s, j, j)
    with sp.Fori(0, BLOCKS // LOADS - 1) as i:
        for j in range(LOADS):
            store_block(sp, m, s, i * LOADS + j, j)
            load_block(sp, m, s, i * LOADS + (LOADS + j), j)
    for j in range(LOADS):
        store_block(sp, m, s, BLOCKS - LOADS + j, j)


def load_block(sp, m, s, block, j):
    wait(sp, s.in_turned, block - LOADS + 1)
    sp.dma_start(m.xb[:, j, :], m.slots_in[bass.ds(block * P, P), :]).then_inc(s.loaded[j], 16)


def store_block(sp, m, s, block, j):
    wait(sp, s.out, block + 1)
    sp.dma_start(m.slots_out[bass.ds(block * P, P), :], m.ob[:, j % 2, :]).then_inc(s.stored[j % 2], 16)


def block_turn(pe, m, s, block, j, rounds):
    wait(pe, s.loaded[j], rounds * 16 + (16 + s.turn * (16 * BLOCKS // LOADS)))
    wait(pe, s.in_kept, block)
    for part in range(2):
        last = pe.transpose(m.tr16[:, part * P:(part + 1) * P], m.xb[:, j, part * P:(part + 1) * P], m.ident16[:, :])
    last.then_inc(s.in_turned, 1)


def block_up(pe, m, s, block, j, e):
    wait(pe, s.in_kept, block + 1)
    wait(pe, s.gelu, block - 1)
    x = m.xbt[:, j % 2, :, :]
    for c in range(CHUNKS):
        out = m.st[:, j % 2, c * P:(c + 1) * P]
        w = [m.w1[:, part, bass.ds(e * HIDDEN + c * P, P)] for part in range(2)]
        pe.matmul(out, w[0], x[:, 0, :], start=True, stop=False)
        pe.matmul(out, w[0], x[:, 1, :], start=False, stop=False)
        last = pe.matmul(out, w[1], x[:, 0, :], start=False, stop=True)
    last.then_inc(s.up, 1)


def block_down(pe, m, s, block, j, e):
    wait(pe, s.low, block + 1)
    out = m.pvb[:, j % 2, 0:D]
    for c in range(CHUNKS):
        high, low = (x[:, j % 2, c * P:(c + 1) * P] for x in (m.ph, m.pl))
        w = [m.w2[:, part, bass.ds(e * HIDDEN + c * D, D)] for part in range(2)]
        pe.matmul(out, high, w[0], start=(c == 0), stop=False)
        pe.matmul(out, high, w[1], start=False, stop=False)
        last = pe.matmul(out, low, w[0], start=False, stop=(c == CHUNKS - 1))
    last.then_inc(s.down, 1)


def expert_of(eng, m, block):
    return eng.value_load(m.expert[0:1, bass.ds(block, 1)], min_val=0, max_val=EXPERTS - 1)


def blocks_pe(pe, m, s):
    pe.wait_ge(s.expert, 1)
    block_turn(pe, m, s, 0, 0, 0)
    e = expert_of(pe, m, 0)
    block_up(pe, m, s, 0, 0, e)

    def pair(rounds, j, last=False):
        block = rounds * LOADS + j
        if not last:
            block_turn(pe, m, s, block + 1, (j + 1) % LOADS, rounds + (j + 1) // LOADS)
            block_up(pe, m, s, block + 1, (j + 1) % LOADS, expert_of(pe, m, block + 1))
        block_down(pe, m, s, block, j, expert_of(pe, m, block))

    for j in range(LOADS):
        pair(0, j)
    with pe.Fori(1, BLOCKS // LOADS - 1) as i:
        for j in range(LOADS):
            pair(i, j)
    for j in range(LOADS):
        pair(BLOCKS // LOADS - 1, j, last=(j == LOADS - 1))


def blocks_act(act, m, s):
    act.wait_ge(s.expert, 1)
    with act.Fori(0, BLOCKS // LOADS) as i:
        for j in range(LOADS):
            block = i * LOADS + j
            e = expert_of(act, m, block)
            wait(act, s.up, block + 1)
            for c in range(CHUNKS):
                part = slice(c * P, (c + 1) * P)
                last = act.activation(m.pf[:, j, part], m.st[:, j % 2, part], ACT.Gelu,
                                      bias=m.b1[:, bass.ds(e * CHUNKS + c, 1)], scale=1 / WSCALE)
            last.then_inc(s.gelu, 1)


def blocks_dve(dve, m, s):
    dve.wait_ge(s.expert, 1)

    def keep_input(block, j):
        wait(dve, s.in_turned, block + 1)
        dve.tensor_copy(m.xbt[:, j % 2, :, :], m.tr16[:, 0:2 * P].rearrange("p (x q) -> p x q", x=2))\
            .then_inc(s.in_kept, 1)

    def split(block, j):
        wait(dve, s.gelu, block + 1)
        dve.tensor_copy(m.ph[:, j % 2, :], m.pf[:, j, :]).then_inc(s.high, 1)
        wait(dve, s.high, block + 1)
        dve.tensor_tensor(m.pl[:, j % 2, :], m.pf[:, j, :], m.ph[:, j % 2, :], ALU.subtract).then_inc(s.low, 1)

    def keep_output(rounds, j):
        block = rounds * LOADS + j
        e = expert_of(dve, m, block)
        wait(dve, s.down, block + 1)
        wait(dve, s.stored[j % 2], rounds * (8 * LOADS) + (16 * (j // 2) + s.turn * 8 * BLOCKS))
        dve.scalar_tensor_tensor(out=m.ob[:, j % 2, :], in0=m.pvb[:, j % 2, 0:D], scalar=1 / WSCALE,
                                 in1=m.b2[:, bass.ds(e * D, D)], op0=ALU.mult, op1=ALU.add).then_inc(s.out, 1)

    def step(rounds, j, last=False):
        block = rounds * LOADS + j
        if not last:
            keep_input(block + 1, (j + 1) % LOADS)
        split(block, j)
        keep_output(rounds, j)

    keep_input(0, 0)
    for j in range(LOADS + 1):
        step(j // LOADS, j % LOADS)
    with dve.Fori(1, BLOCKS // LOADS - 1) as i:
        for j in range(1, LOADS + 1):
            step(i + j // LOADS, j % LOADS)
    for j in range(1, LOADS):
        step(BLOCKS // LOADS - 1, j, last=(j == LOADS - 1))


def gather_pool(pool, m, s):
    for stored in s.stored:
        pool.wait_ge(stored, 8 * BLOCKS * (s.turn + 1))
    pool.wait_ge(s.gated, 1)
    for n in range(TILES):
        for k in range(TOP):
            c = n * TOP + k
            if c >= GATHERS:
                pool.wait_ge(s.x_added, c - GATHERS + 1)
            pool.indirect_dma_start(out=m.back[:, c % GATHERS, :], out_offset=None, in_=m.slots_out[:, :],
                                    in_offset=bass.IndirectOffsetOnAxis(ap=m.slot[:, k, n:n + 1], axis=0))\
                .then_inc(s.gathered[c % GATHERS], 16)


def gather_dve(dve, m, s):
    for n in range(TILES):
        for k in range(TOP):
            c = n * TOP + k
            dve.wait_ge(s.gathered[c % GATHERS], 16 * (c // GATHERS + 1 + s.turn * TOP * TILES // GATHERS))
            if k:
                dve.wait_ge(s.x_added, c)
            x = m.x[:, n * D:(n + 1) * D]
            dve.scalar_tensor_tensor(out=x, in0=m.back[:, c % GATHERS, :], scalar=m.gate[:, k, n:n + 1], in1=x,
                                     op0=ALU.mult, op1=ALU.add).then_inc(s.x_added, 1)




def act_std(act, m, g, k):
    act.wait_ge(g.moments, 3 * k + 3)
    act.activation(m.std[:, :], m.var[:, :], ACT.Sqrt, scale=1 / D, bias=m.eps[:, 0:1]).then_inc(g.std_ready, 1)


def dve_rstd(dve, m, g, k, stats, count):
    bn = m.bn[:, :].rearrange("p (n v) -> p v n", v=BN)
    mean_e, sum_e, mean_o, sum_o = (bn[:, v, :] for v in (1, 2, 4, 5))
    dve.wait_ge(stats, count)
    dve.tensor_tensor(m.half[:, :], mean_e, mean_o, ALU.subtract)
    dve.tensor_tensor(m.var[:, :], sum_e, sum_o, ALU.add)
    dve.tensor_tensor(m.mean[:, :], mean_e, mean_o, ALU.add).then_inc(g.moments, 1)
    dve.wait_ge(g.moments, 3 * k + 1)
    dve.tensor_scalar(m.mean[:, :], m.mean[:, :], 0.5, None, ALU.mult)
    dve.scalar_tensor_tensor(out=m.half[:, :], in0=m.half[:, :], scalar=D / 4, in1=m.half[:, :],
                             op0=ALU.mult, op1=ALU.mult).then_inc(g.moments, 1)
    dve.wait_ge(g.moments, 3 * k + 2)
    dve.tensor_tensor(m.var[:, :], m.var[:, :], m.half[:, :], ALU.add).then_inc(g.moments, 1)
    dve.wait_ge(g.std_ready, k + 1)
    dve.reciprocal(m.rstd[:, :], m.std[:, :]).then_inc(g.rstd_ready, 1)
    dve.wait_ge(g.rstd_ready, k + 1)


class Memory:
    pass


class GlobalSignals:
    def __init__(self, new):
        self.x_loaded, self.loaded, self.zeroed, self.stored = (new(n) for n in ("x_loaded", "loaded", "zeroed", "stored"))
        self.weights_high, self.weights_low = new("weights_high"), new("weights_low")
        self.cleared, self.consts = new("cleared"), new("consts")
        self.moments, self.std_ready, self.rstd_ready = new("moments"), new("std_ready"), new("rstd_ready")


def build(nc, x, a_w, a_wo, b_w, b_wo, cos, sin, wg, bg, w1, b1, w2, b2, out, upto=4):
    ctx = ExitStack()
    with ctx:
        def sb(name, shape, dt):
            return ctx.enter_context(nc.sbuf_tensor(name, shape, dt))

        def ps(name, shape, dt):
            return ctx.enter_context(nc.psum_tensor(name, shape, dt))

        def sem(name):
            return ctx.enter_context(nc.semaphore(name))

        a, b = spec_a(), spec_b()
        m = Memory()
        m.x = sb("x", [P, B * NT * D], F32)
        m.mean = sb("mean", [P, B * NT], F32)
        m.var = sb("var", [P, B * NT], F32)
        m.std = sb("std", [P, B * NT], F32)
        m.rstd = sb("rstd", [P, B * NT], F32)
        m.eps = sb("eps", [P, 1], F32)
        m.bn = sb("bn", [P, TILES * BN], F32)
        m.half = sb("half", [P, TILES], F32)
        m.xn = sb("xn", [P, NT, D], F32)
        m.xn16 = sb("xn16", [P, NT, 2, D], F16)
        m.xt = sb("xt", [P, 2, T], F16)
        m.w = {"a": sb("wa", [P, 2, STEPS, a.columns], F16), "b": sb("wb", [P, 2, STEPS, b.columns], F16)}
        m.wo = {"a": sb("woa", [P, HEADS // 2, D], F32), "b": sb("wob", [P, HEADS // 2, D], F32)}
        m.cos = sb("cos", [P, NT, HD], F32)
        m.sin = sb("sin", [P, NT, HD], F32)
        m.ident16 = sb("ident16", [P, P], F16)
        m.ident32 = sb("ident32", [P, P], F32)
        m.mask_q = sb("mask_q", [P, P], F16)
        m.mask_k = sb("mask_k", [P, P], F16)
        m.tmq = sb("tmq", [P, NT, GROUP, 3 * HD], F16)
        m.tmk = sb("tmk", [P, NT, GROUP, 4 * HD], F16)
        qt = sb("qt", [P, 2, GROUP, T], F16)
        tt = sb("tt", [P, 2, GROUP, T], F16)
        kt = sb("kt", [P, 2, 2, GROUP, T], F16)
        m.qt, m.tt, m.kt = ([v[:, i] for i in range(2)] for v in (qt, tt, kt))
        m.vb = [sb(f"vb{i}", [P, NT, GROUP, VW + HD], F16) for i in range(2)]
        m.pf = sb("pf", [P, RING, T], F32)
        m.ph = sb("ph", [P, RING, T], F16)
        m.pl = sb("pl", [P, RING, T], F16)
        m.rope1 = sb("rope1", [P, GROUP + 1, HD], F32)
        m.rope2 = sb("rope2", [P, GROUP + 1, HD], F32)
        m.qr = sb("qr", [P, 2, GROUP + 1, HD], F32)
        m.rs = sb("rs", [P, 2, NT], F32)
        m.y = sb("y", [P, NT, GROUP, HD], F32)
        m.yt = sb("yt", [P, HEADS // 2, T], F32)
        m.pj = ps("pj", [P, 512], F32)
        m.mx = ps("mx", [P, 2, 512], F32)
        m.st = ps("st", [P, 2, 512], F32)
        pv = ps("pv", [P, 2, 512], F32)
        m.pv = pv[:, :, 0:NT * VW].rearrange("p b (t v) -> p b t v", t=NT)
        m.tr32 = ps("tr", [P, 512], F32)
        m.tr16 = m.tr32[:, :].bitcast(F16)
        m.rows = sb("rows", [P, TILES * 2 * D], F16)
        m.w1 = sb("w1", [P, 2, EXPERTS * HIDDEN], F16)
        m.w2 = sb("w2", [P, 2, EXPERTS * HIDDEN], F16)
        m.wg = sb("wg", [P, 2, EXPERTS], F16)
        m.wg_f = sb("wg_f", [P, EXPERTS], F32)
        m.bg = sb("bg", [P, EXPERTS], F32)
        m.b1 = sb("b1", [P, EXPERTS * CHUNKS], F32)
        m.b2 = sb("b2", [P, EXPERTS * D], F32)
        m.before = sb("before", [P, P], F16)
        m.ones = sb("ones", [P, P], F16)
        m.rank = sb("rank", [P, EXPERTS], F32)
        m.earlier = sb("earlier", [P, EXPERTS, EXPERTS], F32)
        m.tile_start = sb("tile_start", [P, TILES], F32)
        m.block_no = sb("block_no", [P, BLOCKS], F32)
        m.best = sb("best", [P, TOP, TILES], F32)
        m.t2 = sb("t2", [P, TILES], F32)
        m.count = sb("count", [P, 4, EXPERTS], F32)
        m.t8 = sb("t8", [P, EXPERTS, EXPERTS], F32)
        m.slot_f = sb("slot_f", [P, TOP, TILES], F32)
        m.slot = sb("slot", [P, TOP, TILES], mybir.dt.uint32)
        m.gate = sb("gate", [P, TOP, TILES], F32)
        m.expert = sb("expert", [P, BLOCKS], mybir.dt.int32)
        m.expert_f = sb("expert_f", [P, BLOCKS], F32)
        m.xb = sb("xb", [P, LOADS, 2 * D], F16)
        m.xbt = sb("xbt", [P, 2, 2, P], F16)
        m.ob = sb("ob", [P, 2, D], F32)
        free = kt[:, :, :, :, :].rearrange("p a b c d -> p (a b c d)").bitcast(F32)
        cut = lambda k: free[:, k * 256:(k + 1) * 256].rearrange("p (n e) -> p n e", e=EXPERTS)
        m.logit = free[:, 0:256]
        m.one1, m.one2, m.t1, m.t3, m.gate_exp = (cut(k) for k in range(1, 6))
        m.t1b = free[:, 1536:1792].rearrange("p (e n) -> p e n", e=EXPERTS)
        m.t_blocks = free[:, 2048:2048 + BLOCKS * (EXPERTS - 1)].rearrange("p (j e) -> p j e", e=EXPERTS - 1)
        m.choice = free[:, 1792:1920].bitcast(F16).rearrange("p (n e) -> p n e", e=EXPERTS)
        m.back = m.y[:, :, :, :].rearrange("p t h d -> p (t h d)").rearrange("p (c d) -> p c d", d=D)
        m.pvb = pv
        stage = {"a": m.pf[:, :, :].rearrange("p a b -> p (a b)")[:, 0:STEPS * a.columns],
                 "b": free[:, 0:STEPS * b.columns],
                 "w1": m.yt[:, :, :].rearrange("p a b -> p (a b)"),
                 "w2": m.rows[:, :].bitcast(F32), "wg": m.wg_f[:, :]}
        split = {"a": m.w["a"][:, :, :, :].rearrange("p x g c -> p x (g c)"),
                 "b": m.w["b"][:, :, :, :].rearrange("p x g c -> p x (g c)"),
                 "w1": m.w1, "w2": m.w2, "wg": m.wg}
        m.slots_in = nc.dram_tensor("slots_in", [BLOCKS * P, 2 * D], F16, kind="Internal").ap()
        m.slots_out = nc.dram_tensor("slots_out", [BLOCKS * P, D], F32, kind="Internal").ap()

        g = GlobalSignals(sem)
        attention = {"a": (a, AttentionSignals(sem, "a")), "b": (b, AttentionSignals(sem, "b"))}
        experts = [ExpertSignals(sem, f"experts{k}") for k in range(2)]
        loaded = [sem(f"loaded{k}") for k in range(LOADS)]
        stored = [sem(f"stored{k}") for k in range(2)]
        gathered = [sem(f"gathered{k}") for k in range(GATHERS)]
        for turn, s in enumerate(experts):
            s.loaded, s.stored, s.gathered, s.turn = loaded, stored, gathered, turn
        first_stats = sem("first_stats")
        weights = ("a", "b", "w1", "w2", "wg")
        loaded_weights = {name: sem(f"loaded_{name}") for name in weights}
        phases = ("a", 0, "b", 1)[:upto]
        stats = [(first_stats, 1)] + [(attention[k][1].stats, B) if k in attention else (experts[k].stats, 1)
                                      for k in phases]
        block = ctx.enter_context(nc.Block())

        @block.sync
        def _(sp):
            sp.dma_start(m.x[:, :].rearrange("p (n d) -> p n d", d=D), x.rearrange("(n p) d -> p n d", p=P))\
              .then_inc(g.x_loaded, 16)
            for name, src in zip(weights, (a_w, b_w, w1, w2, wg)):
                sp.dma_start(stage[name], src).then_inc(loaded_weights[name], 16)
            sp.dma_start(m.cos[:, :, :], cos).then_inc(g.loaded, 16)
            sp.dma_start(m.sin[:, :, :], sin).then_inc(g.loaded, 16)
            sp.dma_start(m.wo["a"][:, :, :], a_wo).then_inc(g.loaded, 16)
            sp.dma_start(m.wo["b"][:, :, :], b_wo).then_inc(g.loaded, 16)
            sp.dma_start(m.b1[:, :], b1).then_inc(g.loaded, 16)
            sp.dma_start(m.bg[:, :], bg.partition_broadcast(P)).then_inc(g.loaded, 16)
            sp.dma_start(m.b2[:, :], b2.partition_broadcast(P)).then_inc(g.loaded, 16)
            sp.wait_ge(g.cleared, 1)
            sp.dma_start(m.slots_in.rearrange("(j p) c -> p j c", p=P),
                         m.xb[:, 0:1, :].to_broadcast([P, BLOCKS, 2 * D])).then_inc(g.zeroed, 16)
            for k in phases:
                if k in (0, 1):
                    route_sp(sp, m, experts[k])
                    blocks_sp(sp, m, experts[k])
            sp.wait_ge(*stats[-1])
            sp.dma_start(out.rearrange("(n p) d -> p n d", p=P), m.x[:, :].rearrange("p (n d) -> p n d", d=D))\
              .then_inc(g.stored, 16)
            sp.wait_ge(g.stored, 16)

        @block.gpsimd
        def _(pool):
            pool.memset(m.xb[:, 0, :], 0.0)
            for t in (m.ident16, m.ident32, m.mask_q, m.mask_k):
                pool.memset(t[:, :], 0.0)
            pool.memset(m.ones[:, :], 1.0)
            pool.memset(m.before[:, :], 1.0)
            pool.memset(m.earlier[:, :, :], 1.0)
            pool.memset(m.tmq[:, :, :, P:3 * HD], 0.0)
            pool.memset(m.tmk[:, :, :, 3 * HD:4 * HD], 0.0).then_inc(g.cleared, 1)
            pool.wait_ge(g.cleared, 1)
            for i in range(2):
                pool.memset(m.vb[i][:, :, :, HD:HD + 1], 1.0)
                pool.memset(m.vb[i][:, :, :, HD + 1:VW], 0.0)
            pool.memset(m.tmk[:, :, :, 3 * HD:3 * HD + 1], -1.0)
            for t in (m.ident16, m.ident32):
                pool.affine_select(out=t[:, :], in_=t[:, :], compare_op=ALU.not_equal, fill=1.0, base=0,
                                   pattern=[[-1, P]], channel_multiplier=1)
            pool.affine_select(out=m.mask_q[:, :], in_=m.mask_q[:, :], compare_op=ALU.is_ge, fill=MASKED, base=0,
                               pattern=[[-1, P]], channel_multiplier=1)
            pool.affine_select(out=m.mask_k[:, :], in_=m.mask_k[:, :], compare_op=ALU.is_ge, fill=MASKED, base=0,
                               pattern=[[1, P]], channel_multiplier=-1)
            pool.affine_select(out=m.before[:, :], in_=m.before[:, :], compare_op=ALU.is_gt, fill=0.0, base=0,
                               pattern=[[1, P]], channel_multiplier=-1)
            pool.affine_select(out=m.earlier[:, :, :], in_=m.earlier[:, :, :], compare_op=ALU.is_gt, fill=0.0,
                               base=0, pattern=[[1, EXPERTS], [-1, EXPERTS]], channel_multiplier=0)
            exact = dict(allow_small_or_imprecise_dtypes=True)
            pool.iota(m.rank[:, :], [[-1, EXPERTS]], base=EXPERTS, channel_multiplier=0, **exact)
            pool.iota(m.tile_start[:, :], [[P, TILES]], base=0, channel_multiplier=0, **exact)
            pool.iota(m.block_no[:, :], [[1, BLOCKS]], base=0, channel_multiplier=0, **exact).then_inc(g.consts, 1)
            for k in phases:
                if k in (0, 1):
                    scatter_pool(pool, m, experts[k], g)
                    gather_pool(pool, m, experts[k])
                else:
                    attention_pool(pool, m, *attention[k])

        @block.scalar
        def _(act):
            for name in weights:
                act.wait_ge(loaded_weights[name], 16)
                act.activation(split[name][:, 0, :], stage[name], ACT.Copy, scale=WSCALE)\
                   .then_inc(g.weights_high, 1)
            for n, k in enumerate(phases):
                act_std(act, m, g, n)
                if k in (0, 1):
                    route_act(act, m, experts[k])
                    blocks_act(act, m, experts[k])
                else:
                    attention_act(act, m, *attention[k])

        @block.vector
        def _(dve):
            dve.memset(m.eps[:, :], EPS)
            for k, name in enumerate(weights):
                dve.wait_ge(g.weights_high, k + 1)
                dve.scalar_tensor_tensor(out=split[name][:, 1, :], in0=stage[name], scalar=WSCALE,
                                         in1=split[name][:, 0, :], op0=ALU.mult, op1=ALU.subtract)\
                   .then_inc(g.weights_low, 1)
            dve.wait_ge(g.x_loaded, 16)
            stats_dve(dve, m, first_stats)
            dve.wait_ge(g.loaded, 16 * 7)
            dve.wait_ge(g.consts, 1)
            for n, k in enumerate(phases):
                dve_rstd(dve, m, g, n, *stats[n])
                if k in (0, 1):
                    s = experts[k]
                    route_dve(dve, m, s)
                    blocks_dve(dve, m, s)
                    gather_dve(dve, m, s)
                    dve.wait_ge(s.x_added, TOP * TILES)
                    stats_dve(dve, m, s.stats)
                else:
                    attention_dve(dve, m, *attention[k])

        @block.tensor
        def _(pe):
            pe.wait_ge(g.consts, 1)
            pe.wait_ge(g.weights_low, len(weights))
            pe.wait_ge(g.loaded, 16 * 7)
            for k in phases:
                if k in (0, 1):
                    route_pe(pe, m, experts[k])
                    blocks_pe(pe, m, experts[k])
                else:
                    attention_pe(pe, m, *attention[k])


def stats_dve(dve, m, stats):
    with dve.Fori(0, B - 1) as b:
        dve_stats(dve, m, b)
    dve_stats(dve, m, B - 1).then_inc(stats, 1)


def lay_out(inputs):
    f = np.float32
    A = lambda n: np.ascontiguousarray(inputs["L0_" + n])
    wq = A("attn_a_Wq").reshape(D, STEPS, GROUP, HD // 2, 2).transpose(0, 1, 2, 4, 3).reshape(D, STEPS, GROUP * HD)
    wk = A("attn_a_Wk").reshape(D, STEPS, HD // 2, 2).transpose(0, 1, 3, 2).reshape(D, STEPS, HD)
    wv = A("attn_a_Wv").reshape(D, STEPS, HD)
    a_w = np.concatenate([wq, wk, wv], axis=2).reshape(D, -1)
    b_w = A("attn_b_W_qkv").reshape(D, STEPS, GROUP, HD, 3).transpose(0, 1, 4, 2, 3).reshape(D, -1)
    wo = lambda n: A(n).reshape(HEADS // 2, P, D).transpose(1, 0, 2)
    inv = (f(1) / f(10000.0) ** (np.arange(0, HD, 2, dtype=f) / f(HD))).astype(f)
    ang = (np.arange(T, dtype=f)[:, None] * inv[None, :]).astype(f)
    c, s = np.cos(ang).astype(f) / f(WSCALE), np.sin(ang).astype(f) / f(WSCALE)
    tiles = lambda v: v.reshape(NT, P, HD).transpose(1, 0, 2)
    arrays = {"x": A("attn_a_x").reshape(B * T, D), "a_w": a_w, "a_wo": wo("attn_a_Wo"), "b_w": b_w,
            "b_wo": wo("attn_b_W_out"), "cos": tiles(np.concatenate([c, c], 1)),
            "sin": tiles(np.concatenate([-s, s], 1)),
            "wg": A("ffn_Wg"), "bg": A("ffn_bg"), "w1": A("ffn_W1").transpose(1, 0, 2).reshape(D, -1),
            "b1": A("ffn_b1").reshape(EXPERTS, CHUNKS, P).transpose(2, 0, 1).reshape(P, -1),
            "w2": A("ffn_W2").reshape(EXPERTS, CHUNKS, P, D).transpose(2, 0, 1, 3).reshape(P, -1),
            "b2": A("ffn_b2").reshape(-1)}
    return {name: np.ascontiguousarray(v) for name, v in arrays.items()}




def kernel(**inputs):
    import concourse.bacc as bacc
    from concourse.bass_utils import run_bass_kernel_spmd

    nc = bacc.Bacc("TRN2", target_bir_lowering=False, num_devices=1)
    arrays = lay_out(inputs)
    args = [nc.dram_tensor(f"in_{name}_dram", v.shape, mybir.dt.from_np(v.dtype), kind="ExternalInput").ap()
            for name, v in arrays.items()]
    args.append(nc.dram_tensor("out_0_dram", (B * T, D), F32, kind="ExternalOutput").ap())
    build(nc, *args)
    r = run_bass_kernel_spmd(nc, [{f"in_{name}_dram": v for name, v in arrays.items()}], core_ids=[0])
    return r.results[0]["out_0_dram"].reshape(B, T, D)
```

```python
from contextlib import ExitStack

import numpy as np

import concourse.bass as bass
from concourse import mybir

F32 = mybir.dt.float32
F16 = mybir.dt.float16
ALU = mybir.AluOpType
ACT = mybir.ActivationFunctionType
AX = mybir.AxisListType

B, T, D = 8, 512, 128
P = 128
NT = T // P
HEADS, HD = 16, 64
GROUP = 4
STEPS = HEADS // GROUP
UNITS = GROUP * NT
AHEAD = 2
RING = 4
WSCALE = 64.0
EPS = 1e-5
MASKED = -60000.0
BN = 6
VW = HD + 2


class Step:

    def __init__(self, b, g):
        self.b, self.g = b, g

    def count(self, per_step, k):
        return self.b * (STEPS * per_step) + (self.g * per_step + k)

    def next(self):
        return Step(self.b, self.g + 1) if self.g + 1 < STEPS else Step(self.b + 1, 0)

    def previous(self):
        return Step(self.b, self.g - 1) if self.g else Step(self.b - 1, STEPS - 1)

    def is_first(self):
        return isinstance(self.b, int) and (self.b, self.g) == (0, 0)

    def is_last_batch(self):
        return isinstance(self.b, int) and self.b == B - 1


def wait(eng, sem, value):
    if isinstance(value, int) and value <= 0:
        return
    eng.wait_ge(sem, value)


class Attention:

    def __init__(self, name, causal, rotary, kv, tasks, evacuated_by, pool_tiles):
        self.name, self.causal, self.rotary, self.kv = name, causal, rotary, kv
        self.queries_keys = (GROUP + kv) * HD
        self.columns = (GROUP + 2 * kv) * HD
        self.tasks = tasks
        self.evacuated_by = evacuated_by
        self.pool_tiles = pool_tiles
        self.transposed = [x for u in range(UNITS) for x in tasks[u].split() if x in evacuated_by]

    def order(self, task):
        return self.transposed.index(task)

    def evacuations(self, engine, upto):
        return sum(self.evacuated_by[x] == engine for x in self.transposed[:self.order(upto) + 1])

    def lows(self, on_pool, unit):
        return sum((u % NT in self.pool_tiles) == on_pool for u in range(unit + 1))


def first_attention():
    tasks = ["V0 TQ01", "V1 TK01", "V2 YT0", "V3 m00",
             "TQ23 m01 m02", "YT1 m03 m10", "WO m11 m12 TX", "m13 LX",
             "Q0 m20 m21 TT01", "m22 m23 qh0", "m30 XH", "Q1 m31",
             "Q2 m32 qh1 XL", "m33 qh2", "Q3", "TT23 qh3"]
    by = {"TK01": "dve", "TQ01": "dve", "TQ23": "act", "TT01": "dve", "TT23": "act"}
    return Attention("a", True, True, 1, tasks, by, (1, 3))


def second_attention():
    tasks = ["V0 TQ01", "V1 TK01", "V2 YT0 m00", "V3 TQ23 m01",
             "YT1 m02 m03", "TK23 m10 WO", "TX m11 m12", "TL01 m13 LX",
             "Q0 m20", "TT01 m21 m22 XH", "Q1 m23", "TL23 m30 m31 XL",
             "Q2 m32", "m33", "Q3", "TT23"]
    by = {"TQ01": "dve", "TK01": "dve", "TQ23": "dve", "TK23": "dve", "TL01": "act", "TL23": "act",
          "TT01": "dve", "TT23": "dve"}
    return Attention("b", False, False, GROUP, tasks, by, (1, 3))


class AttentionSignals:

    def __init__(self, new, phase):
        self.q_projected = new(f"{phase}_q_projected")
        self.q_free = new(f"{phase}_q_free")
        self.v_projected = new(f"{phase}_v_projected")
        self.v_free = new(f"{phase}_v_free")
        self.rope_sum = new(f"{phase}_rope_sum")
        self.heads_high = new(f"{phase}_heads_high")
        self.heads_low = new(f"{phase}_heads_low")
        self.v_high = new(f"{phase}_v_high")
        self.transposed = new(f"{phase}_transposed")
        self.evacuated_dve = new(f"{phase}_evacuated_dve")
        self.evacuated_act = new(f"{phase}_evacuated_act")
        self.max_scored = new(f"{phase}_max_scored")
        self.max_taken = new(f"{phase}_max_taken")
        self.scored = new(f"{phase}_scored")
        self.exped = new(f"{phase}_exped")
        self.low_dve = new(f"{phase}_low_dve")
        self.low_pool = new(f"{phase}_low_pool")
        self.mixed = new(f"{phase}_mixed")
        self.recip = new(f"{phase}_recip")
        self.normed = new(f"{phase}_normed")
        self.y_turned = new(f"{phase}_y_turned")
        self.y_kept = new(f"{phase}_y_kept")
        self.out_projected = new(f"{phase}_out_projected")
        self.x_added = new(f"{phase}_x_added")
        self.stats = new(f"{phase}_stats")
        self.ln_done = new(f"{phase}_ln_done")
        self.ln_high = new(f"{phase}_ln_high")
        self.ln_low = new(f"{phase}_ln_low")
        self.x_turned = new(f"{phase}_x_turned")
        self.x_kept = new(f"{phase}_x_kept")




def pe_projection(pe, m, a, s, n, task):
    t = int(task[1])
    cols = slice(0, a.queries_keys) if task[0] == "Q" else slice(a.queries_keys, a.columns)
    w = m.w[a.name][:, :, n.g, cols]
    out = m.pj[:, 0:cols.stop - cols.start]
    tile = slice(t * P, (t + 1) * P)
    pe.matmul(out, m.xt[:, 0, tile], w[:, 0, :], start=True, stop=False)
    pe.matmul(out, m.xt[:, 1, tile], w[:, 0, :], start=False, stop=False)
    pe.matmul(out, m.xt[:, 0, tile], w[:, 1, :], start=False, stop=True)\
      .then_inc(s.q_projected if task[0] == "Q" else s.v_projected, 1)


def turn_wait(pe, a, s, n, before):
    if before is None:
        before, ref = a.transposed[-1], Step(n.b, n.g - 1)
    else:
        ref = n
    if before == "TX":
        wait(pe, s.x_kept, n.b + 2)
    elif before[:2] == "YT":
        wait(pe, s.y_kept, Step(n.b, n.g - 2).count(2, int(before[2]) + 1))
    else:
        e = a.evacuated_by[before]
        sem = s.evacuated_dve if e == "dve" else s.evacuated_act
        per = a.evacuations(e, a.transposed[-1])
        wait(pe, sem, ref.count(per, a.evacuations(e, before)))


def pe_turn(pe, m, a, s, n, task):
    tmq, tmk = m.tmq[n.g % 2], m.tmk[n.g % 2]
    if task[1] == "T":
        wait(pe, s.max_taken, n.count(HEADS, 8 if task == "TT01" else 16))
    else:
        wait(pe, s.heads_low if a.rotary else s.q_free, n.count(4, 4))
    h0 = int(task[2])
    for j in range(2):
        for t in range(NT):
            if task[1] == "Q":
                src = tmq[:, t, h0 + j, 0:P]
            elif task[1] == "T":
                src = tmq[:, t, h0 + j, HD:HD + P]
            elif a.kv == 1:
                src = tmk[:, t, 0, j * P:(j + 1) * P]
            else:
                src = tmk[:, t, h0 + j, 0:P] if task[1] == "K" else tmk[:, t, h0 + j, P:2 * P]
            last = pe.transpose(m.tr16[:, (j * NT + t) * P:(j * NT + t + 1) * P], src, m.ident16[:, :])
    last.then_inc(s.transposed, 1)


def pe_turn_x(pe, m, s, b):
    wait(pe, s.ln_low, b + 1)
    for part in range(2):
        for t in range(NT):
            last = pe.transpose(m.tr16[:, (part * NT + t) * P:(part * NT + t + 1) * P],
                                m.xn16[:, t, part, :], m.ident16[:, :])
    last.then_inc(s.x_turned, 1)


def pe_max_scores(pe, m, a, s, n, task):
    par = n.g % 2
    h, qt = int(task[1]), int(task[2])
    k = NT * h + qt
    wait(pe, s.max_taken, n.count(UNITS, k - 1))
    if qt == 0 and h % 2 == 0:
        need = [x for x in (("TQ01", "TK01") if h == 0 else ("TQ23", "TK23")) if x in a.evacuated_by]
        for e in ("dve", "act"):
            mine = [x for x in need if a.evacuated_by[x] == e]
            if mine:
                wait(pe, s.evacuated_dve if e == "dve" else s.evacuated_act,
                     n.count(a.evacuations(e, a.transposed[-1]), a.evacuations(e, max(mine, key=a.order))))
    hk = 0 if a.kv == 1 else h
    keys = (qt + 1) * P if a.causal else T
    last = pe.matmul(m.mx[:, k % 2, 0:keys], m.qt[par][:, h, qt * P:(qt + 1) * P], m.kt[par][:, 0, hk, 0:keys],
                     start=True, stop=not a.causal, skip_group_check=True)
    if a.causal:
        last = pe.matmul(m.mx[:, k % 2, keys - P:keys], m.ident16[:, :], m.mask_q[:, :], start=False, stop=True,
                         skip_group_check=True)
    last.then_inc(s.max_scored, 1)


def pe_scores(pe, m, a, s, st, u):
    par = st.g % 2
    h, kc = divmod(u, NT)
    wait(pe, s.exped, st.count(UNITS, u - 1))
    if u in (0, UNITS // 2):
        upto = "TT01" if u == 0 else "TT23"
        for e in ("dve", "act"):
            per = a.evacuations(e, a.transposed[-1])
            if per:
                wait(pe, s.evacuated_dve if e == "dve" else s.evacuated_act, st.count(per, a.evacuations(e, upto)))
    hk = 0 if a.kv == 1 else h
    q0 = kc * P if a.causal else 0
    out = m.st[:, u % 2, q0:T]
    keys = slice(kc * P, (kc + 1) * P)
    pe.matmul(out, m.kt[par][:, 0, hk, keys], m.qt[par][:, h, q0:T], start=True, stop=False, skip_group_check=True)
    last = pe.matmul(out, m.kt[par][:, 1, hk, keys], m.tt[par][:, h, q0:T], start=False, stop=not a.causal,
                     skip_group_check=True)
    if a.causal:
        last = pe.matmul(m.st[:, u % 2, q0:q0 + P], m.ident16[:, :], m.mask_k[:, :], start=False, stop=True,
                         skip_group_check=True)
    last.then_inc(s.scored, 1)


def pe_mix(pe, m, a, s, st, u):
    par = st.g % 2
    h, kc = divmod(u, NT)
    on_pool = kc in a.pool_tiles
    wait(pe, s.low_pool if on_pool else s.low_dve, st.count(a.lows(on_pool, UNITS - 1), a.lows(on_pool, u)))
    if kc == 0:
        wait(pe, s.normed, st.count(GROUP, h - 1))
    if u == 0:
        wait(pe, s.v_free, st.count(4, 4))
    hv = 0 if a.kv == 1 else h
    v = m.vb[par]
    first = kc == 0
    r = u % RING
    for qt in range(kc if a.causal else 0, NT):
        q = slice(qt * P, (qt + 1) * P)
        pe.matmul(m.pv[:, h % 2, qt, :], m.ph[:, r, q], v[:, kc, hv, 0:VW], start=first, stop=False,
                  skip_group_check=True)
        first = False
        pe.matmul(m.pv[:, h % 2, qt, 0:HD], m.ph[:, r, q], v[:, kc, hv, VW:VW + HD], start=False, stop=False,
                  skip_group_check=True)
        last = pe.matmul(m.pv[:, h % 2, qt, :], m.pl[:, r, q], v[:, kc, hv, 0:VW], start=False,
                         stop=(kc == NT - 1), skip_group_check=True)
    last.then_inc(s.mixed, 1)


def pe_turn_y(pe, m, s, before, p):
    wait(pe, s.normed, before.count(GROUP, 2 * p + 2))
    for t in range(NT):
        last = pe.transpose(m.tr32[:, t * P:(t + 1) * P],
                            m.y[:, t, 2 * p:2 * p + 2, :].rearrange("p h d -> p (h d)"), m.ident32[:, :])
    last.then_inc(s.y_turned, 1)


def pe_output(pe, m, a, s, b):
    wait(pe, s.y_kept, b * (2 * STEPS) + 2 * STEPS)
    for t in range(NT):
        for p in range(HEADS // 2):
            last = pe.matmul(m.pj[:, t * P:(t + 1) * P], m.yt[:, p, t * P:(t + 1) * P], m.wo[a.name][:, p, :],
                             start=(p == 0), stop=(p == HEADS // 2 - 1))
    last.then_inc(s.out_projected, 1)


def pe_step(pe, m, a, s, st, main=True, prep=True, queries=True):
    n, n2 = st.next(), st.next().next()
    before = None
    for u in range(UNITS):
        ahead = u + AHEAD
        if ahead < UNITS and main:
            pe_scores(pe, m, a, s, st, ahead)
        elif ahead >= UNITS and prep:
            pe_scores(pe, m, a, s, n, ahead - UNITS)
        for task in a.tasks[u].split():
            if task[:2] == "YT" and main and not st.is_first():
                turn_wait(pe, a, s, n, before)
                pe_turn_y(pe, m, s, st.previous(), int(task[2]))
                before = task
            elif task == "WO" and main and st.g == 0 and not st.is_first():
                wait(pe, s.v_free, n.count(4, 4))
                pe_output(pe, m, a, s, st.b - 1)
            elif task == "TX" and main and st.g == 2 and not st.is_last_batch():
                turn_wait(pe, a, s, n, before)
                pe_turn_x(pe, m, s, st.b + 1)
                before = task
            elif task[0] == "V" and prep:
                t = int(task[1])
                wait(pe, s.v_free if t else s.q_free, n.count(4, t if t else 4))
                if t == 0 and n.is_first():
                    wait(pe, s.x_kept, 1)
                pe_projection(pe, m, a, s, n, task)
            elif task[0] == "Q" and queries:
                t = int(task[1])
                if t:
                    wait(pe, s.q_free, n2.count(4, t))
                else:
                    wait(pe, s.v_free, n.count(4, 4))
                    if main and st.g == 0 and not st.is_first():
                        wait(pe, s.x_added, st.b)
                    if n2.g == 0:
                        wait(pe, s.x_kept, n2.b + 1)
                pe_projection(pe, m, a, s, n2, task)
            elif task[0] == "m" and prep:
                pe_max_scores(pe, m, a, s, n, task)
            elif task in a.evacuated_by and prep:
                turn_wait(pe, a, s, n, before)
                pe_turn(pe, m, a, s, n, task)
                before = task
        if main:
            pe_mix(pe, m, a, s, st, u)


def every_step(eng, step, ends):
    step(Step(-1, STEPS - 2), main=False, prep=False)
    step(Step(-1, STEPS - 1), main=False)
    step(Step(0, 0))
    with eng.Fori(0, B - 1) as b:
        for g in range(1, STEPS):
            step(Step(b, g))
        step(Step(b + 1, 0))
    for g in range(1, STEPS):
        step(Step(B - 1, g), prep=(g < STEPS - 1), queries=(g < STEPS - 2))
    ends(Step(B - 1, STEPS - 1))


def attention_pe(pe, m, a, s):
    pe_turn_x(pe, m, s, 0)

    def ends(last):
        for p in range(2):
            wait(pe, s.y_kept, last.count(2, p))
            pe_turn_y(pe, m, s, last, p)
        pe_output(pe, m, a, s, B - 1)

    every_step(pe, lambda st, **k: pe_step(pe, m, a, s, st, **k), ends)




def act_exp(act, m, a, s, st, u):
    h, kc = divmod(u, NT)
    q0 = kc * P if a.causal else 0
    r = u % RING
    wait(act, s.scored, st.count(UNITS, u + 1))
    wait(act, s.mixed, st.count(UNITS, u - RING + 1))
    act.activation(m.pf[:, r, q0:T], m.st[:, u % 2, q0:T], ACT.Exp, scale=HD ** -0.5)
    act.activation(m.ph[:, r, q0:T], m.st[:, u % 2, q0:T], ACT.Exp, scale=HD ** -0.5).then_inc(s.exped, 1)


def act_values_high(act, m, a, s, n, t):
    wait(act, s.v_projected, n.count(4, t + 1))
    act.activation(m.vb[n.g % 2][:, t, 0:a.kv, 0:HD], m.pj[:, 0:a.kv * HD].rearrange("p (h d) -> p h d", d=HD),
                   ACT.Copy, scale=1 / WSCALE).then_inc(s.v_high, 1)


def act_heads_high(act, m, a, s, n, t):
    tmq, tmk = m.tmq[n.g % 2], m.tmk[n.g % 2]
    if a.rotary:
        wait(act, s.rope_sum, n.count(4, t + 1))
        q, k, scale = m.qr[:, t % 2, 0:GROUP, :], m.qr[:, t % 2, GROUP:GROUP + 1, :], 1.0
    else:
        wait(act, s.q_projected, n.count(4, t + 1))
        heads = m.pj[:, :].rearrange("p (h d) -> p h d", d=HD)
        q, k, scale = heads[:, 0:GROUP, :], heads[:, GROUP:2 * GROUP, :], 1 / WSCALE
    act.activation(tmq[:, t, :, HD:P], q, ACT.Copy, scale=scale)
    act.activation(tmk[:, t, 0:a.kv, 0:P].rearrange("p h (x d) -> p h x d", x=2),
                   k.unsqueeze(2).to_broadcast([P, a.kv, 2, HD]), ACT.Copy, scale=scale).then_inc(s.heads_high, 1)


def act_ln_high(act, m, s, b, row_kept=None):
    wait(act, s.ln_done, b + 1)
    if row_kept is not None:
        wait(act, row_kept, b * 16)
    wait(act, s.x_turned, b)
    act.activation(m.xn16[:, :, 0, :], m.xn[:, :, :], ACT.Copy).then_inc(s.ln_high, 1)


def act_keep_y(act, m, s, before, p):
    wait(act, s.y_turned, before.count(2, p + 1))
    act.activation(m.yt[:, 2 * before.g + p, :], m.tr32[:, :], ACT.Copy).then_inc(s.y_kept, 1)


def turned_into(m, a, n, task):
    par, h0 = n.g % 2, int(task[2])
    if task[1] == "Q":
        return m.qt[par][:, h0:h0 + 2, :]
    if task[1] == "T":
        return m.tt[par][:, h0:h0 + 2, :]
    if a.kv == 1:
        return m.kt[par][:, 0:2, 0, :]
    return m.kt[par][:, "KL".index(task[1]), h0:h0 + 2, :]


def act_step(act, m, a, s, st, main=True, prep=True, queries=True):
    n, n2 = st.next(), st.next().next()
    for u in range(UNITS):
        ahead = u + AHEAD
        if ahead < UNITS and main:
            act_exp(act, m, a, s, st, ahead)
        elif ahead >= UNITS and prep:
            act_exp(act, m, a, s, n, ahead - UNITS)
        for task in a.tasks[u].split():
            if task[:2] == "YT" and main and not st.is_first():
                act_keep_y(act, m, s, st.previous(), int(task[2]))
            elif task == "XH" and main and st.g == 1 and not st.is_last_batch():
                act_ln_high(act, m, s, st.b + 1)
            elif task[0] == "V" and prep:
                act_values_high(act, m, a, s, n, int(task[1]))
            elif task[:2] == ("qh" if a.rotary else "Q" + task[-1]) and queries:
                act_heads_high(act, m, a, s, n2, int(task[-1]))
            elif task in a.evacuated_by and prep and a.evacuated_by[task] == "act":
                wait(act, s.transposed, n.count(len(a.transposed), a.order(task) + 1))
                act.activation(turned_into(m, a, n, task), m.tr16[:, :].rearrange("p (h q) -> p h q", h=2),
                               ACT.Copy).then_inc(s.evacuated_act, 1)
    if main and st.g == 0:
        wait(act, s.out_projected, st.b)


def attention_act(act, m, a, s):
    act_ln_high(act, m, s, 0)

    def ends(last):
        for p in range(2):
            act_keep_y(act, m, s, last, p)

    every_step(act, lambda st, **k: act_step(act, m, a, s, st, **k), ends)




def dve_ln(dve, m, s, b):
    wait(dve, s.ln_low, b)
    for t in range(NT):
        last = dve.tensor_scalar(m.xn[:, t, :], m.x[:, bass.ds(b * (NT * D) + t * D, D)],
                                 m.mean[:, bass.ds(b * NT + t, 1)], m.rstd[:, bass.ds(b * NT + t, 1)],
                                 ALU.subtract, ALU.mult)
    last.then_inc(s.ln_done, 1)


def dve_ln_low(dve, m, s, b):
    wait(dve, s.ln_high, b + 1)
    dve.tensor_tensor(m.xn16[:, :, 1, :], m.xn[:, :, :], m.xn16[:, :, 0, :], ALU.subtract).then_inc(s.ln_low, 1)


def dve_keep_x(dve, m, s, b):
    wait(dve, s.x_turned, b + 1)
    dve.tensor_copy(m.xt[:, :, :], m.tr16[:, :].rearrange("p (x q) -> p x q", x=2)).then_inc(s.x_kept, 1)


def dve_stats(dve, m, b):
    for t in range(NT):
        last = dve.bn_stats(m.bn[:, bass.ds(b * (NT * BN) + t * BN, BN)], m.x[:, bass.ds(b * (NT * D) + t * D, D)])
    return last


def dve_add_output(dve, m, s, b):
    wait(dve, s.out_projected, b + 1)
    x = m.x[:, bass.ds(b * (NT * D), NT * D)]
    dve.tensor_tensor(x, m.pj[:, :], x, ALU.add).then_inc(s.x_added, 1)


def dve_low(dve, m, a, s, st, u):
    kc = u % NT
    q0 = kc * P if a.causal else 0
    r = u % RING
    wait(dve, s.exped, st.count(UNITS, u + 1))
    dve.tensor_tensor(m.pl[:, r, q0:T], m.pf[:, r, q0:T], m.ph[:, r, q0:T], ALU.subtract)\
        .then_inc(s.low_pool if kc in a.pool_tiles else s.low_dve, 1)


def dve_norm(dve, m, s, st, h):
    wait(dve, s.mixed, st.count(UNITS, NT * (h + 1)))
    if h % 2 == 0:
        wait(dve, s.y_turned, st.count(2, h // 2 - 1))
    dve.reciprocal(m.rs[:, h % 2, :], m.pv[:, h % 2, :, HD]).then_inc(s.recip, 1)
    wait(dve, s.recip, st.count(GROUP, h + 1))
    dve.tensor_tensor(m.y[:, :, h, :], m.pv[:, h % 2, :, 0:HD],
                      m.rs[:, h % 2, :].unsqueeze(2).to_broadcast([P, NT, HD]), ALU.mult).then_inc(s.normed, 1)


def dve_rope(dve, m, s, n, t):
    heads = GROUP + 1
    wait(dve, s.q_projected, n.count(4, t + 1))
    wait(dve, s.rope_sum, n.count(4, t))
    qk = m.pj[:, 0:heads * HD]
    dve.tensor_tensor(m.rope1[:, :, :], qk.rearrange("p (h d) -> p h d", d=HD),
                      m.cos[:, t, :].unsqueeze(1).to_broadcast([P, heads, HD]), ALU.mult)
    halves = qk.rearrange("p (h x d) -> p h x d", x=2, d=HD // 2)[:, :, ::-1, :]
    dve.tensor_tensor(m.rope2[:, :, :].rearrange("p h (x d) -> p h x d", x=2), halves,
                      m.sin[:, t, :].rearrange("p (x d) -> p x d", x=2).unsqueeze(1)
                      .to_broadcast([P, heads, 2, HD // 2]), ALU.mult).then_inc(s.q_free, 1)


def dve_heads_low(dve, m, s, n, t):
    tmq, tmk = m.tmq[n.g % 2], m.tmk[n.g % 2]
    heads = m.pj[:, :].rearrange("p (h d) -> p h d", d=HD)
    wait(dve, s.heads_high, n.count(4, t + 1))
    dve.scalar_tensor_tensor(out=tmq[:, t, :, 0:HD], in0=heads[:, 0:GROUP, :], scalar=1 / WSCALE,
                             in1=tmq[:, t, :, HD:P], op0=ALU.mult, op1=ALU.subtract)
    dve.scalar_tensor_tensor(out=tmk[:, t, :, P:P + HD], in0=heads[:, GROUP:2 * GROUP, :], scalar=1 / WSCALE,
                             in1=tmk[:, t, :, 0:HD], op0=ALU.mult, op1=ALU.subtract).then_inc(s.q_free, 1)


def dve_values_low(dve, m, a, s, n, t):
    v = m.vb[n.g % 2]
    wait(dve, s.v_high, n.count(4, t + 1))
    dve.scalar_tensor_tensor(out=v[:, t, 0:a.kv, VW:VW + HD],
                             in0=m.pj[:, 0:a.kv * HD].rearrange("p (h d) -> p h d", d=HD),
                             scalar=1 / WSCALE, in1=v[:, t, 0:a.kv, 0:HD],
                             op0=ALU.mult, op1=ALU.subtract).then_inc(s.v_free, 1)


def dve_max(dve, m, a, s, n, task):
    h, qt = int(task[1]), int(task[2])
    k = NT * h + qt
    wait(dve, s.max_scored, n.count(UNITS, k + 1))
    dve.tensor_reduce(m.tmq[n.g % 2][:, qt, h, P:P + 1], m.mx[:, k % 2, 0:(qt + 1) * P if a.causal else T],
                      AX.X, ALU.max).then_inc(s.max_taken, 1)


def dve_step(dve, m, a, s, st, main=True, prep=True, queries=True):
    n, n2 = st.next(), st.next().next()
    for u in range(UNITS):
        if main and u % NT == 0 and not (u == 0 and st.is_first()):
            dve_norm(dve, m, s, st if u else st.previous(), (u // NT - 1) % GROUP)
        ahead = u + AHEAD
        if ahead % NT not in a.pool_tiles:
            if ahead < UNITS and main:
                dve_low(dve, m, a, s, st, ahead)
            elif ahead >= UNITS and prep:
                dve_low(dve, m, a, s, n, ahead - UNITS)
        for task in a.tasks[u].split():
            if task == "WO" and main and st.g == 0 and not st.is_first():
                dve_add_output(dve, m, s, st.b - 1)
            elif task == "LX" and main and st.g == 1 and not st.is_last_batch():
                dve_ln(dve, m, s, st.b + 1)
            elif task == "XL" and main and st.g == 1 and not st.is_last_batch():
                dve_ln_low(dve, m, s, st.b + 1)
            elif task == "TX" and main and st.g == 2 and not st.is_last_batch():
                dve_keep_x(dve, m, s, st.b + 1)
            elif task[0] == "V" and prep:
                dve_values_low(dve, m, a, s, n, int(task[1]))
            elif task[0] == "Q" and queries:
                if a.rotary:
                    dve_rope(dve, m, s, n2, int(task[1]))
                else:
                    dve_heads_low(dve, m, s, n2, int(task[1]))
            elif task[0] == "m" and prep:
                if task == "m33" and main and st.g == 0 and not st.is_first():
                    wait(dve, s.x_added, st.b)
                dve_max(dve, m, a, s, n, task)
                if task == "m33" and main and st.g == 0 and not st.is_first():
                    dve_stats(dve, m, st.b - 1).then_inc(s.stats, 1)
            elif task in a.evacuated_by and prep and a.evacuated_by[task] == "dve":
                wait(dve, s.transposed, n.count(len(a.transposed), a.order(task) + 1))
                dve.tensor_copy(turned_into(m, a, n, task), m.tr16[:, :].rearrange("p (h q) -> p h q", h=2))\
                   .then_inc(s.evacuated_dve, 1)


def attention_dve(dve, m, a, s):
    dve_ln(dve, m, s, 0)
    dve_ln_low(dve, m, s, 0)
    dve_keep_x(dve, m, s, 0)

    def ends(last):
        dve_norm(dve, m, s, last, GROUP - 1)
        dve_add_output(dve, m, s, B - 1)
        dve.wait_ge(s.x_added, B)
        dve_stats(dve, m, B - 1).then_inc(s.stats, 1)

    every_step(dve, lambda st, **k: dve_step(dve, m, a, s, st, **k), ends)




def pool_step(pool, m, a, s, st, main=True, prep=True, queries=True):
    n, n2 = st.next(), st.next().next()
    for u in range(UNITS):
        ahead = u + AHEAD
        if ahead % NT in a.pool_tiles:
            if ahead < UNITS and main:
                dve_low(pool, m, a, s, st, ahead)
            elif ahead >= UNITS and prep:
                dve_low(pool, m, a, s, n, ahead - UNITS)
        for task in a.tasks[u].split():
            if not (a.rotary and queries and task[0] in "Qq"):
                continue
            t = int(task[-1])
            tmq, tmk = m.tmq[n2.g % 2], m.tmk[n2.g % 2]
            if task[0] == "Q":
                wait(pool, s.q_free, n2.count(4, t + 1))
                wait(pool, s.heads_low, n2.count(4, t - 1))
                pool.tensor_tensor(m.qr[:, t % 2, :, :], m.rope1[:, :, :], m.rope2[:, :, :], ALU.add)\
                    .then_inc(s.rope_sum, 1)
            else:
                wait(pool, s.heads_high, n2.count(4, t + 1))
                pool.tensor_tensor(tmq[:, t, :, 0:HD], m.qr[:, t % 2, 0:GROUP, :], tmq[:, t, :, HD:P],
                                   ALU.subtract)
                pool.tensor_tensor(tmk[:, t, 0, P:P + HD], m.qr[:, t % 2, GROUP, :], tmk[:, t, 0, 0:HD],
                                   ALU.subtract).then_inc(s.heads_low, 1)


def attention_pool(pool, m, a, s):
    every_step(pool, lambda st, **k: pool_step(pool, m, a, s, st, **k), lambda last: None)



EXPERTS, HIDDEN, TOP = 8, 512, 2
TILES = B * NT
CHUNKS = HIDDEN // P
BLOCKS = (TILES * TOP + EXPERTS - 1 + 3) // 4 * 4
LOADS = 4
GATE_FLOOR = 1e-12
GATHERS = 8


class ExpertSignals:

    def __init__(self, new, phase):
        self.ln_done = new(f"{phase}_ln_done")
        self.ln_high = new(f"{phase}_ln_high")
        self.ln_low = new(f"{phase}_ln_low")
        self.x_turned = new(f"{phase}_x_turned")
        self.x_kept = new(f"{phase}_x_kept")
        self.row_kept = new(f"{phase}_row_kept")
        self.logits = new(f"{phase}_logits")
        self.logit_kept = new(f"{phase}_logit_kept")
        self.chosen = new(f"{phase}_chosen")
        self.placed = new(f"{phase}_placed")
        self.exped = new(f"{phase}_exped")
        self.route = new(f"{phase}_route")
        self.gated = new(f"{phase}_gated")
        self.scattered = new(f"{phase}_scattered")
        self.in_turned = new(f"{phase}_in_turned")
        self.in_kept = new(f"{phase}_in_kept")
        self.up = new(f"{phase}_up")
        self.gelu = new(f"{phase}_gelu")
        self.high = new(f"{phase}_high")
        self.low = new(f"{phase}_low")
        self.down = new(f"{phase}_down")
        self.out = new(f"{phase}_out")
        self.linked = new(f"{phase}_linked")
        self.x_added = new(f"{phase}_x_added")
        self.stats = new(f"{phase}_stats")
        self.expert = new(f"{phase}_expert")


def route_pe(pe, m, s):
    def batch(b):
        pe_turn_x(pe, m, s, b)
        wait(pe, s.x_kept, b + 1)
        wait(pe, s.logit_kept, b)
        for t in range(NT):
            out = m.pj[:, t * EXPERTS:(t + 1) * EXPERTS]
            tile = slice(t * P, (t + 1) * P)
            pe.matmul(out, m.xt[:, 0, tile], m.wg[:, 0, :], start=True, stop=False)
            pe.matmul(out, m.xt[:, 1, tile], m.wg[:, 0, :], start=False, stop=False)
            last = pe.matmul(out, m.xt[:, 0, tile], m.wg[:, 1, :], start=False, stop=True)
        last.then_inc(s.logits, 1)

    batch(0)
    with pe.Fori(1, B) as b:
        batch(b)
    wait(pe, s.chosen, 1)
    wait(pe, s.logit_kept, B)
    place = m.pj[:, 0:TILES * EXPERTS]
    pe.matmul(place, m.before[:, :], m.choice[:, :, :].rearrange("p n e -> p (n e)"), start=True, stop=False,
              skip_group_check=True)
    for n in range(TILES - 1):
        rest = TILES - 1 - n
        pe.matmul(place[:, (n + 1) * EXPERTS:].rearrange("p (n e) -> p n e", e=EXPERTS), m.ones[:, :],
                  m.choice[:, n:n + 1, :].to_broadcast([P, rest, EXPERTS]), start=False, stop=(rest == 1),
                  skip_group_check=True)
    pe.matmul(m.mx[:, 0, 0:TILES * EXPERTS], m.ones[:, :], m.choice[:, :, :].rearrange("p n e -> p (n e)"),
              start=True, stop=True).then_inc(s.placed, 1)


def route_act(act, m, s):
    act_ln_high(act, m, s, 0)
    with act.Fori(1, B) as b:
        act_ln_high(act, m, s, b, row_kept=s.row_kept)
    wait(act, s.route, 1)
    act.activation(m.gate_exp[:, :, :], m.gate_exp[:, :, :], ACT.Exp).then_inc(s.exped, 1)


def route_dve(dve, m, s):
    def batch(b):
        dve_ln(dve, m, s, b)
        dve_ln_low(dve, m, s, b)
        dve_keep_x(dve, m, s, b)
        wait(dve, s.logits, b + 1)
        dve.scalar_tensor_tensor(out=m.logit[:, bass.ds(b * (NT * EXPERTS), NT * EXPERTS)]
                                 .rearrange("p (t e) -> p t e", e=EXPERTS),
                                 in0=m.pj[:, 0:NT * EXPERTS].rearrange("p (t e) -> p t e", e=EXPERTS),
                                 scalar=1 / WSCALE, in1=m.bg[:, :].unsqueeze(1).to_broadcast([P, NT, EXPERTS]),
                                 op0=ALU.mult, op1=ALU.add).then_inc(s.logit_kept, 1)
    batch(0)
    with dve.Fori(1, B) as b:
        batch(b)
    wait(dve, s.logit_kept, B)
    logit = m.logit[:, :].rearrange("p (n e) -> p n e", e=EXPERTS)
    all_ = [P, TILES, EXPERTS]
    done = [0]

    def link(ins):
        done[0] += 1
        ins.then_inc(s.linked, 1)
        dve.wait_ge(s.linked, done[0])

    rank = m.rank[:, :].unsqueeze(1).to_broadcast(all_)
    over = lambda v: v.unsqueeze(2).to_broadcast(all_)
    for k, (src, one) in enumerate(((logit, m.one1), (m.t3, m.one2))):
        best = m.best[:, k, :]
        link(dve.tensor_reduce(best, src, AX.X, ALU.max))
        link(dve.tensor_tensor(m.t1[:, :, :], src if k == 0 else m.t3[:, :, :], over(best), ALU.is_equal))
        link(dve.tensor_tensor(m.t1[:, :, :], m.t1[:, :, :], rank, ALU.mult))
        link(dve.tensor_reduce(m.t2[:, :], m.t1[:, :, :], AX.X, ALU.max))
        link(dve.tensor_tensor(one[:, :, :], rank, over(m.t2[:, :]), ALU.is_equal))
        if k == 0:
            link(dve.scalar_tensor_tensor(out=m.t3[:, :, :], in0=one[:, :, :], scalar=-3e38, in1=logit,
                                          op0=ALU.mult, op1=ALU.add))
    dve.tensor_tensor(m.choice[:, :, :], m.one1[:, :, :], m.one2[:, :, :], ALU.add).then_inc(s.chosen, 1)
    dve.tensor_tensor(m.gate_exp[:, :, :], logit, over(m.best[:, 0, :]), ALU.subtract).then_inc(s.route, 1)
    dve.wait_ge(s.placed, 1)
    link(dve.tensor_reduce(m.count[:, 0, :], m.mx[:, 0, 0:TILES * EXPERTS].rearrange("p (n e) -> p e n", e=EXPERTS),
                           AX.X, ALU.add))
    by_tile = [P, EXPERTS, TILES]
    link(dve.tensor_tensor(m.t1b[:, :, :], m.tile_start[:, :].unsqueeze(1).to_broadcast(by_tile),
                           m.count[:, 0, :].unsqueeze(2).to_broadcast(by_tile), ALU.is_lt))
    link(dve.tensor_reduce(m.count[:, 1, :], m.t1b[:, :, :], AX.X, ALU.add))
    link(dve.tensor_tensor(m.t8[:, :, :], m.earlier[:, :, :],
                           m.count[:, 1, :].unsqueeze(1).to_broadcast([P, EXPERTS, EXPERTS]), ALU.mult))
    link(dve.tensor_reduce(m.count[:, 2, :], m.t8[:, :, :], AX.X, ALU.add))
    link(dve.scalar_tensor_tensor(out=m.t3[:, :, :], in0=m.count[:, 2:3, :].to_broadcast(all_), scalar=float(P),
                                  in1=m.pj[:, 0:TILES * EXPERTS].rearrange("p (n e) -> p n e", e=EXPERTS),
                                  op0=ALU.mult, op1=ALU.add))
    for k, one in enumerate((m.one1, m.one2)):
        link(dve.tensor_tensor(m.t1[:, :, :], m.t3[:, :, :], one[:, :, :], ALU.mult))
        link(dve.tensor_reduce(m.slot_f[:, k, :], m.t1[:, :, :], AX.X, ALU.add))
    dve.tensor_copy(m.slot[:, :, :], m.slot_f[:, :, :]).then_inc(s.route, 1)
    link(dve.tensor_tensor(m.count[:, 3, :], m.count[:, 1, :], m.count[:, 2, :], ALU.add))
    by_block = [P, BLOCKS, EXPERTS - 1]
    link(dve.tensor_tensor(m.t_blocks[:, :, :], m.block_no[:, :].unsqueeze(2).to_broadcast(by_block),
                           m.count[:, 3:4, 0:EXPERTS - 1].to_broadcast(by_block), ALU.is_ge))
    link(dve.tensor_reduce(m.expert_f[:, :], m.t_blocks[:, :, :], AX.X, ALU.add))
    dve.tensor_copy(m.expert[:, :], m.expert_f[:, :]).then_inc(s.expert, 1)
    dve.wait_ge(s.exped, 1)
    link(dve.tensor_reduce(m.t2[:, :], m.gate_exp[:, :, :], AX.X, ALU.add))
    link(dve.reciprocal(m.t2[:, :], m.t2[:, :]))
    link(dve.tensor_tensor(m.gate_exp[:, :, :], m.gate_exp[:, :, :], over(m.t2[:, :]), ALU.mult))
    for k, one in enumerate((m.one1, m.one2)):
        link(dve.tensor_tensor(m.t1[:, :, :], m.gate_exp[:, :, :], one[:, :, :], ALU.mult))
        link(dve.tensor_reduce(m.gate[:, k, :], m.t1[:, :, :], AX.X, ALU.add))
    link(dve.tensor_tensor(m.t2[:, :], m.gate[:, 0, :], m.gate[:, 1, :], ALU.add))
    link(dve.tensor_scalar(m.t2[:, :], m.t2[:, :], GATE_FLOOR, None, ALU.max))
    link(dve.reciprocal(m.t2[:, :], m.t2[:, :]))
    dve.tensor_tensor(m.gate[:, :, :], m.gate[:, :, :], m.t2[:, :].unsqueeze(1).to_broadcast([P, TOP, TILES]),
                      ALU.mult).then_inc(s.gated, 1)


def route_sp(sp, m, s):
    with sp.Fori(0, B) as b:
        wait(sp, s.ln_low, b + 1)
        sp.dma_start(m.rows[:, bass.ds(b * (NT * 2 * D), NT * 2 * D)],
                     m.xn16[:, :, :, :].rearrange("p t x d -> p (t x d)")).then_inc(s.row_kept, 16)


def scatter_pool(pool, m, s, g):
    pool.wait_ge(s.route, 2)
    pool.wait_ge(g.zeroed, 16)
    pool.wait_ge(s.row_kept, 16 * B)
    for n in range(TILES):
        for k in range(TOP):
            pool.indirect_dma_start(out=m.slots_in[:, :],
                                    out_offset=bass.IndirectOffsetOnAxis(ap=m.slot[:, k, n:n + 1], axis=0),
                                    in_=m.rows[:, n * 2 * D:(n + 1) * 2 * D], in_offset=None)\
                .then_inc(s.scattered, 16)


def blocks_sp(sp, m, s):
    sp.wait_ge(s.scattered, 16 * TILES * TOP)
    for j in range(LOADS):
        load_block(sp, m, s, j, j)
    with sp.Fori(0, BLOCKS // LOADS - 1) as i:
        for j in range(LOADS):
            store_block(sp, m, s, i * LOADS + j, j)
            load_block(sp, m, s, i * LOADS + (LOADS + j), j)
    for j in range(LOADS):
        store_block(sp, m, s, BLOCKS - LOADS + j, j)


def load_block(sp, m, s, block, j):
    wait(sp, s.in_turned, block - LOADS + 1)
    sp.dma_start(m.xb[:, j, :], m.slots_in[bass.ds(block * P, P), :]).then_inc(s.loaded[j], 16)


def store_block(sp, m, s, block, j):
    wait(sp, s.out, block + 1)
    sp.dma_start(m.slots_out[bass.ds(block * P, P), :], m.ob[:, j % 2, :]).then_inc(s.stored[j % 2], 16)


def block_turn(pe, m, s, block, j, rounds):
    wait(pe, s.loaded[j], rounds * 16 + (16 + s.turn * (16 * BLOCKS // LOADS)))
    wait(pe, s.in_kept, block)
    for part in range(2):
        last = pe.transpose(m.tr16[:, part * P:(part + 1) * P], m.xb[:, j, part * P:(part + 1) * P], m.ident16[:, :])
    last.then_inc(s.in_turned, 1)


def block_up(pe, m, s, block, j, e):
    wait(pe, s.in_kept, block + 1)
    wait(pe, s.gelu, block - 1)
    x = m.xbt[:, j % 2, :, :]
    for c in range(CHUNKS):
        out = m.st[:, j % 2, c * P:(c + 1) * P]
        w = [m.w1[:, part, bass.ds(e * HIDDEN + c * P, P)] for part in range(2)]
        pe.matmul(out, w[0], x[:, 0, :], start=True, stop=False)
        pe.matmul(out, w[0], x[:, 1, :], start=False, stop=False)
        last = pe.matmul(out, w[1], x[:, 0, :], start=False, stop=True)
    last.then_inc(s.up, 1)


def block_down(pe, m, s, block, j, e):
    wait(pe, s.low, block + 1)
    out = m.pvb[:, j % 2, 0:D]
    for c in range(CHUNKS):
        high, low = (x[:, j % 2, c * P:(c + 1) * P] for x in (m.ph, m.pl))
        w = [m.w2[:, part, bass.ds(e * HIDDEN + c * D, D)] for part in range(2)]
        pe.matmul(out, high, w[0], start=(c == 0), stop=False)
        pe.matmul(out, high, w[1], start=False, stop=False)
        last = pe.matmul(out, low, w[0], start=False, stop=(c == CHUNKS - 1))
    last.then_inc(s.down, 1)


def expert_of(eng, m, block):
    return eng.value_load(m.expert[0:1, bass.ds(block, 1)], min_val=0, max_val=EXPERTS - 1)


def blocks_pe(pe, m, s):
    pe.wait_ge(s.expert, 1)
    block_turn(pe, m, s, 0, 0, 0)
    e = expert_of(pe, m, 0)
    block_up(pe, m, s, 0, 0, e)

    def pair(rounds, j, last=False):
        block = rounds * LOADS + j
        if not last:
            block_turn(pe, m, s, block + 1, (j + 1) % LOADS, rounds + (j + 1) // LOADS)
            block_up(pe, m, s, block + 1, (j + 1) % LOADS, expert_of(pe, m, block + 1))
        block_down(pe, m, s, block, j, expert_of(pe, m, block))

    for j in range(LOADS):
        pair(0, j)
    with pe.Fori(1, BLOCKS // LOADS - 1) as i:
        for j in range(LOADS):
            pair(i, j)
    for j in range(LOADS):
        pair(BLOCKS // LOADS - 1, j, last=(j == LOADS - 1))


def blocks_act(act, m, s):
    act.wait_ge(s.expert, 1)
    with act.Fori(0, BLOCKS // LOADS) as i:
        for j in range(LOADS):
            block = i * LOADS + j
            e = expert_of(act, m, block)
            wait(act, s.up, block + 1)
            for c in range(CHUNKS):
                part = slice(c * P, (c + 1) * P)
                last = act.activation(m.pf[:, j, part], m.st[:, j % 2, part], ACT.Gelu,
                                      bias=m.b1[:, bass.ds(e * CHUNKS + c, 1)], scale=1 / WSCALE)
            last.then_inc(s.gelu, 1)


def blocks_dve(dve, m, s):
    dve.wait_ge(s.expert, 1)

    def keep_input(block, j):
        wait(dve, s.in_turned, block + 1)
        dve.tensor_copy(m.xbt[:, j % 2, :, :], m.tr16[:, 0:2 * P].rearrange("p (x q) -> p x q", x=2))\
            .then_inc(s.in_kept, 1)

    def split(block, j):
        wait(dve, s.gelu, block + 1)
        dve.tensor_copy(m.ph[:, j % 2, :], m.pf[:, j, :]).then_inc(s.high, 1)
        wait(dve, s.high, block + 1)
        dve.tensor_tensor(m.pl[:, j % 2, :], m.pf[:, j, :], m.ph[:, j % 2, :], ALU.subtract).then_inc(s.low, 1)

    def keep_output(rounds, j):
        block = rounds * LOADS + j
        e = expert_of(dve, m, block)
        wait(dve, s.down, block + 1)
        wait(dve, s.stored[j % 2], rounds * (8 * LOADS) + (16 * (j // 2) + s.turn * 8 * BLOCKS))
        dve.scalar_tensor_tensor(out=m.ob[:, j % 2, :], in0=m.pvb[:, j % 2, 0:D], scalar=1 / WSCALE,
                                 in1=m.b2[:, bass.ds(e * D, D)], op0=ALU.mult, op1=ALU.add).then_inc(s.out, 1)

    def step(rounds, j, last=False):
        block = rounds * LOADS + j
        if not last:
            keep_input(block + 1, (j + 1) % LOADS)
        split(block, j)
        keep_output(rounds, j)

    keep_input(0, 0)
    for j in range(LOADS + 1):
        step(j // LOADS, j % LOADS)
    with dve.Fori(1, BLOCKS // LOADS - 1) as i:
        for j in range(1, LOADS + 1):
            step(i + j // LOADS, j % LOADS)
    for j in range(1, LOADS):
        step(BLOCKS // LOADS - 1, j, last=(j == LOADS - 1))


def gather_pool(pool, m, s):
    for stored in s.stored:
        pool.wait_ge(stored, 8 * BLOCKS * (s.turn + 1))
    pool.wait_ge(s.gated, 1)
    for n in range(TILES):
        for k in range(TOP):
            c = n * TOP + k
            if c >= GATHERS:
                pool.wait_ge(s.x_added, c - GATHERS + 1)
            pool.indirect_dma_start(out=m.back[:, c % GATHERS, :], out_offset=None, in_=m.slots_out[:, :],
                                    in_offset=bass.IndirectOffsetOnAxis(ap=m.slot[:, k, n:n + 1], axis=0))\
                .then_inc(s.gathered[c % GATHERS], 16)


def gather_dve(dve, m, s):
    for n in range(TILES):
        for k in range(TOP):
            c = n * TOP + k
            dve.wait_ge(s.gathered[c % GATHERS], 16 * (c // GATHERS + 1 + s.turn * TOP * TILES // GATHERS))
            if k:
                dve.wait_ge(s.x_added, c)
            x = m.x[:, n * D:(n + 1) * D]
            dve.scalar_tensor_tensor(out=x, in0=m.back[:, c % GATHERS, :], scalar=m.gate[:, k, n:n + 1], in1=x,
                                     op0=ALU.mult, op1=ALU.add).then_inc(s.x_added, 1)




def act_std(act, m, g, k):
    act.wait_ge(g.moments, 3 * k + 3)
    act.activation(m.std[:, :], m.var[:, :], ACT.Sqrt, scale=1 / D, bias=m.eps[:, 0:1]).then_inc(g.std_ready, 1)


def dve_rstd(dve, m, g, k, stats, count):
    bn = m.bn[:, :].rearrange("p (n v) -> p v n", v=BN)
    mean_e, sum_e, mean_o, sum_o = (bn[:, v, :] for v in (1, 2, 4, 5))
    dve.wait_ge(stats, count)
    dve.tensor_tensor(m.half[:, :], mean_e, mean_o, ALU.subtract)
    dve.tensor_tensor(m.var[:, :], sum_e, sum_o, ALU.add)
    dve.tensor_tensor(m.mean[:, :], mean_e, mean_o, ALU.add).then_inc(g.moments, 1)
    dve.wait_ge(g.moments, 3 * k + 1)
    dve.tensor_scalar(m.mean[:, :], m.mean[:, :], 0.5, None, ALU.mult)
    dve.scalar_tensor_tensor(out=m.half[:, :], in0=m.half[:, :], scalar=D / 4, in1=m.half[:, :],
                             op0=ALU.mult, op1=ALU.mult).then_inc(g.moments, 1)
    dve.wait_ge(g.moments, 3 * k + 2)
    dve.tensor_tensor(m.var[:, :], m.var[:, :], m.half[:, :], ALU.add).then_inc(g.moments, 1)
    dve.wait_ge(g.std_ready, k + 1)
    dve.reciprocal(m.rstd[:, :], m.std[:, :]).then_inc(g.rstd_ready, 1)
    dve.wait_ge(g.rstd_ready, k + 1)


class Memory:
    pass


class GlobalSignals:
    def __init__(self, new):
        self.x_loaded, self.loaded, self.zeroed, self.stored = (new(n) for n in ("x_loaded", "loaded", "zeroed", "stored"))
        self.weights_high, self.weights_low = new("weights_high"), new("weights_low")
        self.cleared, self.consts = new("cleared"), new("consts")
        self.moments, self.std_ready, self.rstd_ready = new("moments"), new("std_ready"), new("rstd_ready")


def build(nc, x, a_w, a_wo, b_w, b_wo, cos, sin, wg, bg, w1, b1, w2, b2, out, upto=4):
    ctx = ExitStack()
    with ctx:
        def sb(name, shape, dt):
            return ctx.enter_context(nc.sbuf_tensor(name, shape, dt))

        def ps(name, shape, dt):
            return ctx.enter_context(nc.psum_tensor(name, shape, dt))

        def sem(name):
            return ctx.enter_context(nc.semaphore(name))

        a, b = first_attention(), second_attention()
        m = Memory()
        m.x = sb("x", [P, B * NT * D], F32)
        m.mean = sb("mean", [P, B * NT], F32)
        m.var = sb("var", [P, B * NT], F32)
        m.std = sb("std", [P, B * NT], F32)
        m.rstd = sb("rstd", [P, B * NT], F32)
        m.eps = sb("eps", [P, 1], F32)
        m.bn = sb("bn", [P, TILES * BN], F32)
        m.half = sb("half", [P, TILES], F32)
        m.xn = sb("xn", [P, NT, D], F32)
        m.xn16 = sb("xn16", [P, NT, 2, D], F16)
        m.xt = sb("xt", [P, 2, T], F16)
        m.w = {"a": sb("wa", [P, 2, STEPS, a.columns], F16), "b": sb("wb", [P, 2, STEPS, b.columns], F16)}
        m.wo = {"a": sb("woa", [P, HEADS // 2, D], F32), "b": sb("wob", [P, HEADS // 2, D], F32)}
        m.cos = sb("cos", [P, NT, HD], F32)
        m.sin = sb("sin", [P, NT, HD], F32)
        m.ident16 = sb("ident16", [P, P], F16)
        m.ident32 = sb("ident32", [P, P], F32)
        m.mask_q = sb("mask_q", [P, P], F16)
        m.mask_k = sb("mask_k", [P, P], F16)
        m.tmq = [sb(f"tmq{i}", [P, NT, GROUP, 3 * HD], F16) for i in range(2)]
        m.tmk = [sb(f"tmk{i}", [P, NT, GROUP, 4 * HD], F16) for i in range(2)]
        turned = sb("turned", [P, 2, 2, GROUP, T], F16)
        qt, tt = turned[:, 0], turned[:, 1]
        kt = sb("kt", [P, 2, 2, GROUP, T], F16)
        m.qt, m.tt, m.kt = ([v[:, i] for i in range(2)] for v in (qt, tt, kt))
        m.vb = [sb(f"vb{i}", [P, NT, GROUP, VW + HD], F16) for i in range(2)]
        m.pf = sb("pf", [P, RING, T], F32)
        m.ph = sb("ph", [P, RING, T], F16)
        m.pl = sb("pl", [P, RING, T], F16)
        m.rope1 = sb("rope1", [P, GROUP + 1, HD], F32)
        m.rope2 = sb("rope2", [P, GROUP + 1, HD], F32)
        m.qr = sb("qr", [P, 2, GROUP + 1, HD], F32)
        m.rs = sb("rs", [P, 2, NT], F32)
        m.y = sb("y", [P, NT, GROUP, HD], F32)
        m.yt = sb("yt", [P, HEADS // 2, T], F32)
        m.pj = ps("pj", [P, 512], F32)
        m.mx = ps("mx", [P, 2, 512], F32)
        m.st = ps("st", [P, 2, 512], F32)
        pv = ps("pv", [P, 2, 512], F32)
        m.pv = pv[:, :, 0:NT * VW].rearrange("p b (t v) -> p b t v", t=NT)
        m.tr32 = ps("tr", [P, 512], F32)
        m.tr16 = m.tr32[:, :].bitcast(F16)
        m.rows = m.yt[:, :, :].rearrange("p a b -> p (a b)").bitcast(F16)
        m.w1 = sb("w1", [P, 2, EXPERTS * HIDDEN], F16)
        m.w2 = sb("w2", [P, 2, EXPERTS * HIDDEN], F16)
        m.wg = sb("wg", [P, 2, EXPERTS], F16)
        m.wg_f = sb("wg_f", [P, EXPERTS], F32)
        m.bg = sb("bg", [P, EXPERTS], F32)
        m.b1 = sb("b1", [P, EXPERTS * CHUNKS], F32)
        m.b2 = sb("b2", [P, EXPERTS * D], F32)
        m.before = sb("before", [P, P], F16)
        m.ones = sb("ones", [P, P], F16)
        m.rank = sb("rank", [P, EXPERTS], F32)
        m.earlier = sb("earlier", [P, EXPERTS, EXPERTS], F32)
        m.tile_start = sb("tile_start", [P, TILES], F32)
        m.block_no = sb("block_no", [P, BLOCKS], F32)
        m.best = sb("best", [P, TOP, TILES], F32)
        m.t2 = sb("t2", [P, TILES], F32)
        m.count = sb("count", [P, 4, EXPERTS], F32)
        m.t8 = sb("t8", [P, EXPERTS, EXPERTS], F32)
        m.slot_f = sb("slot_f", [P, TOP, TILES], F32)
        m.slot = sb("slot", [P, TOP, TILES], mybir.dt.uint32)
        m.gate = sb("gate", [P, TOP, TILES], F32)
        m.expert = sb("expert", [P, BLOCKS], mybir.dt.int32)
        m.expert_f = sb("expert_f", [P, BLOCKS], F32)
        m.xb = sb("xb", [P, LOADS, 2 * D], F16)
        m.xbt = sb("xbt", [P, 2, 2, P], F16)
        m.ob = sb("ob", [P, 2, D], F32)
        free = kt[:, :, :, :, :].rearrange("p a b c d -> p (a b c d)").bitcast(F32)
        cut = lambda k: free[:, k * 256:(k + 1) * 256].rearrange("p (n e) -> p n e", e=EXPERTS)
        m.logit = free[:, 0:256]
        m.one1, m.one2, m.t1, m.t3, m.gate_exp = (cut(k) for k in range(1, 6))
        m.t1b = free[:, 1536:1792].rearrange("p (e n) -> p e n", e=EXPERTS)
        m.t_blocks = free[:, 2048:2048 + BLOCKS * (EXPERTS - 1)].rearrange("p (j e) -> p j e", e=EXPERTS - 1)
        m.choice = free[:, 1792:1920].bitcast(F16).rearrange("p (n e) -> p n e", e=EXPERTS)
        m.back = m.y[:, :, :, :].rearrange("p t h d -> p (t h d)").rearrange("p (c d) -> p c d", d=D)
        m.pvb = pv
        stage = {"a": m.pf[:, :, :].rearrange("p a b -> p (a b)")[:, 0:STEPS * a.columns],
                 "b": turned[:, :, :, :, :].rearrange("p a b c d -> p (a b c d)").bitcast(F32)[:, 0:STEPS * b.columns],
                 "w1": m.yt[:, :, :].rearrange("p a b -> p (a b)"),
                 "w2": free[:, :], "wg": m.wg_f[:, :]}
        split = {"a": m.w["a"][:, :, :, :].rearrange("p x g c -> p x (g c)"),
                 "b": m.w["b"][:, :, :, :].rearrange("p x g c -> p x (g c)"),
                 "w1": m.w1, "w2": m.w2, "wg": m.wg}
        m.slots_in = nc.dram_tensor("slots_in", [BLOCKS * P, 2 * D], F16, kind="Internal").ap()
        m.slots_out = nc.dram_tensor("slots_out", [BLOCKS * P, D], F32, kind="Internal").ap()

        g = GlobalSignals(sem)
        attention = {"a": (a, AttentionSignals(sem, "a")), "b": (b, AttentionSignals(sem, "b"))}
        experts = [ExpertSignals(sem, f"experts{k}") for k in range(2)]
        loaded = [sem(f"loaded{k}") for k in range(LOADS)]
        stored = [sem(f"stored{k}") for k in range(2)]
        gathered = [sem(f"gathered{k}") for k in range(GATHERS)]
        for turn, s in enumerate(experts):
            s.loaded, s.stored, s.gathered, s.turn = loaded, stored, gathered, turn
        first_stats = sem("first_stats")
        weights = ("a", "b", "w1", "w2", "wg")
        loaded_weights = {name: sem(f"loaded_{name}") for name in weights}
        phases = ("a", 0, "b", 1)[:upto]
        stats = [(first_stats, 1)] + [(attention[k][1].stats, B) if k in attention else (experts[k].stats, 1)
                                      for k in phases]
        block = ctx.enter_context(nc.Block())

        @block.sync
        def _(sp):
            sp.dma_start(m.x[:, :].rearrange("p (n d) -> p n d", d=D), x.rearrange("(n p) d -> p n d", p=P))\
              .then_inc(g.x_loaded, 16)
            for name, src in zip(weights, (a_w, b_w, w1, w2, wg)):
                sp.dma_start(stage[name], src).then_inc(loaded_weights[name], 16)
            sp.dma_start(m.cos[:, :, :], cos).then_inc(g.loaded, 16)
            sp.dma_start(m.sin[:, :, :], sin).then_inc(g.loaded, 16)
            sp.dma_start(m.wo["a"][:, :, :], a_wo).then_inc(g.loaded, 16)
            sp.dma_start(m.wo["b"][:, :, :], b_wo).then_inc(g.loaded, 16)
            sp.dma_start(m.b1[:, :], b1).then_inc(g.loaded, 16)
            sp.dma_start(m.bg[:, :], bg.partition_broadcast(P)).then_inc(g.loaded, 16)
            sp.dma_start(m.b2[:, :], b2.partition_broadcast(P)).then_inc(g.loaded, 16)
            sp.wait_ge(g.cleared, 1)
            sp.dma_start(m.slots_in.rearrange("(j p) c -> p j c", p=P),
                         m.xb[:, 0:1, :].to_broadcast([P, BLOCKS, 2 * D])).then_inc(g.zeroed, 16)
            for k in phases:
                if k in (0, 1):
                    route_sp(sp, m, experts[k])
                    blocks_sp(sp, m, experts[k])
            sp.wait_ge(*stats[-1])
            sp.dma_start(out.rearrange("(n p) d -> p n d", p=P), m.x[:, :].rearrange("p (n d) -> p n d", d=D))\
              .then_inc(g.stored, 16)
            sp.wait_ge(g.stored, 16)

        @block.gpsimd
        def _(pool):
            pool.memset(m.xb[:, 0, :], 0.0)
            for t in (m.ident16, m.ident32, m.mask_q, m.mask_k):
                pool.memset(t[:, :], 0.0)
            pool.memset(m.ones[:, :], 1.0)
            pool.memset(m.before[:, :], 1.0)
            pool.memset(m.earlier[:, :, :], 1.0)
            for i in range(2):
                pool.memset(m.tmq[i][:, :, :, P:3 * HD], 0.0)
                last = pool.memset(m.tmk[i][:, :, :, 3 * HD:4 * HD], 0.0)
            last.then_inc(g.cleared, 1)
            pool.wait_ge(g.cleared, 1)
            for i in range(2):
                pool.memset(m.vb[i][:, :, :, HD:HD + 1], 1.0)
                pool.memset(m.vb[i][:, :, :, HD + 1:VW], 0.0)
                pool.memset(m.tmk[i][:, :, :, 3 * HD:3 * HD + 1], -1.0)
            for t in (m.ident16, m.ident32):
                pool.affine_select(out=t[:, :], in_=t[:, :], compare_op=ALU.not_equal, fill=1.0, base=0,
                                   pattern=[[-1, P]], channel_multiplier=1)
            pool.affine_select(out=m.mask_q[:, :], in_=m.mask_q[:, :], compare_op=ALU.is_ge, fill=MASKED, base=0,
                               pattern=[[-1, P]], channel_multiplier=1)
            pool.affine_select(out=m.mask_k[:, :], in_=m.mask_k[:, :], compare_op=ALU.is_ge, fill=MASKED, base=0,
                               pattern=[[1, P]], channel_multiplier=-1)
            pool.affine_select(out=m.before[:, :], in_=m.before[:, :], compare_op=ALU.is_gt, fill=0.0, base=0,
                               pattern=[[1, P]], channel_multiplier=-1)
            pool.affine_select(out=m.earlier[:, :, :], in_=m.earlier[:, :, :], compare_op=ALU.is_gt, fill=0.0,
                               base=0, pattern=[[1, EXPERTS], [-1, EXPERTS]], channel_multiplier=0)
            exact = dict(allow_small_or_imprecise_dtypes=True)
            pool.iota(m.rank[:, :], [[-1, EXPERTS]], base=EXPERTS, channel_multiplier=0, **exact)
            pool.iota(m.tile_start[:, :], [[P, TILES]], base=0, channel_multiplier=0, **exact)
            pool.iota(m.block_no[:, :], [[1, BLOCKS]], base=0, channel_multiplier=0, **exact).then_inc(g.consts, 1)
            for k in phases:
                if k in (0, 1):
                    scatter_pool(pool, m, experts[k], g)
                    gather_pool(pool, m, experts[k])
                else:
                    attention_pool(pool, m, *attention[k])

        @block.scalar
        def _(act):
            for name in weights:
                act.wait_ge(loaded_weights[name], 16)
                act.activation(split[name][:, 0, :], stage[name], ACT.Copy, scale=WSCALE)\
                   .then_inc(g.weights_high, 1)
            for n, k in enumerate(phases):
                act_std(act, m, g, n)
                if k in (0, 1):
                    route_act(act, m, experts[k])
                    blocks_act(act, m, experts[k])
                else:
                    attention_act(act, m, *attention[k])

        @block.vector
        def _(dve):
            dve.memset(m.eps[:, :], EPS)
            for k, name in enumerate(weights):
                dve.wait_ge(g.weights_high, k + 1)
                dve.scalar_tensor_tensor(out=split[name][:, 1, :], in0=stage[name], scalar=WSCALE,
                                         in1=split[name][:, 0, :], op0=ALU.mult, op1=ALU.subtract)\
                   .then_inc(g.weights_low, 1)
            dve.wait_ge(g.x_loaded, 16)
            stats_dve(dve, m, first_stats)
            dve.wait_ge(g.loaded, 16 * 7)
            dve.wait_ge(g.consts, 1)
            for n, k in enumerate(phases):
                dve_rstd(dve, m, g, n, *stats[n])
                if k in (0, 1):
                    s = experts[k]
                    route_dve(dve, m, s)
                    blocks_dve(dve, m, s)
                    gather_dve(dve, m, s)
                    dve.wait_ge(s.x_added, TOP * TILES)
                    stats_dve(dve, m, s.stats)
                else:
                    attention_dve(dve, m, *attention[k])

        @block.tensor
        def _(pe):
            pe.wait_ge(g.consts, 1)
            pe.wait_ge(g.weights_low, len(weights))
            pe.wait_ge(g.loaded, 16 * 7)
            for k in phases:
                if k in (0, 1):
                    route_pe(pe, m, experts[k])
                    blocks_pe(pe, m, experts[k])
                else:
                    attention_pe(pe, m, *attention[k])


def stats_dve(dve, m, stats):
    with dve.Fori(0, B - 1) as b:
        dve_stats(dve, m, b)
    dve_stats(dve, m, B - 1).then_inc(stats, 1)


def lay_out(inputs):
    f = np.float32
    A = lambda n: np.ascontiguousarray(inputs["L0_" + n])
    wq = A("attn_a_Wq").reshape(D, STEPS, GROUP, HD // 2, 2).transpose(0, 1, 2, 4, 3).reshape(D, STEPS, GROUP * HD)
    wk = A("attn_a_Wk").reshape(D, STEPS, HD // 2, 2).transpose(0, 1, 3, 2).reshape(D, STEPS, HD)
    wv = A("attn_a_Wv").reshape(D, STEPS, HD)
    a_w = np.concatenate([wq, wk, wv], axis=2).reshape(D, -1)
    b_w = A("attn_b_W_qkv").reshape(D, STEPS, GROUP, HD, 3).transpose(0, 1, 4, 2, 3).reshape(D, -1)
    wo = lambda n: A(n).reshape(HEADS // 2, P, D).transpose(1, 0, 2)
    inv = (f(1) / f(10000.0) ** (np.arange(0, HD, 2, dtype=f) / f(HD))).astype(f)
    ang = (np.arange(T, dtype=f)[:, None] * inv[None, :]).astype(f)
    c, s = np.cos(ang).astype(f) / f(WSCALE), np.sin(ang).astype(f) / f(WSCALE)
    tiles = lambda v: v.reshape(NT, P, HD).transpose(1, 0, 2)
    arrays = {"x": A("attn_a_x").reshape(B * T, D), "a_w": a_w, "a_wo": wo("attn_a_Wo"), "b_w": b_w,
            "b_wo": wo("attn_b_W_out"), "cos": tiles(np.concatenate([c, c], 1)),
            "sin": tiles(np.concatenate([-s, s], 1)),
            "wg": A("ffn_Wg"), "bg": A("ffn_bg"), "w1": A("ffn_W1").transpose(1, 0, 2).reshape(D, -1),
            "b1": A("ffn_b1").reshape(EXPERTS, CHUNKS, P).transpose(2, 0, 1).reshape(P, -1),
            "w2": A("ffn_W2").reshape(EXPERTS, CHUNKS, P, D).transpose(2, 0, 1, 3).reshape(P, -1),
            "b2": A("ffn_b2").reshape(-1)}
    return {name: np.ascontiguousarray(v) for name, v in arrays.items()}




def kernel(**inputs):
    import concourse.bacc as bacc
    from concourse.bass_utils import run_bass_kernel_spmd

    nc = bacc.Bacc("TRN2", target_bir_lowering=False, num_devices=1)
    arrays = lay_out(inputs)
    args = [nc.dram_tensor(f"in_{name}_dram", v.shape, mybir.dt.from_np(v.dtype), kind="ExternalInput").ap()
            for name, v in arrays.items()]
    args.append(nc.dram_tensor("out_0_dram", (B * T, D), F32, kind="ExternalOutput").ap())
    build(nc, *args)
    r = run_bass_kernel_spmd(nc, [{f"in_{name}_dram": v for name, v in arrays.items()}], core_ids=[0])
    return r.results[0]["out_0_dram"].reshape(B, T, D)
```

```python
from contextlib import ExitStack

import numpy as np

import concourse.bass as bass
from concourse import mybir

F32 = mybir.dt.float32
F16 = mybir.dt.float16
U32 = mybir.dt.uint32
ALU = mybir.AluOpType
ACT = mybir.ActivationFunctionType
AX = mybir.AxisListType

B, T, D = 8, 512, 128
P = 128
NT = T // P
HEADS, HD = 16, 64
GROUP = 4
STEPS = HEADS // GROUP
UNITS = GROUP * NT
AHEAD = 3
RING = 4
WSCALE = 64.0
EPS = 1e-5
MASKED = -60000.0
BN = 6
VW = HD + 2


class Step:

    def __init__(self, b, g):
        self.b, self.g = b, g

    def count(self, per_step, k):
        return self.b * (STEPS * per_step) + (self.g * per_step + k)

    def next(self):
        return Step(self.b, self.g + 1) if self.g + 1 < STEPS else Step(self.b + 1, 0)

    def previous(self):
        return Step(self.b, self.g - 1) if self.g else Step(self.b - 1, STEPS - 1)

    def is_first(self):
        return isinstance(self.b, int) and (self.b, self.g) == (0, 0)

    def is_last_batch(self):
        return isinstance(self.b, int) and self.b == B - 1


def wait(eng, sem, value):
    if isinstance(value, int) and value <= 0:
        return
    eng.wait_ge(sem, value)


class Attention:

    def __init__(self, name, causal, rotary, kv, tasks, evacuated_by, pool_tiles):
        self.name, self.causal, self.rotary, self.kv = name, causal, rotary, kv
        self.queries_keys = (GROUP + kv) * HD
        self.columns = (GROUP + 2 * kv) * HD
        self.tasks = tasks
        self.evacuated_by = evacuated_by
        self.pool_tiles = pool_tiles
        self.transposed = [x for u in range(UNITS) for x in tasks[u].split() if x in evacuated_by]

    def order(self, task):
        return self.transposed.index(task)

    def evacuations(self, engine, upto):
        return sum(self.evacuated_by[x] == engine for x in self.transposed[:self.order(upto) + 1])

    def lows(self, on_pool, unit):
        return sum((u % NT in self.pool_tiles) == on_pool for u in range(unit + 1))


def first_attention():
    tasks = ["", "V0 TQ01 V1", "TK01 V2", "YT0 V3 m00",
             "TQ23 m01 m02", "YT1 m03 m10", "WO m11 m12 TX", "m13 LX",
             "Q0 m20 m21 TT01", "m22 m23 qh0", "m30 XH Q1", "m31",
             "Q2 m32 qh1 XL", "m33 qh2 Q3", "", "TT23 qh3"]
    by = {"TK01": "dve", "TQ01": "dve", "TQ23": "act", "TT01": "act", "TT23": "dve"}
    return Attention("a", True, True, 1, tasks, by, (1, 3))


def second_attention():
    tasks = ["V0", "TQ01 V1 TK01 V2", "YT0 m00 V3", "TQ23 m01",
             "YT1 m02 m03", "TK23 m10 WO", "TX m11", "m12 TL01 m13 LX Q0",
             "m20 TT01", "m21 m22 XH Q1", "", "m23 TL23 m30 m31 XL Q2",
             "m32", "m33", "Q3", "TT23"]
    by = {"TQ01": "dve", "TK01": "dve", "TQ23": "dve", "TK23": "dve", "TL01": "act", "TL23": "act",
          "TT01": "act", "TT23": "dve"}
    return Attention("b", False, False, GROUP, tasks, by, (1, 2))


class AttentionSignals:

    def __init__(self, new, phase):
        self.q_projected = new(f"{phase}_q_projected")
        self.q_free = new(f"{phase}_q_free")
        self.v_projected = new(f"{phase}_v_projected")
        self.v_free = new(f"{phase}_v_free")
        self.rope_sum = new(f"{phase}_rope_sum")
        self.heads_high = new(f"{phase}_heads_high")
        self.heads_low = new(f"{phase}_heads_low")
        self.v_high = new(f"{phase}_v_high")
        self.transposed = new(f"{phase}_transposed")
        self.evacuated_dve = new(f"{phase}_evacuated_dve")
        self.evacuated_act = new(f"{phase}_evacuated_act")
        self.max_scored = new(f"{phase}_max_scored")
        self.max_taken = new(f"{phase}_max_taken")
        self.scored = new(f"{phase}_scored")
        self.exped = new(f"{phase}_exped")
        self.low_dve = new(f"{phase}_low_dve")
        self.low_pool = new(f"{phase}_low_pool")
        self.mixed = new(f"{phase}_mixed")
        self.recip = new(f"{phase}_recip")
        self.normed = new(f"{phase}_normed")
        self.y_turned = new(f"{phase}_y_turned")
        self.y_kept = new(f"{phase}_y_kept")
        self.out_projected = new(f"{phase}_out_projected")
        self.x_added = new(f"{phase}_x_added")
        self.stats = new(f"{phase}_stats")
        self.ln_done = new(f"{phase}_ln_done")
        self.ln_high = new(f"{phase}_ln_high")
        self.ln_low = new(f"{phase}_ln_low")
        self.x_turned = new(f"{phase}_x_turned")
        self.x_kept = new(f"{phase}_x_kept")




def pe_projection(pe, m, a, s, n, task):
    t = int(task[1])
    cols = slice(0, a.queries_keys) if task[0] == "Q" else slice(a.queries_keys, a.columns)
    w = m.w[a.name][:, :, n.g, cols]
    out = m.pj[:, 0:cols.stop - cols.start]
    tile = slice(t * P, (t + 1) * P)
    pe.matmul(out, m.xt[:, 0, tile], w[:, 0, :], start=True, stop=False)
    pe.matmul(out, m.xt[:, 1, tile], w[:, 0, :], start=False, stop=False)
    pe.matmul(out, m.xt[:, 0, tile], w[:, 1, :], start=False, stop=True)\
      .then_inc(s.q_projected if task[0] == "Q" else s.v_projected, 1)


def turn_wait(pe, a, s, n, before):
    if before is None:
        before, ref = a.transposed[-1], Step(n.b, n.g - 1)
    else:
        ref = n
    if before == "TX":
        wait(pe, s.x_kept, n.b + 2)
    elif before[:2] == "YT":
        wait(pe, s.y_kept, Step(n.b, n.g - 2).count(2, int(before[2]) + 1))
    else:
        e = a.evacuated_by[before]
        sem = s.evacuated_dve if e == "dve" else s.evacuated_act
        per = a.evacuations(e, a.transposed[-1])
        wait(pe, sem, ref.count(per, a.evacuations(e, before)))


def pe_turn(pe, m, a, s, n, task):
    tmq, tmk = m.tmq[n.g % 2], m.tmk[n.g % 2]
    if task[1] == "T":
        wait(pe, s.max_taken, n.count(HEADS, 8 if task == "TT01" else 16))
    else:
        wait(pe, s.heads_low if a.rotary else s.q_free, n.count(4, 4))
    h0 = int(task[2])
    for j in range(2):
        for t in range(NT):
            if task[1] == "Q":
                src = tmq[:, t, h0 + j, 0:P]
            elif task[1] == "T":
                src = tmq[:, t, h0 + j, HD:HD + P]
            elif a.kv == 1:
                src = tmk[:, t, 0, j * P:(j + 1) * P]
            else:
                src = tmk[:, t, h0 + j, 0:P] if task[1] == "K" else tmk[:, t, h0 + j, P:2 * P]
            last = pe.transpose(m.tr16[:, (j * NT + t) * P:(j * NT + t + 1) * P], src, m.ident16[:, :])
    last.then_inc(s.transposed, 1)


def pe_turn_x(pe, m, s, b):
    wait(pe, s.ln_low, b + 1)
    for part in range(2):
        for t in range(NT):
            last = pe.transpose(m.tr16[:, (part * NT + t) * P:(part * NT + t + 1) * P],
                                m.xn16[:, t, part, :], m.ident16[:, :])
    last.then_inc(s.x_turned, 1)


def pe_max_scores(pe, m, a, s, n, task):
    par = n.g % 2
    h, qt = int(task[1]), int(task[2])
    k = NT * h + qt
    wait(pe, s.max_taken, n.count(UNITS, k - 1))
    if qt == 0 and h % 2 == 0:
        need = [x for x in (("TQ01", "TK01") if h == 0 else ("TQ23", "TK23")) if x in a.evacuated_by]
        for e in ("dve", "act"):
            mine = [x for x in need if a.evacuated_by[x] == e]
            if mine:
                wait(pe, s.evacuated_dve if e == "dve" else s.evacuated_act,
                     n.count(a.evacuations(e, a.transposed[-1]), a.evacuations(e, max(mine, key=a.order))))
    hk = 0 if a.kv == 1 else h
    keys = (qt + 1) * P if a.causal else T
    last = pe.matmul(m.mx[:, k % 2, 0:keys], m.qt[par][:, h, qt * P:(qt + 1) * P], m.kt[par][:, 0, hk, 0:keys],
                     start=True, stop=not a.causal, skip_group_check=True)
    if a.causal:
        last = pe.matmul(m.mx[:, k % 2, keys - P:keys], m.ident16[:, :], m.mask_q[:, :], start=False, stop=True,
                         skip_group_check=True)
    last.then_inc(s.max_scored, 1)


def pe_scores(pe, m, a, s, st, u):
    par = st.g % 2
    h, kc = divmod(u, NT)
    wait(pe, s.exped, st.count(UNITS, u - 1))
    if u in (0, UNITS // 2):
        upto = "TT01" if u == 0 else "TT23"
        for e in ("dve", "act"):
            per = a.evacuations(e, a.transposed[-1])
            if per:
                wait(pe, s.evacuated_dve if e == "dve" else s.evacuated_act, st.count(per, a.evacuations(e, upto)))
    hk = 0 if a.kv == 1 else h
    q0 = kc * P if a.causal else 0
    out = m.st[:, u % 2, q0:T]
    keys = slice(kc * P, (kc + 1) * P)
    pe.matmul(out, m.kt[par][:, 0, hk, keys], m.qt[par][:, h, q0:T], start=True, stop=False, skip_group_check=True)
    last = pe.matmul(out, m.kt[par][:, 1, hk, keys], m.tt[par][:, h, q0:T], start=False, stop=not a.causal,
                     skip_group_check=True)
    if a.causal:
        last = pe.matmul(m.st[:, u % 2, q0:q0 + P], m.ident16[:, :], m.mask_k[:, :], start=False, stop=True,
                         skip_group_check=True)
    last.then_inc(s.scored, 1)


def pe_mix(pe, m, a, s, st, u):
    par = st.g % 2
    h, kc = divmod(u, NT)
    on_pool = kc in a.pool_tiles
    wait(pe, s.low_pool if on_pool else s.low_dve, st.count(a.lows(on_pool, UNITS - 1), a.lows(on_pool, u)))
    if kc == 0:
        wait(pe, s.normed, st.count(GROUP, h - 1))
    if u == 0:
        wait(pe, s.v_free, st.count(4, 4))
    hv = 0 if a.kv == 1 else h
    v = m.vb[par]
    first = kc == 0
    r = u % RING
    for qt in range(kc if a.causal else 0, NT):
        q = slice(qt * P, (qt + 1) * P)
        pe.matmul(m.pv[:, h % 2, qt, :], m.ph[:, r, q], v[:, kc, hv, 0:VW], start=first, stop=False,
                  skip_group_check=True)
        first = False
        pe.matmul(m.pv[:, h % 2, qt, 0:HD], m.ph[:, r, q], v[:, kc, hv, VW:VW + HD], start=False, stop=False,
                  skip_group_check=True)
        last = pe.matmul(m.pv[:, h % 2, qt, :], m.pl[:, r, q], v[:, kc, hv, 0:VW], start=False,
                         stop=(kc == NT - 1), skip_group_check=True)
    last.then_inc(s.mixed, 1)


def pe_turn_y(pe, m, s, before, p):
    wait(pe, s.normed, before.count(GROUP, 2 * p + 2))
    for t in range(NT):
        last = pe.transpose(m.tr32[:, t * P:(t + 1) * P],
                            m.y[:, t, 2 * p:2 * p + 2, :].rearrange("p h d -> p (h d)"), m.ident32[:, :])
    last.then_inc(s.y_turned, 1)


def pe_output(pe, m, a, s, b):
    wait(pe, s.y_kept, b * (2 * STEPS) + 2 * STEPS)
    for t in range(NT):
        for p in range(HEADS // 2):
            last = pe.matmul(m.pj[:, t * P:(t + 1) * P], m.yt[:, p, t * P:(t + 1) * P], m.wo[a.name][:, p, :],
                             start=(p == 0), stop=(p == HEADS // 2 - 1))
    last.then_inc(s.out_projected, 1)


def pe_step(pe, m, a, s, st, main=True, prep=True, queries=True):
    n, n2 = st.next(), st.next().next()
    before = None
    for u in range(UNITS):
        ahead = u + AHEAD
        if ahead < UNITS and main:
            pe_scores(pe, m, a, s, st, ahead)
        elif ahead >= UNITS and prep:
            pe_scores(pe, m, a, s, n, ahead - UNITS)
        if main:
            pe_mix(pe, m, a, s, st, u)
        for task in a.tasks[u].split():
            if task[:2] == "YT" and main and not st.is_first():
                turn_wait(pe, a, s, n, before)
                pe_turn_y(pe, m, s, st.previous(), int(task[2]))
                before = task
            elif task == "WO" and main and st.g == 0 and not st.is_first():
                wait(pe, s.v_free, n.count(4, 4))
                pe_output(pe, m, a, s, st.b - 1)
            elif task == "TX" and main and st.g == 2 and not st.is_last_batch():
                turn_wait(pe, a, s, n, before)
                pe_turn_x(pe, m, s, st.b + 1)
                before = task
            elif task[0] == "V" and prep:
                t = int(task[1])
                wait(pe, s.v_free if t else s.q_free, n.count(4, t if t else 4))
                if t == 0 and n.is_first():
                    wait(pe, s.x_kept, 1)
                pe_projection(pe, m, a, s, n, task)
            elif task[0] == "Q" and queries:
                t = int(task[1])
                if t:
                    wait(pe, s.q_free, n2.count(4, t))
                else:
                    wait(pe, s.v_free, n.count(4, 4))
                    if main and st.g == 0 and not st.is_first():
                        wait(pe, s.x_added, st.b)
                    if n2.g == 0:
                        wait(pe, s.x_kept, n2.b + 1)
                pe_projection(pe, m, a, s, n2, task)
            elif task[0] == "m" and prep:
                pe_max_scores(pe, m, a, s, n, task)
            elif task in a.evacuated_by and prep:
                turn_wait(pe, a, s, n, before)
                pe_turn(pe, m, a, s, n, task)
                before = task


def every_step(eng, step, ends):
    step(Step(-1, STEPS - 2), main=False, prep=False)
    step(Step(-1, STEPS - 1), main=False)
    step(Step(0, 0))
    with eng.Fori(0, B - 1) as b:
        for g in range(1, STEPS):
            step(Step(b, g))
        step(Step(b + 1, 0))
    for g in range(1, STEPS):
        step(Step(B - 1, g), prep=(g < STEPS - 1), queries=(g < STEPS - 2))
    ends(Step(B - 1, STEPS - 1))


def attention_pe(pe, m, a, s):
    pe_turn_x(pe, m, s, 0)

    def ends(last):
        for p in range(2):
            wait(pe, s.y_kept, last.count(2, p))
            pe_turn_y(pe, m, s, last, p)
        pe_output(pe, m, a, s, B - 1)

    every_step(pe, lambda st, **k: pe_step(pe, m, a, s, st, **k), ends)




def act_exp(act, m, a, s, st, u):
    h, kc = divmod(u, NT)
    q0 = kc * P if a.causal else 0
    r = u % RING
    wait(act, s.scored, st.count(UNITS, u + 1))
    wait(act, s.mixed, st.count(UNITS, u - RING + 1))
    act.activation(m.pf[:, r, q0:T], m.st[:, u % 2, q0:T], ACT.Exp, scale=HD ** -0.5)
    act.activation(m.ph[:, r, q0:T], m.st[:, u % 2, q0:T], ACT.Exp, scale=HD ** -0.5).then_inc(s.exped, 1)


def act_values_high(act, m, a, s, n, t):
    wait(act, s.v_projected, n.count(4, t + 1))
    act.activation(m.vb[n.g % 2][:, t, 0:a.kv, 0:HD], m.pj[:, 0:a.kv * HD].rearrange("p (h d) -> p h d", d=HD),
                   ACT.Copy, scale=1 / WSCALE).then_inc(s.v_high, 1)


def act_heads_high(act, m, a, s, n, t):
    tmq, tmk = m.tmq[n.g % 2], m.tmk[n.g % 2]
    if a.rotary:
        wait(act, s.rope_sum, n.count(4, t + 1))
        q, k, scale = m.qr[:, t % 2, 0:GROUP, :], m.qr[:, t % 2, GROUP:GROUP + 1, :], 1.0
    else:
        wait(act, s.q_projected, n.count(4, t + 1))
        heads = m.pj[:, :].rearrange("p (h d) -> p h d", d=HD)
        q, k, scale = heads[:, 0:GROUP, :], heads[:, GROUP:2 * GROUP, :], 1 / WSCALE
    act.activation(tmq[:, t, :, HD:P], q, ACT.Copy, scale=scale)
    act.activation(tmk[:, t, 0:a.kv, 0:P].rearrange("p h (x d) -> p h x d", x=2),
                   k.unsqueeze(2).to_broadcast([P, a.kv, 2, HD]), ACT.Copy, scale=scale).then_inc(s.heads_high, 1)


def act_ln_high(act, m, s, b, row_kept=None):
    wait(act, s.ln_done, b + 1)
    if row_kept is not None:
        wait(act, row_kept, b * (16 * 2))
    wait(act, s.x_turned, b)
    act.activation(m.xn16[:, :, 0, :], m.xn[:, :, :], ACT.Copy).then_inc(s.ln_high, 1)


def act_keep_y(act, m, s, before, p):
    wait(act, s.y_turned, before.count(2, p + 1))
    act.activation(m.yt[:, 2 * before.g + p, :], m.tr32[:, :], ACT.Copy).then_inc(s.y_kept, 1)


def turned_into(m, a, n, task):
    par, h0 = n.g % 2, int(task[2])
    if task[1] == "Q":
        return m.qt[par][:, h0:h0 + 2, :]
    if task[1] == "T":
        return m.tt[par][:, h0:h0 + 2, :]
    if a.kv == 1:
        return m.kt[par][:, 0:2, 0, :]
    return m.kt[par][:, "KL".index(task[1]), h0:h0 + 2, :]


def act_step(act, m, a, s, st, main=True, prep=True, queries=True):
    n, n2 = st.next(), st.next().next()
    for u in range(UNITS):
        ahead = u + AHEAD
        if ahead < UNITS and main:
            act_exp(act, m, a, s, st, ahead)
        elif ahead >= UNITS and prep:
            act_exp(act, m, a, s, n, ahead - UNITS)
        for task in a.tasks[u].split():
            if task[:2] == "YT" and main and not st.is_first():
                act_keep_y(act, m, s, st.previous(), int(task[2]))
            elif task == "XH" and main and st.g == 1 and not st.is_last_batch():
                act_ln_high(act, m, s, st.b + 1)
            elif task[0] == "V" and prep:
                act_values_high(act, m, a, s, n, int(task[1]))
            elif task[:2] == ("qh" if a.rotary else "Q" + task[-1]) and queries:
                act_heads_high(act, m, a, s, n2, int(task[-1]))
            elif task in a.evacuated_by and prep and a.evacuated_by[task] == "act":
                wait(act, s.transposed, n.count(len(a.transposed), a.order(task) + 1))
                act.activation(turned_into(m, a, n, task), m.tr16[:, :].rearrange("p (h q) -> p h q", h=2),
                               ACT.Copy).then_inc(s.evacuated_act, 1)
    if main and st.g == 0:
        wait(act, s.out_projected, st.b)


def attention_act(act, m, a, s):
    act_ln_high(act, m, s, 0)

    def ends(last):
        for p in range(2):
            act_keep_y(act, m, s, last, p)

    every_step(act, lambda st, **k: act_step(act, m, a, s, st, **k), ends)




def dve_ln(dve, m, s, b):
    wait(dve, s.ln_low, b)
    for t in range(NT):
        last = dve.tensor_scalar(m.xn[:, t, :], m.x[:, bass.ds(b * (NT * D) + t * D, D)],
                                 m.mean[:, bass.ds(b * NT + t, 1)], m.rstd[:, bass.ds(b * NT + t, 1)],
                                 ALU.subtract, ALU.mult)
    last.then_inc(s.ln_done, 1)


def dve_ln_low(dve, m, s, b):
    wait(dve, s.ln_high, b + 1)
    dve.tensor_tensor(m.xn16[:, :, 1, :], m.xn[:, :, :], m.xn16[:, :, 0, :], ALU.subtract).then_inc(s.ln_low, 1)


def dve_keep_x(dve, m, s, b):
    wait(dve, s.x_turned, b + 1)
    dve.tensor_copy(m.xt[:, :, :], m.tr16[:, :].rearrange("p (x q) -> p x q", x=2)).then_inc(s.x_kept, 1)


def dve_stats(dve, m, b):
    for t in range(NT):
        last = dve.bn_stats(m.bn[:, bass.ds(b * (NT * BN) + t * BN, BN)], m.x[:, bass.ds(b * (NT * D) + t * D, D)])
    return last


def dve_add_output(dve, m, s, b):
    wait(dve, s.out_projected, b + 1)
    x = m.x[:, bass.ds(b * (NT * D), NT * D)]
    dve.tensor_tensor(x, m.pj[:, :], x, ALU.add).then_inc(s.x_added, 1)


def dve_low(dve, m, a, s, st, u):
    kc = u % NT
    q0 = kc * P if a.causal else 0
    r = u % RING
    wait(dve, s.exped, st.count(UNITS, u + 1))
    dve.tensor_tensor(m.pl[:, r, q0:T], m.pf[:, r, q0:T], m.ph[:, r, q0:T], ALU.subtract)\
        .then_inc(s.low_pool if kc in a.pool_tiles else s.low_dve, 1)


def dve_norm(dve, m, s, st, h):
    wait(dve, s.mixed, st.count(UNITS, NT * (h + 1)))
    if h % 2 == 0:
        wait(dve, s.y_turned, st.count(2, h // 2 - 1))
    dve.reciprocal(m.rs[:, h % 2, :], m.pv[:, h % 2, :, HD]).then_inc(s.recip, 1)
    wait(dve, s.recip, st.count(GROUP, h + 1))
    dve.tensor_tensor(m.y[:, :, h, :], m.pv[:, h % 2, :, 0:HD],
                      m.rs[:, h % 2, :].unsqueeze(2).to_broadcast([P, NT, HD]), ALU.mult).then_inc(s.normed, 1)


def dve_rope(dve, m, s, n, t):
    heads = GROUP + 1
    wait(dve, s.q_projected, n.count(4, t + 1))
    wait(dve, s.rope_sum, n.count(4, t))
    qk = m.pj[:, 0:heads * HD]
    dve.tensor_tensor(m.rope1[:, :, :], qk.rearrange("p (h d) -> p h d", d=HD),
                      m.cos[:, t, :].unsqueeze(1).to_broadcast([P, heads, HD]), ALU.mult)
    halves = qk.rearrange("p (h x d) -> p h x d", x=2, d=HD // 2)[:, :, ::-1, :]
    dve.tensor_tensor(m.rope2[:, :, :].rearrange("p h (x d) -> p h x d", x=2), halves,
                      m.sin[:, t, :].rearrange("p (x d) -> p x d", x=2).unsqueeze(1)
                      .to_broadcast([P, heads, 2, HD // 2]), ALU.mult).then_inc(s.q_free, 1)


def dve_heads_low(dve, m, s, n, t):
    tmq, tmk = m.tmq[n.g % 2], m.tmk[n.g % 2]
    heads = m.pj[:, :].rearrange("p (h d) -> p h d", d=HD)
    wait(dve, s.heads_high, n.count(4, t + 1))
    dve.scalar_tensor_tensor(out=tmq[:, t, :, 0:HD], in0=heads[:, 0:GROUP, :], scalar=1 / WSCALE,
                             in1=tmq[:, t, :, HD:P], op0=ALU.mult, op1=ALU.subtract)
    dve.scalar_tensor_tensor(out=tmk[:, t, :, P:P + HD], in0=heads[:, GROUP:2 * GROUP, :], scalar=1 / WSCALE,
                             in1=tmk[:, t, :, 0:HD], op0=ALU.mult, op1=ALU.subtract).then_inc(s.q_free, 1)


def dve_values_low(dve, m, a, s, n, t):
    v = m.vb[n.g % 2]
    wait(dve, s.v_high, n.count(4, t + 1))
    dve.scalar_tensor_tensor(out=v[:, t, 0:a.kv, VW:VW + HD],
                             in0=m.pj[:, 0:a.kv * HD].rearrange("p (h d) -> p h d", d=HD),
                             scalar=1 / WSCALE, in1=v[:, t, 0:a.kv, 0:HD],
                             op0=ALU.mult, op1=ALU.subtract).then_inc(s.v_free, 1)


def dve_max(dve, m, a, s, n, task):
    h, qt = int(task[1]), int(task[2])
    k = NT * h + qt
    wait(dve, s.max_scored, n.count(UNITS, k + 1))
    dve.tensor_reduce(m.tmq[n.g % 2][:, qt, h, P:P + 1], m.mx[:, k % 2, 0:(qt + 1) * P if a.causal else T],
                      AX.X, ALU.max).then_inc(s.max_taken, 1)


def dve_step(dve, m, a, s, st, main=True, prep=True, queries=True):
    n, n2 = st.next(), st.next().next()
    for u in range(UNITS):
        if main and u % NT == 0 and not (u == 0 and st.is_first()):
            dve_norm(dve, m, s, st if u else st.previous(), (u // NT - 1) % GROUP)
        for task in a.tasks[u].split():
            if task == "WO" and main and st.g == 0 and not st.is_first():
                dve_add_output(dve, m, s, st.b - 1)
            elif task == "LX" and main and st.g == 1 and not st.is_last_batch():
                dve_ln(dve, m, s, st.b + 1)
            elif task == "XL" and main and st.g == 1 and not st.is_last_batch():
                dve_ln_low(dve, m, s, st.b + 1)
            elif task == "TX" and main and st.g == 2 and not st.is_last_batch():
                dve_keep_x(dve, m, s, st.b + 1)
            elif task[0] == "V" and prep:
                dve_values_low(dve, m, a, s, n, int(task[1]))
            elif task[0] == "Q" and queries:
                if a.rotary:
                    dve_rope(dve, m, s, n2, int(task[1]))
                else:
                    dve_heads_low(dve, m, s, n2, int(task[1]))
            elif task[0] == "m" and prep:
                if task == "m33" and main and st.g == 0 and not st.is_first():
                    wait(dve, s.x_added, st.b)
                dve_max(dve, m, a, s, n, task)
                if task == "m33" and main and st.g == 0 and not st.is_first():
                    dve_stats(dve, m, st.b - 1).then_inc(s.stats, 1)
            elif task in a.evacuated_by and prep and a.evacuated_by[task] == "dve":
                wait(dve, s.transposed, n.count(len(a.transposed), a.order(task) + 1))
                dve.tensor_copy(turned_into(m, a, n, task), m.tr16[:, :].rearrange("p (h q) -> p h q", h=2))\
                   .then_inc(s.evacuated_dve, 1)
        ahead = u + AHEAD
        if ahead % NT not in a.pool_tiles:
            if ahead < UNITS and main:
                dve_low(dve, m, a, s, st, ahead)
            elif ahead >= UNITS and prep:
                dve_low(dve, m, a, s, n, ahead - UNITS)


def attention_dve(dve, m, a, s):
    dve_ln(dve, m, s, 0)
    dve_ln_low(dve, m, s, 0)
    dve_keep_x(dve, m, s, 0)

    def ends(last):
        dve_norm(dve, m, s, last, GROUP - 1)
        dve_add_output(dve, m, s, B - 1)
        dve.wait_ge(s.x_added, B)
        dve_stats(dve, m, B - 1).then_inc(s.stats, 1)

    every_step(dve, lambda st, **k: dve_step(dve, m, a, s, st, **k), ends)




def pool_step(pool, m, a, s, st, main=True, prep=True, queries=True):
    n, n2 = st.next(), st.next().next()
    for u in range(UNITS):
        ahead = u + AHEAD
        if ahead % NT in a.pool_tiles:
            if ahead < UNITS and main:
                dve_low(pool, m, a, s, st, ahead)
            elif ahead >= UNITS and prep:
                dve_low(pool, m, a, s, n, ahead - UNITS)
        for task in a.tasks[u].split():
            if not (a.rotary and queries and task[0] in "Qq"):
                continue
            t = int(task[-1])
            tmq, tmk = m.tmq[n2.g % 2], m.tmk[n2.g % 2]
            if task[0] == "Q":
                wait(pool, s.q_free, n2.count(4, t + 1))
                wait(pool, s.heads_low, n2.count(4, t - 1))
                pool.tensor_tensor(m.qr[:, t % 2, :, :], m.rope1[:, :, :], m.rope2[:, :, :], ALU.add)\
                    .then_inc(s.rope_sum, 1)
            else:
                wait(pool, s.heads_high, n2.count(4, t + 1))
                pool.tensor_tensor(tmq[:, t, :, 0:HD], m.qr[:, t % 2, 0:GROUP, :], tmq[:, t, :, HD:P],
                                   ALU.subtract)
                pool.tensor_tensor(tmk[:, t, 0, P:P + HD], m.qr[:, t % 2, GROUP, :], tmk[:, t, 0, 0:HD],
                                   ALU.subtract).then_inc(s.heads_low, 1)


def attention_pool(pool, m, a, s):
    every_step(pool, lambda st, **k: pool_step(pool, m, a, s, st, **k), lambda last: None)



EXPERTS, HIDDEN, TOP = 8, 512, 2
TILES = B * NT
TOKENS = B * T
CHUNKS = HIDDEN // P
WIDE = 2
BLOCK = WIDE * P
REGION = TOKENS
UNROLL = 4
BLOCKS = -(-(TOKENS * TOP + EXPERTS * (BLOCK - 1)) // BLOCK // UNROLL) * UNROLL
SLOTS = EXPERTS * REGION + (BLOCKS - (TOKENS * TOP) // BLOCK) * BLOCK
ROW = 2 * D + 2
NOWHERE = 4 * TOKENS
GATE_FLOOR = 1e-12
LINKS = 26
RETURNS = 4


class ExpertSignals:

    def __init__(self, new, phase):
        self.ln_done = new(f"{phase}_ln_done")
        self.ln_high = new(f"{phase}_ln_high")
        self.ln_low = new(f"{phase}_ln_low")
        self.x_turned = new(f"{phase}_x_turned")
        self.x_kept = new(f"{phase}_x_kept")
        self.row_kept = new(f"{phase}_row_kept")
        self.logits = new(f"{phase}_logits")
        self.logit_kept = new(f"{phase}_logit_kept")
        self.chosen = new(f"{phase}_chosen")
        self.placed = new(f"{phase}_placed")
        self.gate_logit = new(f"{phase}_gate_logit")
        self.exped = new(f"{phase}_exped")
        self.slots = new(f"{phase}_slots")
        self.gated = new(f"{phase}_gated")
        self.scattered = [new(f"{phase}_scattered{k}") for k in range(2)]
        self.in_turned = new(f"{phase}_in_turned")
        self.in_kept = new(f"{phase}_in_kept")
        self.up = new(f"{phase}_up")
        self.gelu = new(f"{phase}_gelu")
        self.high = new(f"{phase}_high")
        self.low = new(f"{phase}_low")
        self.down = new(f"{phase}_down")
        self.half = new(f"{phase}_half")
        self.out = new(f"{phase}_out")
        self.linked = new(f"{phase}_linked")
        self.x_added = new(f"{phase}_x_added")
        self.stats = new(f"{phase}_stats")
        self.expert = new(f"{phase}_expert")


def batches(eng, batch):
    for r in range(2):
        batch(r, 0, r)
    with eng.Fori(1, B // 2) as i:
        for r in range(2):
            batch(i * 2 + r, i, r)


def route_pe(pe, m, s):
    def batch(b, i, r):
        pe_turn_x(pe, m, s, b)
        wait(pe, s.x_kept, b + 1)
        wait(pe, s.logit_kept, b)
        for t in range(NT):
            out = m.pj[:, t * EXPERTS:(t + 1) * EXPERTS]
            tile = slice(t * P, (t + 1) * P)
            pe.matmul(out, m.xt[:, 0, tile], m.wg[:, 0, :], start=True, stop=False)
            pe.matmul(out, m.xt[:, 1, tile], m.wg[:, 0, :], start=False, stop=False)
            last = pe.matmul(out, m.xt[:, 0, tile], m.wg[:, 1, :], start=False, stop=True)
        last.then_inc(s.logits, 1)
        wait(pe, s.chosen, b + 1)
        place = m.mx[:, 0, 0:NT * EXPERTS]
        pe.matmul(place, m.before[:, :], m.choice[:, :, :].rearrange("p n e -> p (n e)"), start=True, stop=False,
                  skip_group_check=True)
        for n in range(NT - 1):
            rest = NT - 1 - n
            pe.matmul(place[:, (n + 1) * EXPERTS:].rearrange("p (n e) -> p n e", e=EXPERTS), m.ones[:, :],
                      m.choice[:, n:n + 1, :].to_broadcast([P, rest, EXPERTS]), start=False, stop=(rest == 1),
                      skip_group_check=True)
        for n in range(NT):
            last = pe.matmul(m.mx[:, 1, 0:EXPERTS], m.ones[:, :], m.choice[:, n, :], start=(n == 0),
                             stop=(n == NT - 1))
        last.then_inc(s.placed, 1)

    batches(pe, batch)


def route_act(act, m, s):
    def batch(b, i, r):
        act_ln_high(act, m, s, b, row_kept=s.row_kept)
        wait(act, s.gate_logit, b + 1)
        act.activation(m.gate_exp[:, :, :], m.gate_exp[:, :, :], ACT.Exp).then_inc(s.exped, 1)

    batches(act, batch)


def route_dve(dve, m, s):
    all_ = [P, NT, EXPERTS]
    logit = m.logit[:, :, :]
    rank = m.rank[:, :].unsqueeze(1).to_broadcast(all_)
    over = lambda v: v.unsqueeze(2).to_broadcast(all_)
    dve.tensor_copy(m.free[:, :], m.region[:, :])
    dve.tensor_copy(m.home[:, :, :], m.first_home[:, :, :]).then_inc(s.linked, 1)
    dve.wait_ge(s.linked, 1)

    def normed_low(b, i, r):
        wait(dve, s.scattered[r], i * (NT * TOP * 16))
        dve_ln_low(dve, m, s, b)

    def batch(b, i, r, last=False):
        done = [0]
        following = (b + 1, i + r, 1 - r)

        def link(ins):
            done[0] += 1
            ins.then_inc(s.linked, 1)
            dve.wait_ge(s.linked, b * LINKS + (1 + done[0]))

        wait(dve, s.logits, b + 1)
        dve.scalar_tensor_tensor(out=logit, in0=m.pj[:, 0:NT * EXPERTS].rearrange("p (t e) -> p t e", e=EXPERTS),
                                 scalar=1 / WSCALE, in1=m.bg[:, :].unsqueeze(1).to_broadcast(all_),
                                 op0=ALU.mult, op1=ALU.add).then_inc(s.logit_kept, 1)
        wait(dve, s.logit_kept, b + 1)
        for k, (src, one) in enumerate(((logit, m.one1), (m.t3[:, :, :], m.one2))):
            link(dve.tensor_reduce(m.best[:, k, :], src, AX.X, ALU.max))
            link(dve.tensor_tensor(m.t1[:, :, :], src, over(m.best[:, k, :]), ALU.is_equal))
            link(dve.tensor_tensor(m.t1[:, :, :], m.t1[:, :, :], rank, ALU.mult))
            link(dve.tensor_reduce(m.t2[:, :], m.t1[:, :, :], AX.X, ALU.max))
            link(dve.tensor_tensor(one[:, :, :], rank, over(m.t2[:, :]), ALU.is_equal))
            if k == 0:
                link(dve.scalar_tensor_tensor(out=m.t3[:, :, :], in0=one[:, :, :], scalar=-3e38, in1=logit,
                                              op0=ALU.mult, op1=ALU.add))
        dve.tensor_tensor(m.choice[:, :, :], m.one1[:, :, :], m.one2[:, :, :], ALU.add).then_inc(s.chosen, 1)
        dve.tensor_tensor(m.gate_exp[:, :, :], logit, over(m.best[:, 0, :]), ALU.subtract)\
           .then_inc(s.gate_logit, 1)
        if not last:
            dve_ln(dve, m, s, b + 1)
        dve.tensor_copy(m.send[:, r, :, :, 2 * D:ROW].bitcast(F32).rearrange("p t k c -> p k (t c)"),
                        m.home[:, :, :]).then_inc(s.slots, 1)
        wait(dve, s.slots, b * 2 + 1)
        dve.tensor_scalar(m.home[:, :, :], m.home[:, :, :], float(T), None, ALU.add)
        wait(dve, s.placed, b + 1)
        link(dve.tensor_tensor(m.t3[:, :, :], m.free[:, :].unsqueeze(1).to_broadcast(all_),
                               m.mx[:, 0, 0:NT * EXPERTS].rearrange("p (n e) -> p n e", e=EXPERTS), ALU.add))
        dve.tensor_tensor(m.free[:, :], m.free[:, :], m.mx[:, 1, 0:EXPERTS], ALU.add)
        for k, one in enumerate((m.one1, m.one2)):
            link(dve.tensor_tensor(m.t1[:, :, :], m.t3[:, :, :], one[:, :, :], ALU.mult))
            link(dve.tensor_reduce(m.slot_f[:, k, :], m.t1[:, :, :], AX.X, ALU.add))
        dve.tensor_copy(m.slot[:, r, :, :], m.slot_f[:, :, :]).then_inc(s.slots, 1)
        if not last:
            normed_low(*following)
        wait(dve, s.exped, b + 1)
        link(dve.tensor_reduce(m.t2[:, :], m.gate_exp[:, :, :], AX.X, ALU.add))
        link(dve.reciprocal(m.t2[:, :], m.t2[:, :]))
        link(dve.tensor_tensor(m.gate_exp[:, :, :], m.gate_exp[:, :, :], over(m.t2[:, :]), ALU.mult))
        for k, one in enumerate((m.one1, m.one2)):
            link(dve.tensor_tensor(m.t1[:, :, :], m.gate_exp[:, :, :], one[:, :, :], ALU.mult))
            link(dve.tensor_reduce(m.two[:, k, :], m.t1[:, :, :], AX.X, ALU.add))
        link(dve.tensor_tensor(m.t2[:, :], m.two[:, 0, :], m.two[:, 1, :], ALU.add))
        link(dve.tensor_scalar(m.t2[:, :], m.t2[:, :], GATE_FLOOR, None, ALU.max))
        link(dve.reciprocal(m.t2[:, :], m.t2[:, :]))
        dve.tensor_tensor(m.gate[:, :, bass.ds(b * NT, NT)], m.two[:, :, :],
                          m.t2[:, :].unsqueeze(1).to_broadcast([P, TOP, NT]), ALU.mult).then_inc(s.gated, 1)
        assert done[0] == LINKS
        if not last:
            dve_keep_x(dve, m, s, b + 1)

    dve_ln(dve, m, s, 0)
    normed_low(0, 0, 0)
    dve_keep_x(dve, m, s, 0)
    for r in range(2):
        batch(r, 0, r)
    with dve.Fori(1, B // 2 - 1) as i:
        for r in range(2):
            batch(i * 2 + r, i, r)
    for r in range(2):
        batch(B - 2 + r, B // 2 - 1, r, last=(r == 1))
    dve_blocks_table(dve, m, s)


def dve_blocks_table(dve, m, s):
    done = [0]

    def link(ins):
        done[0] += 1
        ins.then_inc(s.linked, 1)
        dve.wait_ge(s.linked, B * LINKS + 1 + done[0])

    dve.wait_ge(s.gated, B)
    tokens, blocks, upto, skipped = (m.count[:, k, :] for k in range(4))
    link(dve.tensor_tensor(tokens, m.free[:, :], m.region[:, :], ALU.subtract))
    by_block = [P, EXPERTS, REGION // BLOCK]
    link(dve.tensor_tensor(m.t_full[:, :, :], m.block_start[:, :].unsqueeze(1).to_broadcast(by_block),
                           tokens.unsqueeze(2).to_broadcast(by_block), ALU.is_lt))
    link(dve.tensor_reduce(blocks, m.t_full[:, :, :], AX.X, ALU.add))
    link(dve.tensor_tensor(m.t8[:, :, :], m.upto[:, :, :],
                           blocks.unsqueeze(1).to_broadcast([P, EXPERTS, EXPERTS]), ALU.mult))
    link(dve.tensor_reduce(upto, m.t8[:, :, :], AX.X, ALU.add))
    link(dve.tensor_scalar(skipped, blocks, -float(BLOCK), float(REGION), ALU.mult, ALU.add))
    of_last = [P, BLOCKS, EXPERTS - 1]
    link(dve.tensor_tensor(m.t_blocks[:, :, :], m.block_no[:, :].unsqueeze(2).to_broadcast(of_last),
                           upto[:, 0:EXPERTS - 1].unsqueeze(1).to_broadcast(of_last), ALU.is_ge))
    link(dve.tensor_reduce(m.expert_f[:, 0, :], m.t_blocks[:, :, :], AX.X, ALU.add))
    link(dve.tensor_tensor(m.t_blocks[:, :, :], m.t_blocks[:, :, :],
                           skipped[:, 0:EXPERTS - 1].unsqueeze(1).to_broadcast(of_last), ALU.mult))
    link(dve.tensor_reduce(m.expert_f[:, 1, :], m.t_blocks[:, :, :], AX.X, ALU.add))
    link(dve.scalar_tensor_tensor(out=m.expert_f[:, 1, :], in0=m.block_no[:, :], scalar=float(BLOCK),
                                  in1=m.expert_f[:, 1, :], op0=ALU.mult, op1=ALU.add))
    dve.tensor_copy(m.expert[:, :, :], m.expert_f[:, :, :]).then_inc(s.expert, 1)


def route_sp(sp, m, s):
    def batch(b, i, r):
        wait(sp, s.ln_low, b + 1)
        for k in range(TOP):
            sp.dma_start(m.send[:, r, :, k, 0:2 * D], m.xn16[:, :, :, :].rearrange("p t x d -> p t (x d)"))\
              .then_inc(s.row_kept, 16)

    batches(sp, batch)


def scatter_pool(pool, m, s, g):
    pool.wait_ge(g.zeroed, 16 * 2)

    def batch(b, i, r):
        wait(pool, s.slots, b * 2 + 2)
        wait(pool, s.row_kept, b * (16 * TOP) + 16 * TOP)
        pool.sem_inc(g.carried, 1)
        for t in range(NT):
            for k in range(TOP):
                pool.indirect_dma_start(out=s.slots_in[:, :],
                                        out_offset=bass.IndirectOffsetOnAxis(ap=m.slot[:, r, k, t:t + 1], axis=0),
                                        in_=m.send[:, r, t, k, :], in_offset=None).then_inc(s.scattered[r], 16)

    batches(pool, batch)


def blocks_sp(sp, m, s):
    for scattered in s.scattered:
        sp.wait_ge(scattered, 16 * TILES * TOP // 2)
    sp.wait_ge(s.expert, 1)
    for j in range(UNROLL):
        load_block(sp, m, s, j, j)
    with sp.Fori(1, BLOCKS // UNROLL) as i:
        for j in range(UNROLL):
            load_block(sp, m, s, i * UNROLL + j, j)


def load_block(sp, m, s, block, j):
    slot = sp.value_load(m.expert[0:1, 1, bass.ds(block, 1)], min_val=0, max_val=SLOTS - BLOCK)
    wait(sp, s.in_kept, block - UNROLL + 1)
    sp.dma_start(m.xb[:, j, :, :], s.slots_in[bass.ds(slot, BLOCK), :].rearrange("(i p) c -> p i c", p=P))\
      .then_inc(s.loaded[j], 16)


def block_turn(pe, m, s, block, j, rounds):
    wait(pe, s.loaded[j], rounds * 16 + (16 + s.turn * (16 * BLOCKS // UNROLL)))
    wait(pe, s.in_kept, block)
    for part in range(2):
        for i in range(WIDE):
            last = pe.transpose(m.tr16[:, (part * WIDE + i) * P:(part * WIDE + i + 1) * P],
                                m.xb[:, j, i, part * P:(part + 1) * P], m.ident16[:, :])
    last.then_inc(s.in_turned, 1)


def block_up(pe, m, s, block, j, e):
    wait(pe, s.in_kept, block + 1)
    wait(pe, s.gelu, block * 2 - 2)
    x = m.xbt[:, j % 2, :, :]
    for c in range(CHUNKS):
        out = m.hid[j % 2][:, c, :]
        w = [m.w1[:, part, bass.ds(e * HIDDEN + c * P, P)] for part in range(2)]
        pe.matmul(out, w[0], x[:, 0, :], start=True, stop=False)
        pe.matmul(out, w[0], x[:, 1, :], start=False, stop=False)
        last = pe.matmul(out, w[1], x[:, 0, :], start=False, stop=True)
    last.then_inc(s.up, 1)


def block_down(pe, m, s, block, j, e):
    wait(pe, s.out, block - 1)
    for c in range(CHUNKS):
        if c % 2 == 0:
            wait(pe, s.low, block * 2 + (c // 2 + 1))
        both, of_high = m.w2[:, 0:2, bass.ds(e * HIDDEN + c * D, D)], m.w2[:, 0, bass.ds(e * HIDDEN + c * D, D)]
        for i in range(WIDE):
            out = m.pvb[:, j % 2, i * 2 * D:(i + 1) * 2 * D]
            high, low = (x[:, j, c, i * P:(i + 1) * P] for x in (m.gh, m.gl))
            pe.matmul(out.rearrange("p (x d) -> p x d", x=2), high, both, start=(c == 0 and i == 0), stop=False,
                      skip_group_check=True)
            last = pe.matmul(out[:, 0:D], low, of_high, start=False, stop=(c == CHUNKS - 1), skip_group_check=True)
    last.then_inc(s.down, 1)


def expert_of(eng, m, block):
    return eng.value_load(m.expert[0:1, 0, bass.ds(block, 1)], min_val=0, max_val=EXPERTS - 1)


def blocks_pe(pe, m, s):
    pe.wait_ge(s.expert, 1)
    turn = lambda rounds, j: block_turn(pe, m, s, (rounds + j // UNROLL) * UNROLL + j % UNROLL, j % UNROLL,
                                        rounds + j // UNROLL)
    for j in range(2):
        turn(0, j)
        block_up(pe, m, s, j, j, expert_of(pe, m, j))
    turn(0, 2)

    def round_(rounds, last=False):
        experts = [None, None]
        for j in range(UNROLL):
            block = rounds * UNROLL + j
            if not (last and j + 2 >= UNROLL):
                experts.append(expert_of(pe, m, block + 2))
            if not (last and j + 3 >= UNROLL):
                turn(rounds, j + 3)
            if not (last and j + 2 >= UNROLL):
                block_up(pe, m, s, block + 2, (j + 2) % UNROLL, experts[j + 2])
            block_down(pe, m, s, block, j, experts[j] if j >= 2 else expert_of(pe, m, block))

    round_(0)
    with pe.Fori(1, BLOCKS // UNROLL - 1) as i:
        round_(i)
    round_(BLOCKS // UNROLL - 1, last=True)


def rounds_of(eng, step):
    for j in range(UNROLL):
        step(0, j)
    with eng.Fori(1, BLOCKS // UNROLL) as i:
        for j in range(UNROLL):
            step(i, j)


def blocks_act(act, m, s):
    act.wait_ge(s.expert, 1)

    def step(rounds, j):
        block = rounds * UNROLL + j
        e = expert_of(act, m, block)
        wait(act, s.up, block + 1)
        wait(act, s.low, block * 2 - 2)
        for c in range(CHUNKS):
            last = act.activation(m.gf[:, j % 2, c, :], m.hid[j % 2][:, c, :], ACT.Gelu,
                                  bias=m.b1[:, bass.ds(e * CHUNKS + c, 1)], scale=1 / WSCALE)
            if c % 2:
                last.then_inc(s.gelu, 1)
        wait(act, s.down, block - UNROLL + 1)
        for half in range(2):
            wait(act, s.gelu, block * 2 + (half + 1))
            act.activation(m.gh[:, j, 2 * half:2 * half + 2, :], m.gf[:, j % 2, 2 * half:2 * half + 2, :], ACT.Copy)\
               .then_inc(s.high, 1)

    rounds_of(act, step)


def blocks_dve(dve, m, s):
    dve.wait_ge(s.expert, 1)

    def keep_input(rounds, j):
        block = rounds * UNROLL + j
        wait(dve, s.in_turned, block + 1)
        wait(dve, s.up, block - 1)
        wait(dve, s.out, block - UNROLL + 1)
        dve.tensor_tensor(m.to_f[:, j, :], m.xb[:, j, :, 2 * D:ROW].bitcast(F32).rearrange("p i c -> p (i c)"),
                          m.dump[:, j, :], ALU.min)
        dve.tensor_copy(m.xbt[:, j % 2, :, :], m.tr16[:, 0:2 * BLOCK].rearrange("p (x q) -> p x q", x=2))\
            .then_inc(s.in_kept, 1)

    def split(block, j):
        wait(dve, s.down, block - UNROLL + 1)
        for half in range(2):
            wait(dve, s.high, block * 2 + (half + 1))
            part = slice(2 * half, 2 * half + 2)
            dve.tensor_tensor(m.gl[:, j, part, :], m.gf[:, j % 2, part, :], m.gh[:, j, part, :], ALU.subtract)\
                .then_inc(s.low, 1)

    def keep_output(rounds, j, e):
        block = rounds * UNROLL + j
        wait(dve, s.down, block + 1)
        wait(dve, s.sent[j % 2], rounds * (WIDE * 16 * 2) + (WIDE * 16 * (j // 2) + s.turn * sent_of_run()))
        dve.tensor_copy(m.to[:, j, :], m.to_f[:, j, :])
        halves = m.pvb[:, j % 2, :].rearrange("p (i x d) -> p x i d", i=WIDE, x=2)
        dve.scalar_tensor_tensor(out=m.half_out[:, j % 2, :, :], in0=halves[:, 0], scalar=1 / WSCALE,
                                 in1=m.b2[:, bass.ds(e * D, D)].unsqueeze(1).to_broadcast([P, WIDE, D]),
                                 op0=ALU.mult, op1=ALU.add).then_inc(s.half, 1)
        wait(dve, s.half, block + 1)
        dve.scalar_tensor_tensor(out=m.ob[:, j % 2, :, :], in0=halves[:, 1], scalar=1 / WSCALE,
                                 in1=m.half_out[:, j % 2, :, :], op0=ALU.mult, op1=ALU.add).then_inc(s.out, 1)

    def step(rounds, j, last=False):
        e = expert_of(dve, m, rounds * UNROLL + j)
        if not (last and j + 3 >= UNROLL):
            keep_input(rounds + (j + 3) // UNROLL, (j + 3) % UNROLL)
        if not (last and j + 1 >= UNROLL):
            split(rounds * UNROLL + (j + 1), (j + 1) % UNROLL)
        keep_output(rounds, j, e)

    for j in range(3):
        keep_input(0, j)
    split(0, 0)
    for j in range(UNROLL):
        step(0, j)
    with dve.Fori(1, BLOCKS // UNROLL - 1) as i:
        for j in range(UNROLL):
            step(i, j)
    for j in range(UNROLL):
        step(BLOCKS // UNROLL - 1, j, last=True)


def sent_of_run():
    return 16 * WIDE * BLOCKS // 2


def blocks_pool(pool, m, s, g):
    with pool.Fori(0, BLOCKS // UNROLL) as i:
        for j in range(UNROLL):
            wait(pool, s.out, i * UNROLL + (j + 1))
            pool.sem_inc(g.carried, 1)
            for k in range(WIDE):
                pool.indirect_dma_start(out=m.returned[:, :],
                                        out_offset=bass.IndirectOffsetOnAxis(ap=m.to[:, j, k:k + 1], axis=0),
                                        in_=m.ob[:, j % 2, k, :], in_offset=None).then_inc(s.sent[j % 2], 16)


def combine_sp(sp, m, s):
    for sent in s.sent:
        sp.wait_ge(sent, sent_of_run() * (s.turn + 1))
    rows = m.returned[0:TOP * TOKENS, :].rearrange("(k n p) d -> p k n d", k=TOP, p=P)
    for b in range(B):
        wait(sp, s.x_added, TOP * (b - RETURNS + 1))
        for k in range(TOP):
            sp.dma_start(m.back[:, b % RETURNS, k, :, :], rows[:, k, b * NT:(b + 1) * NT, :])\
              .then_inc(s.back[b % RETURNS], 16)


def combine_dve(dve, m, s, stats):
    for b in range(B):
        dve.wait_ge(s.back[b % RETURNS], 16 * TOP * (b // RETURNS + 1 + s.turn * B // RETURNS))
        for k in range(TOP):
            if k:
                dve.wait_ge(s.x_added, TOP * b + 1)
            for t in range(NT):
                n = b * NT + t
                x = m.x[:, n * D:(n + 1) * D]
                last = dve.scalar_tensor_tensor(out=x, in0=m.back[:, b % RETURNS, k, t, :],
                                                scalar=m.gate[:, k, n:n + 1], in1=x, op0=ALU.mult, op1=ALU.add)
            last.then_inc(s.x_added, 1)
        if stats:
            dve.wait_ge(s.x_added, TOP * (b + 1))
            last = dve_stats(dve, m, b)
    if stats:
        last.then_inc(s.stats, 1)




def act_std(act, m, g, k):
    act.wait_ge(g.moments, 3 * k + 3)
    act.activation(m.std[:, :], m.var[:, :], ACT.Sqrt, scale=1 / D, bias=m.eps[:, 0:1]).then_inc(g.std_ready, 1)


def dve_rstd(dve, m, g, k, stats, count):
    bn = m.bn[:, :].rearrange("p (n v) -> p v n", v=BN)
    mean_e, sum_e, mean_o, sum_o = (bn[:, v, :] for v in (1, 2, 4, 5))
    dve.wait_ge(stats, count)
    dve.tensor_tensor(m.half[:, :], mean_e, mean_o, ALU.subtract)
    dve.tensor_tensor(m.var[:, :], sum_e, sum_o, ALU.add)
    dve.tensor_tensor(m.mean[:, :], mean_e, mean_o, ALU.add).then_inc(g.moments, 1)
    dve.wait_ge(g.moments, 3 * k + 1)
    dve.tensor_scalar(m.mean[:, :], m.mean[:, :], 0.5, None, ALU.mult)
    dve.scalar_tensor_tensor(out=m.half[:, :], in0=m.half[:, :], scalar=D / 4, in1=m.half[:, :],
                             op0=ALU.mult, op1=ALU.mult).then_inc(g.moments, 1)
    dve.wait_ge(g.moments, 3 * k + 2)
    dve.tensor_tensor(m.var[:, :], m.var[:, :], m.half[:, :], ALU.add).then_inc(g.moments, 1)
    dve.wait_ge(g.std_ready, k + 1)
    dve.reciprocal(m.rstd[:, :], m.std[:, :]).then_inc(g.rstd_ready, 1)
    dve.wait_ge(g.rstd_ready, k + 1)


class Memory:
    pass


class GlobalSignals:
    def __init__(self, new):
        self.x_loaded, self.loaded, self.zeroed, self.stored = (new(n) for n in ("x_loaded", "loaded", "zeroed", "stored"))
        self.weights_high, self.weights_low = new("weights_high"), new("weights_low")
        self.cleared, self.consts = new("cleared"), new("consts")
        self.carried = new("carried")
        self.moments, self.std_ready, self.rstd_ready = new("moments"), new("std_ready"), new("rstd_ready")


def build(nc, x, a_w, a_wo, b_w, b_wo, cos, sin, wg, bg, w1, b1, w2, b2, out, upto=4):
    ctx = ExitStack()
    with ctx:
        def sb(name, shape, dt):
            return ctx.enter_context(nc.sbuf_tensor(name, shape, dt))

        def ps(name, shape, dt):
            return ctx.enter_context(nc.psum_tensor(name, shape, dt))

        def sem(name):
            return ctx.enter_context(nc.semaphore(name))

        a, b = first_attention(), second_attention()
        m = Memory()
        m.x = sb("x", [P, B * NT * D], F32)
        m.mean = sb("mean", [P, B * NT], F32)
        m.var = sb("var", [P, B * NT], F32)
        m.std = sb("std", [P, B * NT], F32)
        m.rstd = sb("rstd", [P, B * NT], F32)
        m.eps = sb("eps", [P, 1], F32)
        m.bn = sb("bn", [P, TILES * BN], F32)
        m.half = sb("half", [P, TILES], F32)
        m.xn = sb("xn", [P, NT, D], F32)
        m.xn16 = sb("xn16", [P, NT, 2, D], F16)
        m.xt = sb("xt", [P, 2, T], F16)
        m.w = {"a": sb("wa", [P, 2, STEPS, a.columns], F16), "b": sb("wb", [P, 2, STEPS, b.columns], F16)}
        m.wo = {"a": sb("woa", [P, HEADS // 2, D], F32), "b": sb("wob", [P, HEADS // 2, D], F32)}
        m.cos = sb("cos", [P, NT, HD], F32)
        m.sin = sb("sin", [P, NT, HD], F32)
        m.ident16 = sb("ident16", [P, P], F16)
        m.ident32 = sb("ident32", [P, P], F32)
        m.mask_q = sb("mask_q", [P, P], F16)
        m.mask_k = sb("mask_k", [P, P], F16)
        m.tmq = [sb(f"tmq{i}", [P, NT, GROUP, 3 * HD], F16) for i in range(2)]
        m.tmk = [sb(f"tmk{i}", [P, NT, GROUP, 4 * HD], F16) for i in range(2)]
        turned = sb("turned", [P, 2, 2, GROUP, T], F16)
        qt, tt = turned[:, 0], turned[:, 1]
        kt = sb("kt", [P, 2, 2, GROUP, T], F16)
        m.qt, m.tt, m.kt = ([v[:, i] for i in range(2)] for v in (qt, tt, kt))
        m.vb = [sb(f"vb{i}", [P, NT, GROUP, VW + HD], F16) for i in range(2)]
        m.pf = sb("pf", [P, RING, T], F32)
        m.ph = sb("ph", [P, RING, T], F16)
        m.pl = sb("pl", [P, RING, T], F16)
        m.rope1 = sb("rope1", [P, GROUP + 1, HD], F32)
        m.rope2 = sb("rope2", [P, GROUP + 1, HD], F32)
        m.qr = sb("qr", [P, 2, GROUP + 1, HD], F32)
        m.rs = sb("rs", [P, 2, NT], F32)
        m.y = sb("y", [P, NT, GROUP, HD], F32)
        m.yt = sb("yt", [P, HEADS // 2, T], F32)
        m.pj = ps("pj", [P, 512], F32)
        m.mx = ps("mx", [P, 2, 512], F32)
        m.st = ps("st", [P, 2, 512], F32)
        pv = ps("pv", [P, 2, 512], F32)
        m.pv = pv[:, :, 0:NT * VW].rearrange("p b (t v) -> p b t v", t=NT)
        m.tr32 = ps("tr", [P, 512], F32)
        m.tr16 = m.tr32[:, :].bitcast(F16)
        m.w1 = sb("w1", [P, 2, EXPERTS * HIDDEN], F16)
        m.w2 = sb("w2", [P, 2, EXPERTS * HIDDEN], F16)
        m.wg = sb("wg", [P, 2, EXPERTS], F16)
        m.wg_f = sb("wg_f", [P, EXPERTS], F32)
        m.bg = sb("bg", [P, EXPERTS], F32)
        m.b1 = sb("b1", [P, EXPERTS * CHUNKS], F32)
        m.b2 = sb("b2", [P, EXPERTS * D], F32)
        m.before = sb("before", [P, P], F16)
        m.ones = sb("ones", [P, P], F16)
        m.rank = sb("rank", [P, EXPERTS], F32)
        m.upto = sb("upto", [P, EXPERTS, EXPERTS], F32)
        m.block_start = sb("block_start", [P, REGION // BLOCK], F32)
        m.block_no = sb("block_no", [P, BLOCKS], F32)
        m.region = sb("region", [P, EXPERTS], F32)
        m.first_home = sb("first_home", [P, TOP, NT], F32)
        m.home = sb("home", [P, TOP, NT], F32)
        m.free = sb("free", [P, EXPERTS], F32)
        m.best = sb("best", [P, TOP, NT], F32)
        m.t2 = sb("t2", [P, NT], F32)
        m.two = sb("two", [P, TOP, NT], F32)
        m.count = sb("count", [P, 4, EXPERTS], F32)
        m.t8 = sb("t8", [P, EXPERTS, EXPERTS], F32)
        m.slot_f = sb("slot_f", [P, TOP, NT], F32)
        m.slot = sb("slot", [P, 2, TOP, NT], U32)
        m.gate = sb("gate", [P, TOP, TILES], F32)
        m.expert = sb("expert", [P, 2, BLOCKS], mybir.dt.int32)
        m.expert_f = sb("expert_f", [P, 2, BLOCKS], F32)
        m.half_out = m.xn[:, :, :].rearrange("p (r i) d -> p r i d", r=2)
        m.to_f = sb("to_f", [P, UNROLL, WIDE], F32)
        m.dump = sb("dump", [P, UNROLL, WIDE], F32)
        m.xb = sb("xb", [P, UNROLL, WIDE, ROW], F16)
        m.to = sb("to", [P, UNROLL, WIDE], U32)
        y = m.y[:, :, :, :].rearrange("p t h d -> p (t h d)")
        m.ob = y[:, 0:2 * BLOCK].rearrange("p (r i d) -> p r i d", r=2, d=D)
        m.xbt = y[:, 2 * BLOCK:4 * BLOCK].bitcast(F16).rearrange("p (r x q) -> p r x q", r=2, x=2)
        m.logit, m.one1, m.one2, m.t1, m.t3, m.gate_exp = (
            sb(name, [P, NT, EXPERTS], F32) for name in ("logit", "one1", "one2", "t1", "t3", "gate_exp"))
        m.choice = sb("choice", [P, NT, EXPERTS], F16)
        free = kt[:, :, :, :, :].rearrange("p a b c d -> p (a b c d)").bitcast(F32)
        m.t_full = free[:, 0:EXPERTS * (REGION // BLOCK)].rearrange("p (e j) -> p e j", e=EXPERTS)
        m.t_blocks = free[:, 512:512 + BLOCKS * (EXPERTS - 1)].rearrange("p (j e) -> p j e", e=EXPERTS - 1)
        m.send = kt[:, :, :, :, :].rearrange("p a b c d -> p (a b c d)")[:, 2048:2048 + 2 * NT * TOP * ROW]\
            .rearrange("p (r t k c) -> p r t k c", r=2, t=NT, k=TOP)
        m.gf = m.pf[:, :, :].rearrange("p a b -> p (a b)").rearrange("p (r c q) -> p r c q", r=2, c=CHUNKS)
        rings = turned[:, :, :, :, :].rearrange("p a b c d -> p (a b c d)")\
            .rearrange("p (x r c q) -> p x r c q", x=2, r=UNROLL, c=CHUNKS)
        m.gh, m.gl = rings[:, 0], rings[:, 1]
        m.hid = [v[:, :, :].rearrange("p b (c q) -> p (b c) q", q=BLOCK) for v in (m.st, m.mx)]
        m.back = m.yt[:, :, :].rearrange("p a b -> p (a b)")\
            .rearrange("p (r k t d) -> p r k t d", r=RETURNS, k=TOP, d=D)
        m.pvb = pv
        stage = {"a": m.pf[:, :, :].rearrange("p a b -> p (a b)")[:, 0:STEPS * a.columns],
                 "b": turned[:, :, :, :, :].rearrange("p a b c d -> p (a b c d)").bitcast(F32)[:, 0:STEPS * b.columns],
                 "w1": m.yt[:, :, :].rearrange("p a b -> p (a b)"),
                 "w2": free[:, :], "wg": m.wg_f[:, :]}
        split = {"a": m.w["a"][:, :, :, :].rearrange("p x g c -> p x (g c)"),
                 "b": m.w["b"][:, :, :, :].rearrange("p x g c -> p x (g c)"),
                 "w1": m.w1, "w2": m.w2, "wg": m.wg}
        m.returned = nc.dram_tensor("returned", [TOP * TOKENS + UNROLL * BLOCK, D], F32, kind="Internal").ap()

        g = GlobalSignals(sem)
        attention = {"a": (a, AttentionSignals(sem, "a")), "b": (b, AttentionSignals(sem, "b"))}
        experts = [ExpertSignals(sem, f"experts{k}") for k in range(2)]
        loaded = [sem(f"loaded{k}") for k in range(UNROLL)]
        sent = [sem(f"sent{k}") for k in range(2)]
        back = [sem(f"back{k}") for k in range(RETURNS)]
        for turn, s in enumerate(experts):
            s.loaded, s.sent, s.back, s.turn = loaded, sent, back, turn
            s.slots_in = nc.dram_tensor(f"slots_in{turn}", [SLOTS, ROW], F16, kind="Internal").ap()
        first_stats = sem("first_stats")
        weights = ("a", "b", "w1", "w2", "wg")
        loaded_weights = {name: sem(f"loaded_{name}") for name in weights}
        phases = ("a", 0, "b", 1)[:upto]
        stats = [(first_stats, 1)] + [(attention[k][1].stats, B) if k in attention else (experts[k].stats, 1)
                                      for k in phases]
        block = ctx.enter_context(nc.Block())

        @block.sync
        def _(sp):
            sp.dma_start(m.x[:, :].rearrange("p (n d) -> p n d", d=D), x.rearrange("(n p) d -> p n d", p=P))\
              .then_inc(g.x_loaded, 16)
            for name, src in zip(weights, (a_w, b_w, w1, w2, wg)):
                sp.dma_start(stage[name], src).then_inc(loaded_weights[name], 16)
            sp.dma_start(m.cos[:, :, :], cos).then_inc(g.loaded, 16)
            sp.dma_start(m.sin[:, :, :], sin).then_inc(g.loaded, 16)
            sp.dma_start(m.wo["a"][:, :, :], a_wo).then_inc(g.loaded, 16)
            sp.dma_start(m.wo["b"][:, :, :], b_wo).then_inc(g.loaded, 16)
            sp.dma_start(m.b1[:, :], b1).then_inc(g.loaded, 16)
            sp.dma_start(m.bg[:, :], bg.partition_broadcast(P)).then_inc(g.loaded, 16)
            sp.dma_start(m.b2[:, :], b2.partition_broadcast(P)).then_inc(g.loaded, 16)
            sp.wait_ge(g.consts, 1)
            for s in experts:
                sp.dma_start(s.slots_in.rearrange("(j p) c -> p j c", p=P),
                             m.xb[:, 0, 0:1, :].to_broadcast([P, SLOTS // P, ROW])).then_inc(g.zeroed, 16)
            for k in phases:
                if k in (0, 1):
                    route_sp(sp, m, experts[k])
                    blocks_sp(sp, m, experts[k])
                    combine_sp(sp, m, experts[k])
            for b in range(B):
                if phases[-1] in (0, 1):
                    sp.wait_ge(experts[phases[-1]].x_added, TOP * (b + 1))
                else:
                    sp.wait_ge(*stats[-1])
                sp.dma_start(out[b * T:(b + 1) * T, :].rearrange("(n p) d -> p n d", p=P),
                             m.x[:, b * NT * D:(b + 1) * NT * D].rearrange("p (n d) -> p n d", d=D))\
                  .then_inc(g.stored, 16)
            sp.wait_ge(g.stored, 16 * B)

        @block.gpsimd
        def _(pool):
            pool.memset(m.xb[:, 0, 0, 0:2 * D], 0.0)
            pool.memset(m.xb[:, 0, 0, 2 * D:ROW].bitcast(F32), float(NOWHERE))
            for t in (m.ident16, m.ident32, m.mask_q, m.mask_k):
                pool.memset(t[:, :], 0.0)
            pool.memset(m.ones[:, :], 1.0)
            pool.memset(m.before[:, :], 1.0)
            pool.memset(m.upto[:, :, :], 1.0)
            for i in range(2):
                pool.memset(m.tmq[i][:, :, :, P:3 * HD], 0.0)
                last = pool.memset(m.tmk[i][:, :, :, 3 * HD:4 * HD], 0.0)
            last.then_inc(g.cleared, 1)
            pool.wait_ge(g.cleared, 1)
            for i in range(2):
                pool.memset(m.vb[i][:, :, :, HD:HD + 1], 1.0)
                pool.memset(m.vb[i][:, :, :, HD + 1:VW], 0.0)
                pool.memset(m.tmk[i][:, :, :, 3 * HD:3 * HD + 1], -1.0)
            for t in (m.ident16, m.ident32):
                pool.affine_select(out=t[:, :], in_=t[:, :], compare_op=ALU.not_equal, fill=1.0, base=0,
                                   pattern=[[-1, P]], channel_multiplier=1)
            pool.affine_select(out=m.mask_q[:, :], in_=m.mask_q[:, :], compare_op=ALU.is_ge, fill=MASKED, base=0,
                               pattern=[[-1, P]], channel_multiplier=1)
            pool.affine_select(out=m.mask_k[:, :], in_=m.mask_k[:, :], compare_op=ALU.is_ge, fill=MASKED, base=0,
                               pattern=[[1, P]], channel_multiplier=-1)
            pool.affine_select(out=m.before[:, :], in_=m.before[:, :], compare_op=ALU.is_gt, fill=0.0, base=0,
                               pattern=[[1, P]], channel_multiplier=-1)
            pool.affine_select(out=m.upto[:, :, :], in_=m.upto[:, :, :], compare_op=ALU.is_ge, fill=0.0,
                               base=0, pattern=[[1, EXPERTS], [-1, EXPERTS]], channel_multiplier=0)
            exact = dict(allow_small_or_imprecise_dtypes=True)
            pool.iota(m.rank[:, :], [[-1, EXPERTS]], base=EXPERTS, channel_multiplier=0, **exact)
            pool.iota(m.dump[:, :, :], [[BLOCK, UNROLL], [P, WIDE]], base=TOP * TOKENS, channel_multiplier=1, **exact)
            pool.iota(m.first_home[:, :, :], [[TOKENS, TOP], [P, NT]], base=0, channel_multiplier=1, **exact)
            pool.iota(m.region[:, :], [[REGION, EXPERTS]], base=0, channel_multiplier=0, **exact)
            pool.iota(m.block_start[:, :], [[BLOCK, REGION // BLOCK]], base=0, channel_multiplier=0, **exact)
            pool.iota(m.block_no[:, :], [[1, BLOCKS]], base=0, channel_multiplier=0, **exact).then_inc(g.consts, 1)
            for k in phases:
                if k in (0, 1):
                    scatter_pool(pool, m, experts[k], g)
                    blocks_pool(pool, m, experts[k], g)
                else:
                    attention_pool(pool, m, *attention[k])

        @block.scalar
        def _(act):
            for name in weights:
                act.wait_ge(loaded_weights[name], 16)
                act.activation(split[name][:, 0, :], stage[name], ACT.Copy, scale=WSCALE)\
                   .then_inc(g.weights_high, 1)
            for n, k in enumerate(phases):
                act_std(act, m, g, n)
                if k in (0, 1):
                    route_act(act, m, experts[k])
                    blocks_act(act, m, experts[k])
                else:
                    attention_act(act, m, *attention[k])

        @block.vector
        def _(dve):
            dve.memset(m.eps[:, :], EPS)
            for k, name in enumerate(weights):
                dve.wait_ge(g.weights_high, k + 1)
                dve.scalar_tensor_tensor(out=split[name][:, 1, :], in0=stage[name], scalar=WSCALE,
                                         in1=split[name][:, 0, :], op0=ALU.mult, op1=ALU.subtract)\
                   .then_inc(g.weights_low, 1)
            dve.wait_ge(g.x_loaded, 16)
            stats_dve(dve, m, first_stats)
            dve.wait_ge(g.loaded, 16 * 7)
            dve.wait_ge(g.consts, 1)
            for n, k in enumerate(phases):
                dve_rstd(dve, m, g, n, *stats[n])
                if k in (0, 1):
                    s = experts[k]
                    route_dve(dve, m, s)
                    blocks_dve(dve, m, s)
                    combine_dve(dve, m, s, stats=(n + 1 < len(phases)))
                else:
                    attention_dve(dve, m, *attention[k])

        @block.tensor
        def _(pe):
            pe.wait_ge(g.consts, 1)
            pe.wait_ge(g.weights_low, len(weights))
            pe.wait_ge(g.loaded, 16 * 7)
            for k in phases:
                if k in (0, 1):
                    route_pe(pe, m, experts[k])
                    blocks_pe(pe, m, experts[k])
                else:
                    attention_pe(pe, m, *attention[k])


def stats_dve(dve, m, stats):
    with dve.Fori(0, B - 1) as b:
        dve_stats(dve, m, b)
    dve_stats(dve, m, B - 1).then_inc(stats, 1)


def lay_out(inputs):
    f = np.float32
    A = lambda n: np.ascontiguousarray(inputs["L0_" + n])
    wq = A("attn_a_Wq").reshape(D, STEPS, GROUP, HD // 2, 2).transpose(0, 1, 2, 4, 3).reshape(D, STEPS, GROUP * HD)
    wk = A("attn_a_Wk").reshape(D, STEPS, HD // 2, 2).transpose(0, 1, 3, 2).reshape(D, STEPS, HD)
    wv = A("attn_a_Wv").reshape(D, STEPS, HD)
    a_w = np.concatenate([wq, wk, wv], axis=2).reshape(D, -1)
    b_w = A("attn_b_W_qkv").reshape(D, STEPS, GROUP, HD, 3).transpose(0, 1, 4, 2, 3).reshape(D, -1)
    wo = lambda n: A(n).reshape(HEADS // 2, P, D).transpose(1, 0, 2)
    inv = (f(1) / f(10000.0) ** (np.arange(0, HD, 2, dtype=f) / f(HD))).astype(f)
    ang = (np.arange(T, dtype=f)[:, None] * inv[None, :]).astype(f)
    c, s = np.cos(ang).astype(f) / f(WSCALE), np.sin(ang).astype(f) / f(WSCALE)
    tiles = lambda v: v.reshape(NT, P, HD).transpose(1, 0, 2)
    arrays = {"x": A("attn_a_x").reshape(B * T, D), "a_w": a_w, "a_wo": wo("attn_a_Wo"), "b_w": b_w,
            "b_wo": wo("attn_b_W_out"), "cos": tiles(np.concatenate([c, c], 1)),
            "sin": tiles(np.concatenate([-s, s], 1)),
            "wg": A("ffn_Wg"), "bg": A("ffn_bg"), "w1": A("ffn_W1").transpose(1, 0, 2).reshape(D, -1),
            "b1": A("ffn_b1").reshape(EXPERTS, CHUNKS, P).transpose(2, 0, 1).reshape(P, -1),
            "w2": A("ffn_W2").reshape(EXPERTS, CHUNKS, P, D).transpose(2, 0, 1, 3).reshape(P, -1),
            "b2": A("ffn_b2").reshape(-1)}
    return {name: np.ascontiguousarray(v) for name, v in arrays.items()}




def kernel(**inputs):
    import concourse.bacc as bacc
    from concourse.bass_utils import run_bass_kernel_spmd

    nc = bacc.Bacc("TRN2", target_bir_lowering=False, num_devices=1)
    arrays = lay_out(inputs)
    args = [nc.dram_tensor(f"in_{name}_dram", v.shape, mybir.dt.from_np(v.dtype), kind="ExternalInput").ap()
            for name, v in arrays.items()]
    args.append(nc.dram_tensor("out_0_dram", (B * T, D), F32, kind="ExternalOutput").ap())
    build(nc, *args)
    r = run_bass_kernel_spmd(nc, [{f"in_{name}_dram": v for name, v in arrays.items()}], core_ids=[0])
    return r.results[0]["out_0_dram"].reshape(B, T, D)
```
